# Optimizing a Trainium2 kernel written in Bass

```python
import numpy as np
import jax
import jax.numpy as jnp

def _softmax(x, axis=-1):
    return jax.nn.softmax(x, axis=axis)

def _gelu(x):
    return jax.nn.gelu(x, approximate=True)

def _silu(x):
    return jax.nn.silu(x)

def _sigmoid(x):
    return jax.nn.sigmoid(x)

def _layernorm(x, axis=-1, eps=1e-05):
    m = jnp.mean(x, axis=axis, keepdims=True)
    v = jnp.var(x, axis=axis, keepdims=True)
    return (x - m) / jnp.sqrt(v + eps)

def _scatter_add(tgt, idx, src, axis=0):
    return tgt.at[idx].add(src)

def _segment_sum(src, seg, n):
    return jax.ops.segment_sum(src, seg, n)
kernel_name = 'mk_macaron_d1_jaxref_r4_07f131'

def setup_inputs(seed: int=0):
    np.random.seed(seed)
    _w = jnp.asarray

    def _L0_attn_setup():
        import jax, jax.numpy as jnp
        import numpy as np
        B, T, D, H = (2, 512, 256, 16)
        d = D // H
        I = 704
        EPS = 1e-06

        def _rmsnorm(x, w):
            return x * jax.lax.rsqrt(jnp.mean(x * x, axis=-1, keepdims=True) + EPS) * w

        def _xlstm_scan(q, k, v, i_gate, f_gate):
            b, t, h, dd = q.shape
            qs = jnp.moveaxis(q, 1, 0)
            ks_ = jnp.moveaxis(k, 1, 0)
            vs = jnp.moveaxis(v, 1, 0)
            ig = jnp.moveaxis(i_gate, 1, 0)
            fg = jnp.moveaxis(f_gate, 1, 0)
            C0 = jnp.zeros((b, h, dd, dd), q.dtype)
            n0 = jnp.zeros((b, h, dd), q.dtype)

            def step(carry, inp):
                C, n = carry
                qt, kt, vt, it, ft = inp
                C = ft[:, :, None, None] * C + it[:, :, None, None] * (vt[..., :, None] * kt[..., None, :])
                n = ft[..., None] * n + it[..., None] * kt
                ht = jnp.einsum('bhde,bhe->bhd', C, qt)
                denom = jnp.maximum(jnp.abs(jnp.einsum('bhd,bhd->bh', n, qt)), 1.0)[..., None]
                return ((C, n), ht / denom)
            _, ys = jax.lax.scan(step, (C0, n0), (qs, ks_, vs, ig, fg))
            return jnp.moveaxis(ys, 0, 1)
        key = jax.random.key(seed)
        ks = jax.random.split(key, 12)
        s = 0.02
        init = lambda k, sh: jax.random.normal(k, sh, dtype=jnp.float32) * s
        return {'x': jax.random.normal(ks[0], (B, T, D), dtype=jnp.float32), 'ln1_w': jnp.ones((D,), jnp.float32), 'ln2_w': jnp.ones((D,), jnp.float32), 'wq': init(ks[1], (D, D)), 'wk': init(ks[2], (D, D)), 'wv': init(ks[3], (D, D)), 'wo': init(ks[4], (D, D)), 'wi': init(ks[5], (D, H)), 'bi': jnp.zeros((H,), jnp.float32), 'wf': init(ks[6], (D, H)), 'bf': jnp.full((H,), 3.0, jnp.float32), 'w_gate': init(ks[7], (D, I)), 'w_up': init(ks[8], (D, I)), 'w_down': init(ks[9], (I, D))}
    _L0_attn_in = _L0_attn_setup()

    def _L0_ffn_setup():
        import jax, jax.numpy as jnp
        import numpy as np
        B, S, D, F, E, R = (4, 512, 256, 1024, 8, 4)
        key = jax.random.key(seed)
        ks = jax.random.split(key, 8)
        s_in = 1.0 / np.sqrt(D)
        s_ff = 1.0 / np.sqrt(F)
        return {'hidden_states': jax.random.normal(ks[0], (B, S, D), jnp.float32), 'gate_W': jax.random.normal(ks[1], (E, D), jnp.float32) * s_in, 'gate_b': jnp.zeros((E,), jnp.float32), 'wi_W': jax.random.normal(ks[2], (F, D), jnp.float32) * s_in, 'wi_b': jnp.zeros((F,), jnp.float32), 'wo_W': jax.random.normal(ks[3], (D, F), jnp.float32) * s_ff, 'wo_b': jnp.zeros((D,), jnp.float32), 'lora_A': jax.random.normal(ks[4], (E, R, D), jnp.float32) * s_in, 'lora_B': jax.random.normal(ks[5], (E, F, R), jnp.float32) * 0.02}
    _L0_ffn_in = _L0_ffn_setup()
    _d = {'L0_attn_x': _L0_attn_in['x'], 'L0_attn_ln1_w': _L0_attn_in['ln1_w'], 'L0_attn_ln2_w': _L0_attn_in['ln2_w'], 'L0_attn_wq': _L0_attn_in['wq'], 'L0_attn_wk': _L0_attn_in['wk'], 'L0_attn_wv': _L0_attn_in['wv'], 'L0_attn_wo': _L0_attn_in['wo'], 'L0_attn_wi': _L0_attn_in['wi'], 'L0_attn_bi': _L0_attn_in['bi'], 'L0_attn_wf': _L0_attn_in['wf'], 'L0_attn_bf': _L0_attn_in['bf'], 'L0_attn_w_gate': _L0_attn_in['w_gate'], 'L0_attn_w_up': _L0_attn_in['w_up'], 'L0_attn_w_down': _L0_attn_in['w_down'], 'L0_ffn_gate_W': _L0_ffn_in['gate_W'], 'L0_ffn_gate_b': _L0_ffn_in['gate_b'], 'L0_ffn_wi_W': _L0_ffn_in['wi_W'], 'L0_ffn_wi_b': _L0_ffn_in['wi_b'], 'L0_ffn_wo_W': _L0_ffn_in['wo_W'], 'L0_ffn_wo_b': _L0_ffn_in['wo_b'], 'L0_ffn_lora_A': _L0_ffn_in['lora_A'], 'L0_ffn_lora_B': _L0_ffn_in['lora_B']}
    _x0 = _d['L0_attn_x']
    _d['L0_attn_x'] = jax.random.normal(jax.random.fold_in(jax.random.key(seed), 1), (4, 1024, 256), dtype=_x0.dtype)
    del _x0
    return _d

def reference(L0_attn_x, L0_attn_ln1_w, L0_attn_ln2_w, L0_attn_wq, L0_attn_wk, L0_attn_wv, L0_attn_wo, L0_attn_wi, L0_attn_bi, L0_attn_wf, L0_attn_bf, L0_attn_w_gate, L0_attn_w_up, L0_attn_w_down, L0_ffn_gate_W, L0_ffn_gate_b, L0_ffn_wi_W, L0_ffn_wi_b, L0_ffn_wo_W, L0_ffn_wo_b, L0_ffn_lora_A, L0_ffn_lora_B):

    def _L0_attn_ref(x, ln1_w, ln2_w, wq, wk, wv, wo, wi, bi, wf, bf, w_gate, w_up, w_down):
        import jax, jax.numpy as jnp
        import numpy as np
        B, T, D, H = (2, 512, 256, 16)
        d = D // H
        I = 704
        EPS = 1e-06

        def _rmsnorm(x, w):
            return x * jax.lax.rsqrt(jnp.mean(x * x, axis=-1, keepdims=True) + EPS) * w

        def _xlstm_scan(q, k, v, i_gate, f_gate):
            b, t, h, dd = q.shape
            qs = jnp.moveaxis(q, 1, 0)
            ks_ = jnp.moveaxis(k, 1, 0)
            vs = jnp.moveaxis(v, 1, 0)
            ig = jnp.moveaxis(i_gate, 1, 0)
            fg = jnp.moveaxis(f_gate, 1, 0)
            C0 = jnp.zeros((b, h, dd, dd), q.dtype)
            n0 = jnp.zeros((b, h, dd), q.dtype)

            def step(carry, inp):
                C, n = carry
                qt, kt, vt, it, ft = inp
                C = ft[:, :, None, None] * C + it[:, :, None, None] * (vt[..., :, None] * kt[..., None, :])
                n = ft[..., None] * n + it[..., None] * kt
                ht = jnp.einsum('bhde,bhe->bhd', C, qt)
                denom = jnp.maximum(jnp.abs(jnp.einsum('bhd,bhd->bh', n, qt)), 1.0)[..., None]
                return ((C, n), ht / denom)
            _, ys = jax.lax.scan(step, (C0, n0), (qs, ks_, vs, ig, fg))
            return jnp.moveaxis(ys, 0, 1)
        b, t, dm = x.shape
        h_heads = wi.shape[1]
        dd = dm // h_heads
        h = _rmsnorm(x, ln1_w)
        q = (h @ wq).reshape(b, t, h_heads, dd)
        k = (h @ wk).reshape(b, t, h_heads, dd)
        v = (h @ wv).reshape(b, t, h_heads, dd)
        i_gate = jnp.exp(jnp.clip(h @ wi + bi, -10.0, 10.0))
        f_gate = jax.nn.sigmoid(h @ wf + bf)
        y = _xlstm_scan(q, k, v, i_gate, f_gate).reshape(b, t, dm)
        x = x + y @ wo
        h2 = _rmsnorm(x, ln2_w)
        mlp = jax.nn.silu(h2 @ w_gate) * (h2 @ w_up) @ w_down
        return x + mlp

    def _L0_ffn_ref(hidden_states, gate_W, gate_b, wi_W, wi_b, wo_W, wo_b, lora_A, lora_B):
        import jax, jax.numpy as jnp
        import numpy as np
        B, S, D, F, E, R = (4, 512, 256, 1024, 8, 4)
        x = hidden_states
        logits = jnp.einsum('bsd,ed->bse', x, gate_W) + gate_b
        top1 = jnp.argmax(jax.nn.softmax(logits, axis=-1), axis=-1)
        base = jnp.einsum('bsd,fd->bsf', x, wi_W) + wi_b
        out = jnp.zeros_like(x)
        for i in range(lora_A.shape[0]):
            lora = jnp.einsum('bsr,fr->bsf', jnp.einsum('bsd,rd->bsr', x, lora_A[i]), lora_B[i])
            inter = jax.nn.relu(base + lora)
            expert_out = jnp.einsum('bsf,df->bsd', inter, wo_W) + wo_b
            mask = (top1 == i).astype(x.dtype)[..., None]
            out = out + mask * expert_out
        return out
    x = L0_attn_x
    x = x + 0.5 * _L0_ffn_ref(_layernorm(x, axis=-1), L0_ffn_gate_W, L0_ffn_gate_b, L0_ffn_wi_W, L0_ffn_wi_b, L0_ffn_wo_W, L0_ffn_wo_b, L0_ffn_lora_A, L0_ffn_lora_B)
    x = x + _L0_attn_ref(_layernorm(x, axis=-1), L0_attn_ln1_w, L0_attn_ln2_w, L0_attn_wq, L0_attn_wk, L0_attn_wv, L0_attn_wo, L0_attn_wi, L0_attn_bi, L0_attn_wf, L0_attn_bf, L0_attn_w_gate, L0_attn_w_up, L0_attn_w_down)
    x = x + 0.5 * _L0_ffn_ref(_layernorm(x, axis=-1), L0_ffn_gate_W, L0_ffn_gate_b, L0_ffn_wi_W, L0_ffn_wi_b, L0_ffn_wo_W, L0_ffn_wo_b, L0_ffn_lora_A, L0_ffn_lora_B)
    return x

_drawn_inputs = setup_inputs


def setup_inputs(seed=0):
    import zlib

    import numpy as np

    out = dict(_drawn_inputs(seed))
    spreads = {'L0_attn_ln1_w': (1.0, 0.6),
     'L0_attn_ln2_w': (1.0, 0.6),
     'L0_attn_bi': (0.0, 0.8),
     'L0_attn_bf': (3.0, 0.6),
     'L0_ffn_gate_b': (0.0, 0.8),
     'L0_ffn_wi_b': (0.0, 0.1),
     'L0_ffn_wo_b': (0.0, 0.1)}
    factors = {'L0_attn_wi': 2.754,
     'L0_attn_wf': 8.0,
     'L0_attn_w_gate': 3.959,
     'L0_attn_w_up': 3.924,
     'L0_attn_w_down': 3.929,
     'L0_ffn_gate_W': 3.578,
     'L0_ffn_lora_A': 3.286,
     'L0_ffn_lora_B': 3.277}
    for name, (base, spread) in spreads.items():
        noise = np.random.default_rng([zlib.crc32(name.encode()), seed]).standard_normal(out[name].shape)
        drawn = base * np.exp(spread * noise) if base else spread * noise
        out[name] = jnp.asarray(drawn.astype(out[name].dtype))
    for name, factor in factors.items():
        out[name] = (out[name] * factor).astype(out[name].dtype)
    return out
```

```python
import numpy as np

import concourse.bass as bass
import concourse.mybir as mybir
from concourse.alu_op_type import AluOpType as ALU

P = 128
N_SEQ, SEQ, D = 4, 1024, 256
TILES = 4
BLOCK = TILES * P
BLOCKS = N_SEQ * SEQ // BLOCK
DC = D // P
F = 1024
FT = F // P
E, R = 8, 4
ER = E * R
GW = E + ER
H, HD = 16, 16
HV = HD + 1
HH = P // HD
I = 704
IT = -(-I // P)
KI = D + 2 * H
QUAD = 4
NQ = H // QUAD
SLOTS = 6
STACK = SLOTS * HD
LS = 3 * ER
LS2 = LS + 2

F32, F32R, BF16 = mybir.dt.float32, mybir.dt.float32r, mybir.dt.bfloat16
ACT = mybir.ActivationFunctionType
AX_X = mybir.AxisListType.X


class Signal:

    def __init__(self, sem, per, step=1):
        self.sem, self.per, self.step = sem, per, step

    def at(self, run, count):
        value = (run * self.per + count) * self.step
        return max(value, 0) if isinstance(value, int) else value


def iteration(ffn2, att, ffn1, ffn2_next):
    present = {"2": ffn2, "a": att, "1": ffn1, "n": ffn2_next}
    steps = ["1 load", "2 tr", "a ln", "2 gate", "a tr", "2 up 0", "a q 0", "2 lora", "a q 1", "2 up 1", "2 act 0",
             "a kv 0", "2 act 1", "2 down 0", "2 up 2", "a kv 1", "2 act 2", "2 down 1", "2 up 3", "a kv 2", "2 act 3",
             "2 down 2", "2 up 4", "a kv 3", "2 act 4", "2 down 3", "a kT", "a fT", "2 up 5", "1 ln", "2 act 5",
             "a decay", "a stack 0", "2 down 4", "2 up 6", "2 act 6", "2 down 5", "2 up 7", "2 act 7", "2 down 6",
             "2 down 7", "2 fin", "1 tr"]
    steps += ["1 gate", "1 up 0", "1 lora", "1 up 1"]
    for j in range(TILES):
        u = NQ * j
        steps += [f"a score {u}", f"a score {u + 1}"]
        if j:
            steps += [f"a yT {j - 1}", f"1 act {j}", f"a wo {j - 1}", f"1 down {j}"]
        else:
            steps += [f"1 act {j}", f"1 down {j}"]
        steps += [f"a mix {u}", f"a score {u + 2}", f"a mix {u + 1}", f"a score {u + 3}", f"a mix {u + 2}",
                  f"1 up {j + 2}", f"a mix {u + 3}", f"a carry {j}"]
        if j == 1:
            steps += ["a stack 1"]
    steps += [f"1 act {TILES}", f"a yT {TILES - 1}", f"1 down {TILES}", f"a wo {TILES - 1}", "1 act 5", "a ln2",
              "1 up 6", "1 down 5", "1 act 6", "a tr2"]
    for i in range(IT):
        steps += [f"a gu {i}"]
        if i == 0:
            steps += ["1 up 7", "1 act 7"]
        if i:
            steps += [f"a mdown {i - 1}"]
    steps += ["1 down 6", f"a mdown {IT - 1}", "a mfin", "n ln", "1 down 7", "1 fin"]
    for text in steps:
        stage, step, *k = text.split()
        if present[stage]:
            yield stage, step, int(k[0]) if k else 0


def build(nc, a, out):
    from contextlib import ExitStack

    ctx = ExitStack()
    with ctx:
        def sb(name, shape, dt=F32):
            return ctx.enter_context(nc.sbuf_tensor(name, shape, dt))

        def sig(name, per=1, step=1):
            return Signal(ctx.enter_context(nc.semaphore(name)), per, step)

        ident = sb("ident", [P, P])
        ident4 = sb("ident4", [P, QUAD * P])
        headmask = sb("headmask", [P, DC * HH * HV])
        headsel = sb("headsel", [H, DC, P])
        prio = sb("prio", [P, TILES, E])
        zeros = sb("zeros", [H, P])
        minus_half = sb("minus_half", [P, TILES])
        def pair(name, shape):
            return sb(name + "_hi", shape, F32R), sb(name + "_lo", shape, F32R)

        wi_h, wi_l = pair("wi", [P, DC, F])
        wo_h, wo_l = pair("wo", [P, FT, D])
        wq_h, wq_l = pair("wq", [P, DC, D])
        wkv_h, wkv_l = pair("wkv", [P, DC, KI + D])
        wao_h, wao_l = pair("wao", [P, DC, D])
        wgu_h, wgu_l = pair("wgu", [P, DC, 2 * I])
        wd_h, wd_l = pair("wd", [P, IT, D])
        lora_b = sb("lora_b", [P, F], F32R)
        route_w = sb("route_w", [P, DC, GW])
        route_b = sb("route_b", [P, E])
        half_wo_b = sb("half_wo_b", [P, D])
        gate_bias = sb("gate_bias", [P, 2 * H])
        ln1 = sb("ln1", [P, DC])
        ln2 = sb("ln2", [P, DC])
        x_in = sb("x_in", [P, TILES, D])
        x_mid = sb("x_mid", [P, TILES, D])
        x_out = sb("x_out", [P, TILES, D])
        f_st = sb("f_st", [P, TILES, 6])
        f_mv = sb("f_mv", [P, 6, TILES])
        f_ve = sb("f_ve", [P, TILES])
        f_rs = sb("f_rs", [P, TILES])
        xn = sb("xn", [P, TILES, D])
        xT = sb("xT", [P, DC, BLOCK])
        xT_h, xT_l = pair("xT", [P, DC, BLOCK])
        lg = sb("lg", [P, TILES, E])
        lmax = sb("lmax", [P, TILES])
        won = sb("won", [P, TILES, E])
        won2 = sb("won2", [P, TILES, E])
        wmax = sb("wmax", [P, TILES])
        onehot = sb("onehot", [P, TILES, E])
        u_rep = sb("u_rep", [P, TILES, 3, ER])
        u_st = sb("u_st", [P, BLOCK], F32R)
        narrow = sb("narrow", [P, BLOCK])
        fT = narrow[0:H].rearrange("h (j t) -> h j t", j=TILES)
        fTz = narrow[32:32 + H].rearrange("h (j t) -> h j t", j=TILES)
        u_hi = narrow[2 * ER:LS]
        r_h = sb("r_h", [P, 2, BLOCK], F32R)
        r_l = sb("r_l", [P, 2, BLOCK], F32R)
        a_st = sb("a_st", [P, TILES, 6])
        a_mv = sb("a_mv", [P, 6, TILES])
        a_sm = sb("a_sm", [P, 6, TILES])
        z = sb("z", [P, TILES, D])
        xc = sb("xc", [P, TILES, D])
        hn = sb("hn", [P, TILES, D])
        hT_h, hT_l = pair("hT", [P, DC, BLOCK])
        q32 = sb("q32", [P, DC, BLOCK])
        pa = sb("pa", [P, DC, BLOCK], BF16)
        pb = sb("pb", [P, DC, BLOCK], BF16)
        pc = sb("pc", [P, DC, BLOCK], BF16)
        r1 = hn[:].rearrange("p (c k) d -> p c (k d)", c=DC)
        k32 = sb("k32", [P, TILES, D])
        vp = sb("vp", [P, TILES, H, HV])
        g32 = sb("g32", [P, TILES, 2 * H])
        fg = sb("fg", [P, TILES, H])
        cumT = sb("cumT", [H, TILES, P])
        decay = sb("decay", [P, TILES * H + DC * TILES])
        dm = sb("dm", [P, NQ, QUAD * P])
        arena = sb("arena", [P, 2, H * BLOCK // 4])
        qs, ks = (arena[0:STACK, n].bitcast(BF16).rearrange("k (h t) -> k h t", h=H) for n in range(2))
        pt = sb("pt", [P, 2, QUAD * P])
        wv = sb("wv", [P, H, HV])
        cb = sb("cb", [P, DC, HH * HV])
        cm = sb("cm", [P, DC, HH * HV])
        keep = sb("keep", [P, 1])
        o1 = sb("o1", [P, H, HV])
        den = sb("den", [P, 3, H])
        y = sb("y", [P, 2, D])
        yT_h, yT_l = pair("yT", [P, DC, P])
        th, gm = pt[:, 0], pt[:, 1]
        m_h = sb("m_h", [P, 2, BLOCK], F32R)
        m_l = sb("m_l", [P, 2, BLOCK], F32R)

        wo_b = y[:, 0]
        psum = [ctx.enter_context(nc.psum_tensor(f"bank{n}", [P, 512], F32)) for n in range(8)]
        T, U, A = psum[0:2], psum[2:4], psum[4:8]

        parts_d = nc.dram_tensor("parts_scratch", (2, 3, H, HD, BLOCK), BF16).ap()
        f_d = nc.dram_tensor("f_scratch", (TILES, NQ, QUAD * P), F32).ap()

        s_const = sig("const_loaded", 1, 16)
        s_early = [sig(f"early_loaded{n}", 1, 16) for n in range(5)]
        s_early_hi, s_early_lo = sig("early_hi"), sig("early_lo")
        s_late = [sig(f"late_loaded{n}", 1, 16) for n in range(2)]
        s_late_scaled, s_late_hi, s_late_lo = sig("late_scaled"), sig("late_hi"), sig("late_lo")
        s_setup = sig("setup_done")
        n_setup = 7
        s_xin = sig("x_loaded", 1, 16)
        s_xout = sig("x_stored", 1, 16)
        f_stats, f_mean, f_var = sig("f_stats", TILES), sig("f_mean", 6), sig("f_var")
        f_rstd, f_xn, f_xb = sig("f_rstd"), sig("f_xn", TILES), sig("f_xb")
        f_tr, f_x32, f_xh, f_xl = sig("f_tr", DC), sig("f_x32", DC), sig("f_xh", DC), sig("f_xl", DC)
        f_route, f_sel, f_u = sig("f_route"), sig("f_sel", 6), sig("f_u", 3)
        f_uT, f_uh, f_ul = sig("f_uT"), sig("f_uh", 2), sig("f_ul")
        f_up, f_rh, f_rl, f_dn, f_y = sig("f_up", FT), sig("f_rh", FT), sig("f_rl", FT), sig("f_dn", FT), sig("f_y", TILES)
        a_stats, a_mean, a_small = sig("a_stats", 2 * TILES), sig("a_mean", 11), sig("a_small", 7)
        a_pow = sig("a_pow", 3)
        a_z, a_h, a_xc, a_xx = sig("a_z", TILES), sig("a_h", 2 * TILES), sig("a_xc"), sig("a_xx")
        a_tr, a_hh, a_hl = sig("a_tr", 2 * DC), sig("a_hh", 2 * DC), sig("a_hl", 2 * DC)
        a_q, a_q32 = sig("a_q", DC), sig("a_q32", DC)
        a_pa, a_r1, a_pb, a_pc = sig("a_pa", 2 * DC), sig("a_r1", 2 * DC), sig("a_pb", 2 * DC), sig("a_pc", 2 * DC)
        a_kv, a_k32, a_g, a_clip = sig("a_kv", 2 * TILES), sig("a_k32", TILES), sig("a_g", TILES), sig("a_clip", TILES)
        a_i, a_tf, a_v, a_f = sig("a_i", TILES), sig("a_tf", TILES), sig("a_v", TILES), sig("a_f", TILES)
        a_kT, a_fT, a_fTs, a_cum = sig("a_kT", DC), sig("a_fT"), sig("a_fTs", 2), sig("a_cum", TILES)
        a_dT, a_dec = sig("a_dT"), sig("a_dec")
        d_parts = sig("d_parts", 2 * 3 * DC, 16)
        d_f = sig("d_f", NQ, 16)
        d_stack = sig("d_stack", 2 * 2 * SLOTS, 16)
        d_fb = [sig(f"d_fb{n}", TILES, 16) for n in range(NQ)]
        a_D, a_S, a_P, a_wv, a_O = (sig(n, TILES * NQ) for n in ("a_D", "a_S", "a_P", "a_wv", "a_O"))
        a_oi, a_t1, a_o, a_den, a_y = sig("a_oi", TILES), sig("a_t1", TILES), sig("a_o", TILES), sig("a_den", 3 * TILES), sig("a_y", TILES)
        a_state, a_cm, a_cb = sig("a_state", TILES), sig("a_cm", TILES), sig("a_cb", 2 * TILES + 2)
        a_yT, a_yh, a_yl, a_wo, a_x2 = (sig(n, TILES) for n in ("a_yT", "a_yh", "a_yl", "a_wo", "a_x2"))
        a_gu, a_th, a_m1, a_m, a_mh, a_ml, a_md = sig("a_gu", 2 * IT), sig("a_th", IT), sig("a_m1", IT), sig("a_m", IT), sig("a_mh", IT), sig("a_ml", IT), sig("a_md", IT)
        a_x3 = sig("a_x3", TILES)


        woT = a["wo"].rearrange("(c p) n -> p c n", p=P)
        half_ft = FT // 2
        early = [(z, a["wi"][0:P], wi_h[:, 0], wi_l[:, 0]), (xc, a["wi"][P:D], wi_h[:, 1], wi_l[:, 1]),
                 (x_mid, a["lora"], lora_b[0:LS2], None),
                 (hn, woT[:, 0:half_ft], wo_h[:, 0:half_ft], wo_l[:, 0:half_ft]),
                 (q32, woT[:, half_ft:FT], wo_h[:, half_ft:FT], wo_l[:, half_ft:FT])]
        n_early_lo = len(early) + 1

        wgu_in = [(a["wgu"][c * P:(c + 1) * P].unsqueeze(1), wgu_h[:, c:c + 1], wgu_l[:, c:c + 1], ln2[:, c:c + 1], 1.0)
                  for c in range(DC)]
        rows_of = lambda name: a[name].rearrange("(c p) n -> p c n", p=P)
        last_rows = I - (IT - 1) * P
        late = [(rows_of("wq"), wq_h, wq_l, ln1, 1.0), (rows_of("wkv"), wkv_h, wkv_l, ln1, 1.0),
                (rows_of("wao"), wao_h, wao_l, None, 1.0), *wgu_in,
                (a["wd"][0:(IT - 1) * P].rearrange("(c p) n -> p c n", p=P), wd_h[:, 0:IT - 1], wd_l[:, 0:IT - 1], None, 0.5),
                (a["wd"][(IT - 1) * P:I].unsqueeze(1), wd_h[0:last_rows, IT - 1:IT], wd_l[0:last_rows, IT - 1:IT], None, 0.5)]

        def late_stage(n):
            hi = late[n][1]
            rows, c, cols = hi.shape
            return arena[0:rows, n % 2, 0:c * cols].rearrange("p (c n) -> p c n", c=c)

        consts = [(ident[:], a["ident"]), (ident4[:], a["ident4"]), (headmask[:], a["headmask"]),
                  (headsel[:], a["headsel"]), (prio[:], a["prio"]),
                  (route_w[:], a["route_w"].rearrange("(c p) n -> p c n", p=P)),
                  (route_b[:], a["route_b"].partition_broadcast(P)),
                  (wo_b, a["wo_b"].partition_broadcast(P)),
                  (gate_bias[:], a["gate_bias"].partition_broadcast(P)),
                  (ln1[:], a["ln1"]), (ln2[:], a["ln2"])]

        def flat(ap):
            return ap.rearrange("p a b -> p (a b)") if len(ap.shape) == 3 else ap

        def held(engine, value):
            return value if isinstance(value, int) else engine.snap(value)

        def ffn1_run(b):
            return 0 if isinstance(b, int) and b == 0 else b * 2 - 1

        def schedule(engine, steps):
            def play(t, run2, att, run1, run_next):
                for stage, step, k in iteration(run2 is not None, att is not None, run1 is not None, run_next is not None):
                    f = steps.get(("a_" if stage == "a" else "f_") + step)
                    if f and stage == "a":
                        f(att, k)
                    elif f:
                        f(*{"1": (run1, t, True), "2": (run2, t - 2, False), "n": (run_next, t - 1, False)}[stage], k)
                    if t is first and step == "ln" and "setup" in steps:
                        steps["setup"]()

            first = 0
            play(first, None, None, 0, None)
            first = None
            play(1, None, 0, 1, 2)
            with engine.Fori(2, BLOCKS) as t:
                play(t, t * 2 - 2, t - 1, t * 2 - 1, t * 2)
            play(BLOCKS, 2 * BLOCKS - 2, BLOCKS - 1, None, 2 * BLOCKS - 1)
            play(BLOCKS + 1, 2 * BLOCKS - 1, None, None, None)

        block = ctx.enter_context(nc.Block())

        @block.sync
        def _(sp):
            def load_x(b):
                sp.dma_start(x_in[:], a["x"][bass.ds(b, 1)].rearrange("a j p d -> p (a j) d")).then_inc(s_xin.sem, 16)

            sp.dma_start(x_in[:], a["x"][0].rearrange("j p d -> p j d")).then_inc(s_xin.sem, 16)
            for n, (stage, src, hi, lo) in enumerate(early):
                dst = stage[0:hi.shape[0]]
                if len(src.shape) == 2:
                    dst = flat(dst)
                sp.dma_start(dst, src).then_inc(s_early[n].sem, 16)
                if n == 0:
                    for to, of in consts:
                        sp.dma_start(to, of).then_inc(s_const.sem, 16)
            for n, (src, hi, lo, _, _) in enumerate(late):
                sp.wait_ge(s_late_lo.sem, s_late_lo.at(0, n - 1))
                sp.dma_start(late_stage(n), src).then_inc(s_late[n % 2].sem, 16)

            def load(run, b, first, k):
                if isinstance(b, int) and b == 0:
                    return
                value = held(sp, f_y.at(ffn1_run(b - 1), TILES))
                sp.wait_ge(s_const.sem, s_const.at(len(consts), 0))
                sp.wait_ge(f_y.sem, value)
                load_x(b)

            def fin(run, b, first, k):
                if not first:
                    value = held(sp, f_y.at(run, TILES))
                    sp.wait_ge(s_const.sem, s_const.at(len(consts), 0))
                    sp.wait_ge(f_y.sem, value)
                    sp.dma_start(out[bass.ds(b, 1)].rearrange("a j p d -> p (a j) d"), x_out[:]).then_inc(s_xout.sem, 16)

            def store_parts(b, u):
                for n, (sem, part) in enumerate(((a_pa, pa), (a_pb, pb), (a_pc, pc))):
                    sp.wait_ge(sem.sem, sem.at(b, DC * (u + 1)))
                    for m in range(DC):
                        sp.dma_start(parts_d[u, n, m * HH:(m + 1) * HH].rearrange("h e t -> (h e) t"), part[:, m]
                                     ).then_inc(d_parts.sem, 16)

            def q(b, m):
                if m == DC - 1:
                    sp.wait_ge(d_stack.sem, d_stack.at(b - 1, 2 * 2 * SLOTS))
                    store_parts(b, 0)

            def load_stack(b, half):
                sp.wait_ge(d_parts.sem, d_parts.at(b, 2 * 3 * DC))
                if half:
                    sp.wait_ge(a_S.sem, a_S.at(b, TILES * NQ // 2))
                else:
                    sp.wait_ge(a_S.sem, a_S.at(b - 1, TILES * NQ))
                for u, (dst, order) in enumerate(((qs, (0, 0, 1, 1, 0, 2)), (ks, (0, 1, 0, 1, 2, 0)))):
                    for slot, n in enumerate(order):
                        src = parts_d[u, n, :, :, half * (BLOCK // 2):(half + 1) * (BLOCK // 2)]
                        sp.dma_start(dst[slot * HD:(slot + 1) * HD], src.rearrange("h e t -> e h t")).then_inc(d_stack.sem, 16)

            def load_f(b, u):
                j, g = divmod(u, NQ)
                value = held(sp, d_f.at(b, NQ))
                sp.wait_ge(s_const.sem, s_const.at(len(consts), 0))
                sp.wait_ge(d_f.sem, value)
                sp.wait_ge(a_P.sem, a_P.at(b, u - NQ + 1))
                sp.wait_ge(a_wv.sem, a_wv.at(b, u - NQ + 1))
                sp.dma_start(dm[:, g], f_d[j, g].partition_broadcast(P)).then_inc(d_fb[g].sem, 16)

            def fT_(b, k):
                store_parts(b, 1)
                sp.wait_ge(a_fTs.sem, a_fTs.at(b, 1))
                for g in range(NQ):
                    sp.wait_ge(d_fb[g].sem, d_fb[g].at(b - 1, TILES))
                for g in range(NQ):
                    sp.dma_start(f_d[:, g].rearrange("j (h t) -> h j t", h=QUAD), fTz[QUAD * g:QUAD * (g + 1)]).then_inc(d_f.sem, 16)
                for u in range(NQ):
                    load_f(b, u)

            def mix(b, u):
                if u + NQ < TILES * NQ:
                    load_f(b, u + NQ)

            schedule(sp, {"f_load": load, "f_fin": fin, "a_q": q, "a_fT": fT_, "a_stack": load_stack, "a_mix": mix})
            sp.wait_ge(s_xout.sem, s_xout.at(BLOCKS, 0))

        @block.gpsimd
        def _(pool):
            nc.gpsimd.memset(minus_half[:], -0.5).then_inc(s_setup.sem, 1)

            def split_late():
                pool.wait_ge(s_const.sem, s_const.at(len(consts), 0))
                pool.wait_ge(s_early_lo.sem, s_early_lo.at(n_early_lo, 0))
                scaled = 0
                for n, (src, hi, lo, factors, const) in enumerate(late):
                    s = late_stage(n)
                    pool.wait_ge(s_late[n % 2].sem, s_late[n % 2].at(n // 2 + 1, 0))
                    if factors is not None:
                        for c in range(hi.shape[1]):
                            nc.gpsimd.tensor_scalar(s[:, c], s[:, c], factors[:, c:c + 1], 1.0, ALU.mult, ALU.mult
                                                    ).then_inc(s_late_scaled.sem, 1)
                        scaled += hi.shape[1]
                    elif const != 1.0:
                        nc.gpsimd.tensor_scalar(s, s, const, 1.0, ALU.mult, ALU.mult).then_inc(s_late_scaled.sem, 1)
                        scaled += 1
                    pool.wait_ge(s_late_scaled.sem, s_late_scaled.at(scaled, 0))
                    nc.gpsimd.tensor_copy(hi[:], s).then_inc(s_late_hi.sem, 1)
                    pool.wait_ge(s_late_hi.sem, s_late_hi.at(n + 1, 0))
                    nc.gpsimd.tensor_tensor(lo[:], s, hi[:].bitcast(F32), ALU.subtract).then_inc(s_late_lo.sem, 1)

            def ln(run, b, first, k):
                if isinstance(run, int) and run == 0:
                    pool.wait_ge(s_setup.sem, s_setup.at(n_setup, 0))
                pool.wait_ge(f_var.sem, f_var.at(run, 1))
                nc.gpsimd.tensor_tensor(f_rs[:], f_ve[:], minus_half[:], ALU.pow).then_inc(f_rstd.sem, 1)
                pool.wait_ge(f_xn.sem, f_xn.at(run, TILES))
                x = x_in if first else x_out
                bias = half_wo_b[:].unsqueeze(1).to_broadcast([P, TILES, D])
                nc.gpsimd.tensor_tensor(x[:], x[:], bias, ALU.add).then_inc(f_xb.sem, 1)

            def aln(b, k):
                pool.wait_ge(a_x3.sem, a_x3.at(b - 1, TILES))
                pool.wait_ge(a_small.sem, a_small.at(b, 1))
                nc.gpsimd.tensor_tensor(a_sm[:, 1], a_sm[:, 0], minus_half[:], ALU.pow).then_inc(a_pow.sem, 1)
                pool.wait_ge(a_small.sem, a_small.at(b, 6))
                nc.gpsimd.tensor_tensor(a_sm[:, 2], a_sm[:, 0], minus_half[:], ALU.pow).then_inc(a_pow.sem, 1)
                nc.gpsimd.tensor_copy(xc[:], x_mid[:]).then_inc(a_xc.sem, 1)

            def split(b, u):
                for m in range(DC):
                    n = DC * u + m
                    pool.wait_ge(a_pb.sem, a_pb.at(b, n + 1))
                    nc.gpsimd.tensor_tensor(pc[:, m], r1[:, m], pb[:, m], ALU.subtract).then_inc(a_pc.sem, 1)

            def mix(b, u):
                j, g = divmod(u, NQ)
                pool.wait_ge(a_D.sem, a_D.at(b, u + 1))
                if j:
                    pool.wait_ge(a_state.sem, a_state.at(b, j))
                else:
                    pool.wait_ge(a_state.sem, a_state.at(b - 1, TILES))
                w = dm[:, g].rearrange("p (h t) -> p h t", h=QUAD)[:, :, P - 1:P].to_broadcast([P, QUAD, HV])
                heads = slice(QUAD * g, QUAD * (g + 1))
                pool.wait_ge(a_v.sem, a_v.at(b, j + 1))
                nc.gpsimd.tensor_tensor(wv[:, heads], vp[:, j, heads], w, ALU.mult).then_inc(a_wv.sem, 1)

            def aln2(b, k):
                pool.wait_ge(a_x2.sem, a_x2.at(b, TILES))
                pool.wait_ge(a_small.sem, a_small.at(b, 7))
                nc.gpsimd.tensor_tensor(a_sm[:, 4], a_sm[:, 3], minus_half[:], ALU.pow).then_inc(a_pow.sem, 1)
                nc.gpsimd.tensor_tensor(xc[:], xc[:], z[:], ALU.add).then_inc(a_xx.sem, 1)

            def gu(b, i):
                rows = P if i < IT - 1 else last_rows
                pool.wait_ge(a_mh.sem, a_mh.at(b, i + 1))
                if i > 1:
                    pool.wait_ge(a_md.sem, a_md.at(b, i - 1))
                nc.gpsimd.tensor_tensor(m_l[:rows, i % 2], gm[:rows], m_h[:rows, i % 2].bitcast(F32), ALU.subtract
                                        ).then_inc(a_ml.sem, 1)

            schedule(pool, {"setup": split_late, "f_ln": ln, "a_ln": aln, "a_q": lambda b, m: split(b, 0) if m else None,
                            "a_kT": lambda b, k: split(b, 1), "a_mix": mix, "a_ln2": aln2, "a_gu": gu})

        @block.scalar
        def _(act):
            act.wait_ge(s_const.sem, s_const.at(len(consts), 0))
            nc.scalar.mul(half_wo_b[:], wo_b, 0.5).then_inc(s_setup.sem, 1)
            for n, (stage, src, hi, lo) in enumerate(early):
                act.wait_ge(s_early[n].sem, s_early[n].at(1, 0))
                nc.scalar.copy(flat(hi), flat(stage[0:hi.shape[0]])).then_inc(s_early_hi.sem, 1)
                if lo is None:
                    act.wait_ge(s_early_lo.sem, s_early_lo.at(n + 1, 0))
                    nc.scalar.copy(hi[LS:LS + 1], flat(stage[LS:LS + 1])).then_inc(s_early_hi.sem, 1)

            def tr(run, b, first, k):
                for c in range(DC):
                    act.wait_ge(f_tr.sem, f_tr.at(run, c + 1))
                    act.wait_ge(f_route.sem, f_route.at(run - 1, 1))
                    nc.scalar.copy(xT[:, c], T[c][:]).then_inc(f_x32.sem, 1)
                    act.wait_ge(f_up.sem, f_up.at(run - 1, FT))
                    nc.scalar.copy(xT_h[:, c], T[c][:]).then_inc(f_xh.sem, 1)

            def lora(run, b, first, k):
                act.wait_ge(f_uT.sem, f_uT.at(run, 1))
                nc.scalar.copy(u_st[0:2 * ER], T[1][0:2 * ER]).then_inc(f_uh.sem, 1)
                act.wait_ge(f_ul.sem, f_ul.at(run - 1, 1))
                nc.scalar.copy(u_hi.bitcast(F32R), T[1][2 * ER:LS]).then_inc(f_uh.sem, 1)

            def relu(run, b, first, f):
                act.wait_ge(f_up.sem, f_up.at(run, f + 1))
                act.wait_ge(f_dn.sem, f_dn.at(run, f - 1))
                nc.scalar.activation(r_h[:, f % 2], U[f % 2][:], ACT.Relu).then_inc(f_rh.sem, 1)

            def atr(b, k):
                for c in range(DC):
                    act.wait_ge(a_tr.sem, a_tr.at(b, c + 1))
                    act.wait_ge(a_gu.sem, a_gu.at(b - 1, 2 * IT))
                    nc.scalar.copy(hT_h[:, c], A[c][:]).then_inc(a_hh.sem, 1)

            def atr2(b, k):
                for c in range(DC):
                    act.wait_ge(a_tr.sem, a_tr.at(b, DC + c + 1))
                    act.wait_ge(a_kv.sem, a_kv.at(b, 2 * TILES))
                    nc.scalar.copy(hT_h[:, c], A[c][:]).then_inc(a_hh.sem, 1)

            def q(b, m):
                act.wait_ge(a_q.sem, a_q.at(b, m + 1))
                act.wait_ge(a_oi.sem, a_oi.at(b - 1, TILES))
                nc.scalar.copy(q32[:, m], A[2 + m][:]).then_inc(a_q32.sem, 1)
                act.wait_ge(d_parts.sem, d_parts.at(b - 1, 6 * DC))
                nc.scalar.copy(pa[:, m], A[2 + m][:]).then_inc(a_pa.sem, 1)
                second_part(b, m)

            def second_part(b, n):
                act.wait_ge(a_r1.sem, a_r1.at(b, n + 1))
                nc.scalar.copy(pb[:, n % DC], r1[:, n % DC]).then_inc(a_pb.sem, 1)

            def kv(b, j):
                act.wait_ge(a_kv.sem, a_kv.at(b, 2 * j + 1))
                act.wait_ge(a_state.sem, a_state.at(b - 1, TILES))
                nc.scalar.copy(k32[:, j], A[0][:, 0:D]).then_inc(a_k32.sem, 1)
                act.wait_ge(a_clip.sem, a_clip.at(b, j + 1))
                act.wait_ge(a_wv.sem, a_wv.at(b - 1, TILES * NQ))
                act.wait_ge(a_O.sem, a_O.at(b - 1, TILES * NQ))
                nc.scalar.activation(vp[:, j, :, HD], g32[:, j, 0:H], ACT.Exp).then_inc(a_i.sem, 1)
                nc.scalar.activation(fg[:, j], g32[:, j, H:2 * H], ACT.Tanh, scale=0.5).then_inc(a_tf.sem, 1)

            def kT(b, k):
                act.wait_ge(d_parts.sem, d_parts.at(b, 3 * DC))
                for m in range(DC):
                    act.wait_ge(a_kT.sem, a_kT.at(b, m + 1))
                    nc.scalar.copy(pa[:, m], A[2 + m][:]).then_inc(a_pa.sem, 1)
                for m in range(DC):
                    second_part(b, DC + m)

            def fT_(b, k):
                act.wait_ge(a_fT.sem, a_fT.at(b, 1))
                act.wait_ge(d_f.sem, d_f.at(b - 1, NQ))
                src = A[0][0:H].rearrange("h (j t) -> h j t", j=TILES)
                nc.scalar.copy(fTz[:, :, 1:P], src[:, :, 1:P]).then_inc(a_fTs.sem, 1)
                nc.scalar.copy(fT[:], src).then_inc(a_fTs.sem, 1)

            def dec(b, k):
                act.wait_ge(a_dT.sem, a_dT.at(b, 1))
                act.wait_ge(a_cb.sem, a_cb.at(b, 0))
                nc.scalar.copy(decay[:], A[1][:, 0:TILES * H + DC * TILES]).then_inc(a_dec.sem, 1)

            def yT_(b, j):
                act.wait_ge(a_yT.sem, a_yT.at(b, j + 1))
                if j:
                    act.wait_ge(a_wo.sem, a_wo.at(b, j))
                else:
                    act.wait_ge(a_wo.sem, a_wo.at(b - 1, TILES))
                nc.scalar.copy(flat(yT_h[:]), A[0][:, 0:D]).then_inc(a_yh.sem, 1)

            def gu(b, i):
                rows = P if i < IT - 1 else last_rows
                act.wait_ge(a_gu.sem, a_gu.at(b, 2 * i + 1))
                nc.scalar.activation(th[:rows], A[2][:rows], ACT.Tanh, scale=0.5).then_inc(a_th.sem, 1)
                act.wait_ge(a_m.sem, a_m.at(b, i + 1))
                if i > 1:
                    act.wait_ge(a_md.sem, a_md.at(b, i - 1))
                nc.scalar.copy(m_h[:rows, i % 2], gm[:rows]).then_inc(a_mh.sem, 1)

            schedule(act, {"f_tr": tr, "f_lora": lora, "f_act": relu, "a_tr": atr, "a_q": q, "a_kv": kv, "a_kT": kT,
                           "a_fT": fT_, "a_decay": dec, "a_yT": yT_, "a_tr2": atr2, "a_gu": gu})

        @block.vector
        def _(dve):
            v = nc.vector
            v.memset(cb[:], 0.0).then_inc(s_setup.sem, 1)
            v.memset(keep[:], 1.0).then_inc(s_setup.sem, 1)
            v.memset(zeros[:], 0.0).then_inc(s_setup.sem, 1)
            v.memset(fTz[:], 0.0).then_inc(s_setup.sem, 1)
            v.memset(u_st[LS:P].bitcast(F32), 1.0).then_inc(s_setup.sem, 1)

            def split_early():
                count = 0
                for n, (stage, src, hi, lo) in enumerate(early):
                    s = flat(stage[0:hi.shape[0]])
                    dve.wait_ge(s_early[n].sem, s_early[n].at(1, 0))
                    dve.wait_ge(s_early_hi.sem, s_early_hi.at(n + 1 + (n > 2), 0))
                    if lo is not None:
                        v.tensor_tensor(flat(lo), s, flat(hi).bitcast(F32), ALU.subtract).then_inc(s_early_lo.sem, 1)
                        continue
                    v.tensor_tensor(hi[LS:LS2], s[LS:LS2], hi[LS:LS2].bitcast(F32), ALU.subtract).then_inc(s_early_lo.sem, 1)
                    v.tensor_tensor(hi[ER:2 * ER], s[ER:2 * ER], hi[ER:2 * ER].bitcast(F32), ALU.subtract
                                    ).then_inc(s_early_lo.sem, 1)

            def moments(st, mv, done, run, before, eps):
                means, squares = (st[:, :, 1], st[:, :, 4]), (st[:, :, 2], st[:, :, 5])
                v.tensor_tensor(mv[:, 0], *means, ALU.add).then_inc(done.sem, 1)
                v.tensor_tensor(mv[:, 1], *means, ALU.subtract).then_inc(done.sem, 1)
                v.tensor_tensor(mv[:, 2], *squares, ALU.add).then_inc(done.sem, 1)
                dve.wait_ge(done.sem, done.at(run, before + 1))
                v.tensor_scalar(mv[:, 3], mv[:, 0], 0.5, None, ALU.mult).then_inc(done.sem, 1)
                dve.wait_ge(done.sem, done.at(run, before + 2))
                v.tensor_tensor(mv[:, 4], mv[:, 1], mv[:, 1], ALU.mult).then_inc(done.sem, 1)
                dve.wait_ge(done.sem, done.at(run, before + 3))
                v.tensor_scalar(mv[:, 5], mv[:, 2], 1.0 / D, eps, ALU.mult, ALU.add).then_inc(done.sem, 1)
                dve.wait_ge(done.sem, done.at(run, before + 6))

            def ln(run, b, first, k):
                if first:
                    dve.wait_ge(s_xin.sem, s_xin.at(b, 1))
                    x = x_in
                else:
                    dve.wait_ge(a_x3.sem, a_x3.at(b, TILES))
                    x = x_out
                for j in range(TILES):
                    v.bn_stats(f_st[:, j], x[:, j]).then_inc(f_stats.sem, 1)
                dve.wait_ge(f_stats.sem, f_stats.at(run, TILES))
                moments(f_st, f_mv, f_mean, run, 0, 1e-5)
                v.scalar_tensor_tensor(f_ve[:], f_mv[:, 4], 0.25, f_mv[:, 5], ALU.mult, ALU.add).then_inc(f_var.sem, 1)
                dve.wait_ge(f_rstd.sem, f_rstd.at(run, 1))
                dve.wait_ge(f_tr.sem, f_tr.at(run - 1, DC))
                for j in range(TILES):
                    v.tensor_scalar(xn[:, j], x[:, j], f_mv[:, 3, j:j + 1], f_rs[:, j:j + 1], ALU.subtract, ALU.mult
                                    ).then_inc(f_xn.sem, 1)

            def tr(run, b, first, k):
                for c in range(DC):
                    dve.wait_ge(f_xh.sem, f_xh.at(run, c + 1))
                    v.tensor_tensor(xT_l[:, c], T[c][:], xT_h[:, c].bitcast(F32), ALU.subtract).then_inc(f_xl.sem, 1)

            def gate(run, b, first, k):
                dve.wait_ge(f_route.sem, f_route.at(run, 1))
                routed = T[0][:, 0:TILES * GW].rearrange("p (j n) -> p j n", j=TILES)
                each = lambda t: t[:].unsqueeze(2).to_broadcast([P, TILES, E])
                v.tensor_tensor(lg[:], routed[:, :, 0:E], route_b[:].unsqueeze(1).to_broadcast([P, TILES, E]), ALU.add
                                ).then_inc(f_sel.sem, 1)
                dve.wait_ge(f_sel.sem, f_sel.at(run, 1))
                v.tensor_reduce(lmax[:], lg[:], AX_X, ALU.max).then_inc(f_sel.sem, 1)
                dve.wait_ge(f_sel.sem, f_sel.at(run, 2))
                v.tensor_tensor(won[:], lg[:], each(lmax), ALU.is_ge).then_inc(f_sel.sem, 1)
                dve.wait_ge(f_sel.sem, f_sel.at(run, 3))
                v.tensor_tensor(won2[:], won[:], prio[:], ALU.mult).then_inc(f_sel.sem, 1)
                dve.wait_ge(f_sel.sem, f_sel.at(run, 4))
                v.tensor_reduce(wmax[:], won2[:], AX_X, ALU.max).then_inc(f_sel.sem, 1)
                dve.wait_ge(f_sel.sem, f_sel.at(run, 5))
                v.tensor_tensor(onehot[:], won2[:], each(wmax), ALU.is_equal).then_inc(f_sel.sem, 1)
                dve.wait_ge(f_sel.sem, f_sel.at(run, 6))
                dve.wait_ge(f_uT.sem, f_uT.at(run - 1, 1))
                for n in range(3):
                    v.tensor_tensor(u_rep[:, :, n].rearrange("p j (e r) -> p j e r", e=E),
                                    routed[:, :, E:GW].rearrange("p j (e r) -> p j e r", e=E),
                                    onehot[:].unsqueeze(3).to_broadcast([P, TILES, E, R]), ALU.mult).then_inc(f_u.sem, 1)

            def lora(run, b, first, k):
                dve.wait_ge(f_uh.sem, f_uh.at(run, 2))
                v.tensor_tensor(u_st[2 * ER:LS], T[1][2 * ER:LS], u_hi, ALU.subtract).then_inc(f_ul.sem, 1)

            def relu(run, b, first, f):
                dve.wait_ge(f_rh.sem, f_rh.at(run, f + 1))
                dve.wait_ge(f_dn.sem, f_dn.at(run, f - 1))
                v.scalar_tensor_tensor(r_l[:, f % 2], U[f % 2][:], 0.0, r_h[:, f % 2].bitcast(F32), ALU.max, ALU.subtract
                                       ).then_inc(f_rl.sem, 1)

            def fin(run, b, first, k):
                dve.wait_ge(f_dn.sem, f_dn.at(run, FT))
                dve.wait_ge(f_xb.sem, f_xb.at(run, 1))
                if first:
                    dve.wait_ge(a_xc.sem, a_xc.at(b - 1, 1))
                x, to = (x_in, x_mid) if first else (x_out, x_out)
                for j in range(TILES):
                    v.scalar_tensor_tensor(to[:, j], T[j // 2][:, (j % 2) * D:(j % 2 + 1) * D], 0.5, x[:, j],
                                           ALU.mult, ALU.add).then_inc(f_y.sem, 1)

            def aln(b, k):
                dve.wait_ge(f_y.sem, f_y.at(ffn1_run(b), TILES))
                for j in range(TILES):
                    v.bn_stats(a_st[:, j], x_mid[:, j]).then_inc(a_stats.sem, 1)
                dve.wait_ge(a_stats.sem, a_stats.at(b, TILES))
                moments(a_st, a_mv, a_mean, b, 0, 1e-5)
                v.scalar_tensor_tensor(a_sm[:, 0], a_mv[:, 4], 0.25, a_mv[:, 5], ALU.mult, ALU.add).then_inc(a_small.sem, 1)
                dve.wait_ge(a_pow.sem, a_pow.at(b, 1))
                dve.wait_ge(a_xx.sem, a_xx.at(b - 1, 1))
                v.tensor_scalar(a_sm[:, 5], a_mv[:, 2], 1.0 / D, None, ALU.mult).then_inc(a_small.sem, 1)
                dve.wait_ge(a_small.sem, a_small.at(b, 2))
                v.scalar_tensor_tensor(a_sm[:, 5], a_mv[:, 4], 0.25, a_sm[:, 5], ALU.mult, ALU.add).then_inc(a_small.sem, 1)
                v.tensor_tensor(a_sm[:, 3], a_sm[:, 1], a_sm[:, 1], ALU.mult).then_inc(a_small.sem, 1)
                for j in range(TILES):
                    v.tensor_scalar(z[:, j], x_mid[:, j], a_mv[:, 3, j:j + 1], a_sm[:, 1, j:j + 1], ALU.subtract, ALU.mult
                                    ).then_inc(a_z.sem, 1)
                dve.wait_ge(a_small.sem, a_small.at(b, 4))
                v.tensor_tensor(a_sm[:, 3], a_sm[:, 3], a_sm[:, 5], ALU.mult).then_inc(a_small.sem, 1)
                dve.wait_ge(a_small.sem, a_small.at(b, 5))
                v.tensor_scalar(a_sm[:, 0], a_sm[:, 3], 1e-6, None, ALU.add).then_inc(a_small.sem, 1)
                dve.wait_ge(a_pow.sem, a_pow.at(b, 2))
                dve.wait_ge(a_tr.sem, a_tr.at(b, 0))
                for j in range(TILES):
                    dve.wait_ge(a_z.sem, a_z.at(b, j + 1))
                    v.tensor_scalar(hn[:, j], z[:, j], a_sm[:, 2, j:j + 1], None, ALU.mult).then_inc(a_h.sem, 1)

            def atr(b, k, n=0):
                for c in range(DC):
                    dve.wait_ge(a_hh.sem, a_hh.at(b, n + c + 1))
                    v.tensor_tensor(hT_l[:, c], A[c][:], hT_h[:, c].bitcast(F32), ALU.subtract).then_inc(a_hl.sem, 1)

            def q(b, m):
                dve.wait_ge(a_pa.sem, a_pa.at(b, m + 1))
                dve.wait_ge(a_pc.sem, a_pc.at(b, 0))
                v.tensor_tensor(r1[:, m], A[2 + m][:], pa[:, m], ALU.subtract).then_inc(a_r1.sem, 1)

            def kv(b, j):
                dve.wait_ge(a_k32.sem, a_k32.at(b, j + 1))
                dve.wait_ge(a_tf.sem, a_tf.at(b, 0))
                v.tensor_tensor(g32[:, j], A[0][:, D:D + 2 * H], gate_bias[:], ALU.add).then_inc(a_g.sem, 1)
                dve.wait_ge(a_g.sem, a_g.at(b, j + 1))
                v.tensor_scalar(g32[:, j, 0:H], g32[:, j, 0:H], -10.0, 10.0, ALU.max, ALU.min).then_inc(a_clip.sem, 1)
                dve.wait_ge(a_i.sem, a_i.at(b, j + 1))
                dve.wait_ge(a_kv.sem, a_kv.at(b, 2 * j + 2))
                v.tensor_tensor(vp[:, j, :, 0:HD], A[1][:, 0:D].rearrange("p (h d) -> p h d", h=H),
                                vp[:, j, :, HD:HV].to_broadcast([P, H, HD]), ALU.mult).then_inc(a_v.sem, 1)
                dve.wait_ge(a_tf.sem, a_tf.at(b, j + 1))
                v.tensor_scalar(fg[:, j], fg[:, j], 0.5, 0.5, ALU.mult, ALU.add).then_inc(a_f.sem, 1)

            def kT(b, k):
                for m in range(DC):
                    dve.wait_ge(a_pa.sem, a_pa.at(b, DC + m + 1))
                    dve.wait_ge(a_pc.sem, a_pc.at(b, m + 1))
                    v.tensor_tensor(r1[:, m], A[2 + m][:], pa[:, m], ALU.subtract).then_inc(a_r1.sem, 1)

            def fT_(b, k):
                dve.wait_ge(a_fTs.sem, a_fTs.at(b, 2))
                dve.wait_ge(a_dT.sem, a_dT.at(b, 0))
                for j in range(TILES):
                    v.tensor_tensor_scan(cumT[:, j], fT[:, j], zeros[:], 1.0, ALU.mult, ALU.add).then_inc(a_cum.sem, 1)

            def score(b, u):
                j, g = divmod(u, NQ)
                dve.wait_ge(d_fb[g].sem, d_fb[g].at(b, j + 1))
                v.tensor_tensor_scan(dm[:, g], dm[:, g], ident4[:], 0.0, ALU.mult, ALU.add).then_inc(a_D.sem, 1)
                dve.wait_ge(a_D.sem, a_D.at(b, u + 1))
                dve.wait_ge(a_S.sem, a_S.at(b, u + 1))
                dve.wait_ge(a_O.sem, a_O.at(b, u - 1))
                v.tensor_tensor(pt[:, u % 2], A[2 + u % 2][:], dm[:, g], ALU.mult).then_inc(a_P.sem, 1)

            def carry(b, j):
                heads = lambda bank: bank[:, 0:H * HV].rearrange("p (h d) -> p h d", h=H)
                dve.wait_ge(a_oi.sem, a_oi.at(b, j + 1))
                cum = decay[:, j * H:(j + 1) * H].unsqueeze(2).to_broadcast([P, H, HV])
                v.tensor_tensor(o1[:], heads(A[1]), cum, ALU.mult).then_inc(a_t1.sem, 1)
                dve.wait_ge(a_t1.sem, a_t1.at(b, j + 1))
                dve.wait_ge(a_O.sem, a_O.at(b, NQ * (j + 1)))
                v.tensor_tensor(o1[:], heads(A[0]), o1[:], ALU.add).then_inc(a_o.sem, 1)
                dve.wait_ge(a_o.sem, a_o.at(b, j + 1))
                v.tensor_scalar(den[:, 0], o1[:, :, HD], 1.0, None, ALU.max).then_inc(a_den.sem, 1)
                dve.wait_ge(a_den.sem, a_den.at(b, 3 * j + 1))
                v.scalar_tensor_tensor(den[:, 1], o1[:, :, HD], -1.0, den[:, 0], ALU.mult, ALU.max).then_inc(a_den.sem, 1)
                dve.wait_ge(a_den.sem, a_den.at(b, 3 * j + 2))
                v.reciprocal(den[:, 2], den[:, 1]).then_inc(a_den.sem, 1)
                dve.wait_ge(a_den.sem, a_den.at(b, 3 * j + 3))
                if j > 1:
                    dve.wait_ge(a_yT.sem, a_yT.at(b, j - 1))
                else:
                    dve.wait_ge(a_yT.sem, a_yT.at(b, 0))
                v.tensor_tensor(y[:, j % 2].rearrange("p (h d) -> p h d", h=H), o1[:, :, 0:HD],
                                den[:, 2].unsqueeze(2).to_broadcast([P, H, HD]), ALU.mult).then_inc(a_y.sem, 1)
                dve.wait_ge(a_state.sem, a_state.at(b, j + 1))
                v.tensor_tensor(flat(cm[:]), A[1][:, 0:DC * HH * HV], headmask[:], ALU.mult).then_inc(a_cm.sem, 1)
                dve.wait_ge(a_cm.sem, a_cm.at(b, j + 1))
                for m in range(DC):
                    last = TILES * H + m * TILES + j
                    v.scalar_tensor_tensor(cb[:, m], cb[:, m], decay[:, last:last + 1], cm[:, m], ALU.mult, ALU.add
                                           ).then_inc(a_cb.sem, 1)
                dve.wait_ge(a_cb.sem, a_cb.at(b, 2 * j + 2))
                if j == TILES - 1:
                    v.tensor_scalar(flat(cb[:]), flat(cb[:]), keep[:, 0:1], None, ALU.mult).then_inc(a_cb.sem, 1)
                    v.tensor_scalar(keep[:], keep[:], -1.0, 1.0, ALU.mult, ALU.add).then_inc(a_cb.sem, 1)

            def yT_(b, j):
                dve.wait_ge(a_yh.sem, a_yh.at(b, j + 1))
                v.tensor_tensor(flat(yT_l[:]), A[0][:, 0:D], flat(yT_h[:]).bitcast(F32), ALU.subtract).then_inc(a_yl.sem, 1)

            def wo(b, j):
                dve.wait_ge(a_wo.sem, a_wo.at(b, j + 1))
                v.tensor_tensor(z[:, j], A[0][:, D:2 * D], z[:, j], ALU.add).then_inc(a_x2.sem, 1)

            def aln2(b, k):
                for j in range(TILES):
                    dve.wait_ge(a_x2.sem, a_x2.at(b, j + 1))
                    v.bn_stats(a_st[:, j], z[:, j]).then_inc(a_stats.sem, 1)
                dve.wait_ge(a_stats.sem, a_stats.at(b, 2 * TILES))
                even, odd = a_st[:, :, 1], a_st[:, :, 4]
                v.tensor_tensor(a_mv[:, 0], even, even, ALU.mult).then_inc(a_mean.sem, 1)
                v.tensor_tensor(a_mv[:, 1], odd, odd, ALU.mult).then_inc(a_mean.sem, 1)
                v.tensor_tensor(a_mv[:, 2], a_st[:, :, 2], a_st[:, :, 5], ALU.add).then_inc(a_mean.sem, 1)
                dve.wait_ge(a_mean.sem, a_mean.at(b, 8))
                v.tensor_tensor(a_mv[:, 3], a_mv[:, 0], a_mv[:, 1], ALU.add).then_inc(a_mean.sem, 1)
                dve.wait_ge(a_mean.sem, a_mean.at(b, 9))
                v.tensor_scalar(a_mv[:, 5], a_mv[:, 2], 1.0 / D, 1e-6, ALU.mult, ALU.add).then_inc(a_mean.sem, 1)
                dve.wait_ge(a_mean.sem, a_mean.at(b, 11))
                v.scalar_tensor_tensor(a_sm[:, 3], a_mv[:, 3], 0.5, a_mv[:, 5], ALU.mult, ALU.add).then_inc(a_small.sem, 1)
                dve.wait_ge(a_pow.sem, a_pow.at(b, 3))
                dve.wait_ge(a_tr.sem, a_tr.at(b, DC))
                dve.wait_ge(a_pc.sem, a_pc.at(b, 2 * DC))
                for j in range(TILES):
                    v.tensor_scalar(hn[:, j], z[:, j], a_sm[:, 4, j:j + 1], None, ALU.mult).then_inc(a_h.sem, 1)

            def gu(b, i):
                rows = P if i < IT - 1 else last_rows
                dve.wait_ge(a_th.sem, a_th.at(b, i + 1))
                dve.wait_ge(a_ml.sem, a_ml.at(b, i))
                v.scalar_tensor_tensor(gm[:rows], th[:rows], 1.0, A[2][:rows], ALU.add, ALU.mult).then_inc(a_m1.sem, 1)
                dve.wait_ge(a_m1.sem, a_m1.at(b, i + 1))
                dve.wait_ge(a_gu.sem, a_gu.at(b, 2 * i + 2))
                v.tensor_tensor(gm[:rows], A[3][:rows], gm[:rows], ALU.mult).then_inc(a_m.sem, 1)

            def mfin(b, k):
                dve.wait_ge(a_md.sem, a_md.at(b, IT))
                dve.wait_ge(a_xx.sem, a_xx.at(b, 1))
                dve.wait_ge(s_xout.sem, s_xout.at(b, 0))
                for j in range(TILES):
                    v.tensor_tensor(x_out[:, j], A[j // 2][:, (j % 2) * D:(j % 2 + 1) * D], xc[:, j], ALU.add
                                    ).then_inc(a_x3.sem, 1)

            dve.wait_ge(s_setup.sem, s_setup.at(n_setup, 0))
            dve.wait_ge(s_const.sem, s_const.at(len(consts), 0))
            schedule(dve, {"setup": split_early, "f_ln": ln, "f_tr": tr, "f_gate": gate, "f_lora": lora, "f_act": relu,
                           "f_fin": fin, "a_ln": aln, "a_tr": atr, "a_q": q, "a_kv": kv, "a_kT": kT, "a_fT": fT_,
                           "a_score": score, "a_carry": carry, "a_yT": yT_, "a_wo": wo, "a_ln2": aln2,
                           "a_tr2": lambda b, k: atr(b, k, DC), "a_gu": gu, "a_mfin": mfin})

        @block.tensor
        def _(pe):
            def product(dst, left, right, first=True, last=True, **more):
                (lh, ll), (rh, rl) = left, right
                nc.tensor.matmul(dst, lh, rh, start=first, stop=False, **more)
                nc.tensor.matmul(dst, ll, rh, start=False, stop=False, **more)
                return nc.tensor.matmul(dst, lh, rl, start=False, stop=last, **more)

            def tiles(j, width=D):
                return slice((j % 2) * width, (j % 2 + 1) * width)

            def tr(run, b, first, k):
                pe.wait_ge(f_y.sem, f_y.at(run - 1, TILES))
                for c in range(DC):
                    for j in range(TILES):
                        pe.wait_ge(f_xn.sem, f_xn.at(run, j + 1))
                        done = nc.tensor.transpose(T[c][:, j * P:(j + 1) * P], xn[:, j, c * P:(c + 1) * P], ident[:])
                    done.then_inc(f_tr.sem, 1)

            def gate(run, b, first, k):
                pe.wait_ge(f_x32.sem, f_x32.at(run, DC))
                pe.wait_ge(f_xl.sem, f_xl.at(run, DC))
                for j in range(TILES):
                    for c in range(DC):
                        done = nc.tensor.matmul(T[0][:, j * GW:(j + 1) * GW], xT[:, c, j * P:(j + 1) * P], route_w[:, c],
                                                start=c == 0, stop=c == DC - 1)
                done.then_inc(f_route.sem, 1)

            def up(run, b, first, f):
                if isinstance(run, int) and run == 0 and f == 0:
                    pe.wait_ge(s_early_hi.sem, s_early_hi.at(len(early) + 1, 0))
                    pe.wait_ge(s_early_lo.sem, s_early_lo.at(n_early_lo, 0))
                pe.wait_ge(f_xl.sem, f_xl.at(run, DC))
                pe.wait_ge(f_rl.sem, f_rl.at(run, f - 1))
                cols = slice(f * P, (f + 1) * P)
                for c in range(DC):
                    product(U[f % 2][:], (wi_h[:, c, cols], wi_l[:, c, cols]), (xT_h[:, c], xT_l[:, c]), c == 0, False)

            def lora(run, b, first, k):
                pe.wait_ge(f_u.sem, f_u.at(run, 3))
                pe.wait_ge(f_xl.sem, f_xl.at(run, DC))
                for j in range(TILES):
                    done = nc.tensor.transpose(T[1][0:LS, j * P:(j + 1) * P], flat(u_rep[:, j]), ident[:])
                done.then_inc(f_uT.sem, 1)

            def act_(run, b, first, f):
                pe.wait_ge(f_ul.sem, f_ul.at(run, 1))
                pe.wait_ge(f_uh.sem, f_uh.at(run, 1))
                nc.tensor.matmul(U[f % 2][:], lora_b[0:LS2, f * P:(f + 1) * P], u_st[0:LS2], start=False, stop=True
                                 ).then_inc(f_up.sem, 1)

            def down(run, b, first, f):
                if f == 0:
                    pe.wait_ge(f_u.sem, f_u.at(run, 3))
                    pe.wait_ge(f_ul.sem, f_ul.at(run, 1))
                pe.wait_ge(f_rl.sem, f_rl.at(run, f + 1))
                for j in range(TILES):
                    t = slice(j * P, (j + 1) * P)
                    done = product(T[j // 2][:, tiles(j)], (r_h[:, f % 2, t], r_l[:, f % 2, t]), (wo_h[:, f], wo_l[:, f]),
                                   f == 0 and j % 2 == 0, f == FT - 1, skip_group_check=True)
                done.then_inc(f_dn.sem, 1)

            def atr(b, k, n=0):
                pe.wait_ge(a_h.sem, a_h.at(b, TILES * (2 if n else 1)))
                if n:
                    pe.wait_ge(a_x2.sem, a_x2.at(b, TILES))
                    pe.wait_ge(a_cb.sem, a_cb.at(b, 2 * TILES))
                else:
                    pe.wait_ge(a_x3.sem, a_x3.at(b - 1, TILES))
                for c in range(DC):
                    for j in range(TILES):
                        done = nc.tensor.transpose(A[c][:, j * P:(j + 1) * P], hn[:, j, c * P:(c + 1) * P], ident[:])
                    done.then_inc(a_tr.sem, 1)

            def q(b, m):
                if isinstance(b, int) and b == 0 and m == 0:
                    pe.wait_ge(s_late_lo.sem, s_late_lo.at(len(late), 0))
                pe.wait_ge(a_hl.sem, a_hl.at(b, DC))
                pe.wait_ge(a_m.sem, a_m.at(b - 1, IT))
                cols = slice(m * P, (m + 1) * P)
                for c in range(DC):
                    done = product(A[2 + m][:], (wq_h[:, c, cols], wq_l[:, c, cols]), (hT_h[:, c], hT_l[:, c]),
                                   c == 0, c == DC - 1)
                done.then_inc(a_q.sem, 1)

            def kv(b, j):
                pe.wait_ge(a_g.sem, a_g.at(b, j))
                t = slice(j * P, (j + 1) * P)
                for n, (lo_col, hi_col) in enumerate(((0, KI), (KI, KI + D))):
                    if n:
                        pe.wait_ge(a_v.sem, a_v.at(b, j))
                        pe.wait_ge(a_hl.sem, a_hl.at(b, DC))
                    for c in range(DC):
                        done = product(A[n][:, 0:hi_col - lo_col], (hT_h[:, c, t], hT_l[:, c, t]),
                                       (wkv_h[:, c, lo_col:hi_col], wkv_l[:, c, lo_col:hi_col]), c == 0, c == DC - 1)
                    done.then_inc(a_kv.sem, 1)

            def kT(b, k):
                pe.wait_ge(a_k32.sem, a_k32.at(b, TILES))
                for m in range(DC):
                    pe.wait_ge(a_r1.sem, a_r1.at(b, m + 1))
                    for j in range(TILES):
                        done = nc.tensor.transpose(A[2 + m][:, j * P:(j + 1) * P], k32[:, j, m * P:(m + 1) * P], ident[:])
                    done.then_inc(a_kT.sem, 1)

            def fT_(b, k):
                pe.wait_ge(a_f.sem, a_f.at(b, TILES))
                pe.wait_ge(a_g.sem, a_g.at(b, TILES))
                for j in range(TILES):
                    done = nc.tensor.transpose(A[0][0:H, j * P:(j + 1) * P], fg[:, j], ident[:])
                done.then_inc(a_fT.sem, 1)

            def dec(b, k):
                value = held(pe, a_cum.at(b, TILES))
                pe.wait_ge(s_const.sem, s_const.at(len(consts), 0))
                pe.wait_ge(a_cum.sem, value)
                pe.wait_ge(a_v.sem, a_v.at(b, TILES))
                for j in range(TILES):
                    nc.tensor.transpose(A[1][:, j * H:(j + 1) * H], cumT[:, j], ident[0:H, 0:H])
                for m in range(DC):
                    at = TILES * H + m * TILES
                    done = nc.tensor.matmul(A[1][:, at:at + TILES], headsel[:, m], cumT[:, :, P - 1], start=True, stop=True)
                done.then_inc(a_dT.sem, 1)

            def score(b, u):
                j, g = divmod(u, NQ)
                pe.wait_ge(d_stack.sem, d_stack.at(b, 2 * SLOTS * (j // 2 + 1)))
                if u < 2:
                    pe.wait_ge(a_r1.sem, a_r1.at(b, 2 * DC))
                else:
                    pe.wait_ge(a_P.sem, a_P.at(b, u - 1))
                t = slice((j % 2) * P, (j % 2 + 1) * P)
                for n in range(QUAD):
                    h = QUAD * g + n
                    done = nc.tensor.matmul(A[2 + u % 2][:, n * P:(n + 1) * P], ks[:, h, t], qs[:, h, t], start=True, stop=True)
                done.then_inc(a_S.sem, 1)

            def mix(b, u):
                j, g = divmod(u, NQ)
                pe.wait_ge(a_P.sem, a_P.at(b, u + 1))
                if u == 0:
                    pe.wait_ge(a_fTs.sem, a_fTs.at(b, 2))
                elif g == 0:
                    pe.wait_ge(a_x2.sem, a_x2.at(b, j))
                for n in range(QUAD):
                    h = QUAD * g + n
                    done = nc.tensor.matmul(A[0][:, h * HV:(h + 1) * HV], pt[:, u % 2, n * P:(n + 1) * P], vp[:, j, h],
                                            start=True, stop=True)
                done.then_inc(a_O.sem, 1)

            def carry(b, j):
                if j == 0:
                    pe.wait_ge(a_dec.sem, a_dec.at(b, 1))
                pe.wait_ge(a_cb.sem, a_cb.at(b, 2 * j))
                t = slice(j * P, (j + 1) * P)
                for m in range(DC):
                    done = nc.tensor.matmul(A[1][:, m * HH * HV:(m + 1) * HH * HV], q32[:, m, t], cb[:, m], start=True, stop=True)
                done.then_inc(a_oi.sem, 1)
                pe.wait_ge(a_t1.sem, a_t1.at(b, j + 1))
                pe.wait_ge(a_wv.sem, a_wv.at(b, NQ * (j + 1)))
                for m in range(DC):
                    done = nc.tensor.matmul(A[1][:, m * HH * HV:(m + 1) * HH * HV], k32[:, j, m * P:(m + 1) * P],
                                            flat(wv[:, m * HH:(m + 1) * HH]), start=True, stop=True)
                done.then_inc(a_state.sem, 1)

            def yT_(b, j):
                pe.wait_ge(a_y.sem, a_y.at(b, j + 1))
                pe.wait_ge(a_o.sem, a_o.at(b, j + 1))
                for c in range(DC):
                    done = nc.tensor.transpose(A[0][:, c * P:(c + 1) * P], y[:, j % 2, c * P:(c + 1) * P], ident[:])
                done.then_inc(a_yT.sem, 1)

            def wo(b, j):
                pe.wait_ge(a_yl.sem, a_yl.at(b, j + 1))
                for c in range(DC):
                    done = product(A[0][:, D:2 * D], (yT_h[:, c], yT_l[:, c]), (wao_h[:, c], wao_l[:, c]), c == 0, c == DC - 1)
                done.then_inc(a_wo.sem, 1)

            def gu(b, i):
                rows = P if i < IT - 1 else last_rows
                pe.wait_ge(a_hl.sem, a_hl.at(b, 2 * DC))
                if i:
                    pe.wait_ge(a_m.sem, a_m.at(b, i))
                else:
                    pe.wait_ge(a_P.sem, a_P.at(b, TILES * NQ))
                for n in range(2):
                    cols = slice(n * I + i * P, n * I + i * P + rows)
                    for c in range(DC):
                        done = product(A[2 + n][:rows], (wgu_h[:, c, cols], wgu_l[:, c, cols]), (hT_h[:, c], hT_l[:, c]),
                                       c == 0, c == DC - 1)
                    done.then_inc(a_gu.sem, 1)

            def mdown(b, i):
                rows = P if i < IT - 1 else last_rows
                pe.wait_ge(a_ml.sem, a_ml.at(b, i + 1))
                for j in range(TILES):
                    t = slice(j * P, (j + 1) * P)
                    done = product(A[j // 2][:, tiles(j)], (m_h[:rows, i % 2, t], m_l[:rows, i % 2, t]),
                                   (wd_h[:rows, i], wd_l[:rows, i]), i == 0 and j % 2 == 0, i == IT - 1, skip_group_check=True)
                done.then_inc(a_md.sem, 1)

            pe.wait_ge(s_const.sem, s_const.at(len(consts), 0))
            pe.wait_ge(s_setup.sem, s_setup.at(n_setup, 0))
            schedule(pe, {"f_tr": tr, "f_gate": gate, "f_up": up, "f_lora": lora, "f_act": act_, "f_down": down,
                          "a_tr": atr, "a_q": q, "a_kv": kv, "a_kT": kT, "a_fT": fT_, "a_decay": dec, "a_score": score,
                          "a_mix": mix, "a_carry": carry, "a_yT": yT_, "a_wo": wo, "a_tr2": lambda b, k: atr(b, k, DC),
                          "a_gu": gu, "a_mdown": mdown})


def kernel(**inputs):
    from concourse import bacc
    from concourse.bass_utils import run_bass_kernel_spmd

    g = {name: np.asarray(v) for name, v in inputs.items()}
    att = lambda name: g["L0_attn_" + name]
    ffn = lambda name: g["L0_ffn_" + name]
    cat = np.concatenate
    lora = ffn("lora_B").transpose(0, 2, 1).reshape(ER, F)
    bias = ffn("wi_b")[None]
    head = np.arange(P) // HD
    arrays = {
        "x": att("x").reshape(BLOCKS, TILES, P, D),
        "wi": ffn("wi_W").T, "wo": ffn("wo_W").T,
        "lora": cat([lora, lora, lora, bias, bias]),
        "wq": att("wq"), "wkv": cat([att("wk"), att("wi"), att("wf"), att("wv")], axis=1), "wao": att("wo"),
        "wgu": cat([att("w_gate"), att("w_up")], axis=1), "wd": att("w_down"),
        "route_w": cat([ffn("gate_W"), ffn("lora_A").reshape(ER, D)]).T,
        "route_b": ffn("gate_b"), "wo_b": ffn("wo_b"), "gate_bias": cat([att("bi"), att("bf")]),
        "ln1": att("ln1_w").reshape(DC, P).T, "ln2": att("ln2_w").reshape(DC, P).T,
        "ident": np.eye(P, dtype=np.float32), "ident4": np.tile(np.eye(P, dtype=np.float32), (1, QUAD)),
        "headmask": np.tile(np.repeat(head[:, None] == np.arange(HH), HV, axis=1), (1, DC)).astype(np.float32),
        "headsel": np.stack([np.arange(H)[:, None] == head + m * HH for m in range(DC)], axis=1).astype(np.float32),
        "prio": np.broadcast_to(np.arange(E, 0, -1, dtype=np.float32), (P, TILES, E)),
    }
    arrays = {k: np.ascontiguousarray(v) for k, v in arrays.items()}
    nc = bacc.Bacc("TRN2", target_bir_lowering=False, num_devices=1, dynamic_dma_scratch_size=1024)
    a = {k: nc.dram_tensor("in_" + k, v.shape, mybir.dt.from_np(v.dtype), kind="ExternalInput").ap() for k, v in arrays.items()}
    out = nc.dram_tensor("out", (BLOCKS, TILES, P, D), F32, kind="ExternalOutput").ap()
    build(nc, a, out)
    r = run_bass_kernel_spmd(nc, [{"in_" + k: v for k, v in arrays.items()}], core_ids=[0])
    return r.results[0]["out"].reshape(N_SEQ, SEQ, D)
```

```python
import numpy as np

import concourse.bass as bass
import concourse.mybir as mybir
from concourse.alu_op_type import AluOpType as ALU

P = 128
N_SEQ, SEQ, D = 4, 1024, 256
TILES = 4
BLOCK = TILES * P
BLOCKS = N_SEQ * SEQ // BLOCK
DC = D // P
F = 1024
FT = F // P
E, R = 8, 4
ER = E * R
GW = E + ER
H, HD = 16, 16
HV = HD + 1
HH = P // HD
I = 704
IT = -(-I // P)
KI = D + 2 * H
QUAD = 4
NQ = H // QUAD
SLOTS = 6
STACK = SLOTS * HD
LS = 3 * ER
LS2 = LS + 2

F32, F32R, BF16 = mybir.dt.float32, mybir.dt.float32r, mybir.dt.bfloat16
ACT = mybir.ActivationFunctionType
AX_X = mybir.AxisListType.X


class Signal:

    def __init__(self, sem, per, step=1):
        self.sem, self.per, self.step = sem, per, step

    def at(self, run, count):
        value = (run * self.per + count) * self.step
        return max(value, 0) if isinstance(value, int) else value


def iteration(ffn2, att, ffn1, ffn2_next):
    present = {"2": ffn2, "a": att, "1": ffn1, "n": ffn2_next, "m": ffn1}
    order = """
        1 load; 2 normal; a kv 0; a kv 1; 2 tr; a kv 2; 2 up 0; a kv 3; 2 up 1 & 2 gate; a kT; a fT; 2 lora; a decay;
        2 act 0; 2 act 1; 2 up 2; 2 down 0; 2 act 2; a copy; 2 up 3; 2 down 1; 2 act 3; a stack 0; 2 down 2; 1 stats; a scan 0; a scan 1;
        2 up 4; 2 act 4; 1 normal; a score 0; a score 1; a scan 2; a scan 3; a carry 0;
        a mix 0 & 2 down 3; a score 2; a mix 1 & 2 up 5; 2 act 5; a score 3; a stack 2; a mix 2 & 2 down 4; a scan 4;
        a mix 3 & 2 up 6; a sum 0; a state 0; 2 act 6; a score 4; a scan 5; 2 down 5; a score 5; a yT 0; 2 up 7; 2 act 7; a wo 0;
        a carry 1; a scan 6;
        a mix 4 & 2 down 6; a score 6; a scan 7; a mix 5 & 2 down 7; 2 fin; a score 7; a stack 3; a mix 6; a scan 8; a mix 7;
        a sum 1; a state 1; a score 8; 1 tr; a yT 1; a scan 9; a score 9; 1 up 0; a wo 1; a carry 2; 1 up 1; a scan 10;
        a mix 8 & 1 gate; a score 10; a scan 11; a mix 9; a score 11; a mix 10; a scan 12; 1 lora;
        a mix 11; a sum 2; a state 2; 1 act 0; 1 act 1; a score 12; 1 up 2; a yT 2; a scan 13; a score 13; 1 down 0; 1 act 2; a wo 2;
        a carry 3; a scan 14; 1 up 3; a mix 12 & 1 down 1; a score 14; 1 act 3; a scan 15; a mix 13 & 1 up 4; a score 15;
        a mix 14 & 1 down 2; 1 act 4; a mix 15 & 1 up 5; a sum 3; a state 3; 1 down 3; 1 act 5; a yT 3; 1 up 6; a wo 3; 1 down 4;
        a ln2; 1 act 6; 1 up 7; 1 down 5; a tr2; 1 act 7; 1 down 6; 1 down 7; 1 fin;
        a gu 0; a gu 1; m stats; a mdown 0; a gu 2; m z; a mdown 1; a gu 3; m normal; a mdown 2; a gu 4; a mdown 3; a gu 5; m tr;
        a mdown 4; m q 0; a mdown 5; m q 1; a mfin; n stats"""
    for group in order.split(";"):
        steps = [step.split() for step in group.split("&")]
        steps = [(stage, name, int(k[0]) if k else 0) for stage, name, *k in steps if present[stage]]
        if steps:
            yield steps


def build(nc, a, out):
    from contextlib import ExitStack

    ctx = ExitStack()
    with ctx:
        def sb(name, shape, dt=F32):
            return ctx.enter_context(nc.sbuf_tensor(name, shape, dt))

        def sig(name, per=1, step=1):
            return Signal(ctx.enter_context(nc.semaphore(name)), per, step)

        ident = sb("ident", [P, P])
        ident4 = sb("ident4", [P, QUAD * P])
        headmask = sb("headmask", [P, DC * HH * HV])
        headsel = sb("headsel", [H, DC, P])
        prio = sb("prio", [P, TILES, E])
        zeros = sb("zeros", [H, P])
        minus_half = sb("minus_half", [P, TILES])
        def pair(name, shape):
            return sb(name + "_hi", shape, F32R), sb(name + "_lo", shape, F32R)

        wi_h, wi_l = pair("wi", [P, DC, F])
        wo_h, wo_l = pair("wo", [P, FT, D])
        wq_h, wq_l = pair("wq", [P, DC, D])
        wkv_h, wkv_l = pair("wkv", [P, DC, KI + D])
        wao_h, wao_l = pair("wao", [P, DC, D])
        wgu_h, wgu_l = pair("wgu", [P, DC, 2 * I])
        wd_h, wd_l = pair("wd", [P, IT, D])
        lora_b = sb("lora_b", [P, F], F32R)
        route_w = sb("route_w", [P, DC, GW])
        route_b = sb("route_b", [P, E])
        half_wo_b = sb("half_wo_b", [P, D])
        gate_bias = sb("gate_bias", [P, 2 * H])
        ln1 = sb("ln1", [P, DC])
        ln2 = sb("ln2", [P, DC])
        x_in = sb("x_in", [P, TILES, D])
        x_mid = sb("x_mid", [P, TILES, D])
        x_out = sb("x_out", [P, TILES, D])
        f_st = sb("f_st", [P, TILES, 6])
        f_mv = sb("f_mv", [P, 6, TILES])
        f_ve = sb("f_ve", [P, TILES])
        f_rs = sb("f_rs", [P, TILES])
        xn = sb("xn", [P, TILES, D])
        xT = sb("xT", [P, DC, BLOCK])
        xT_h, xT_l = pair("xT", [P, DC, BLOCK])
        lg = sb("lg", [P, TILES, E])
        lmax = sb("lmax", [P, TILES])
        won = sb("won", [P, TILES, E])
        won2 = sb("won2", [P, TILES, E])
        wmax = sb("wmax", [P, TILES])
        onehot = sb("onehot", [P, TILES, E])
        u_rep = sb("u_rep", [P, TILES, 3, ER])
        u_st = sb("u_st", [P, BLOCK], F32R)
        narrow = sb("narrow", [P, BLOCK])
        fT = narrow[0:H].rearrange("h (j t) -> h j t", j=TILES)
        fTz = narrow[32:32 + H].rearrange("h (j t) -> h j t", j=TILES)
        u_hi = narrow[2 * ER:LS]
        r_h = sb("r_h", [P, 2, BLOCK], F32R)
        r_l = sb("r_l", [P, 2, BLOCK], F32R)
        a_st = sb("a_st", [P, TILES, 6])
        a_mv = sb("a_mv", [P, 6, TILES])
        a_sm = sb("a_sm", [P, 6, TILES])
        z = sb("z", [P, TILES, D])
        xc = sb("xc", [P, TILES, D])
        hn = sb("hn", [P, TILES, D])
        hT_h, hT_l = pair("hT", [P, DC, BLOCK])
        q32 = sb("q32", [P, DC, BLOCK])
        pa = sb("pa", [P, DC, BLOCK], BF16)
        pb = sb("pb", [P, DC, BLOCK], BF16)
        pc = sb("pc", [P, DC, BLOCK], BF16)
        r1 = hn[:].rearrange("p (c k) d -> p c (k d)", c=DC)
        k32 = sb("k32", [P, TILES, D])
        vp = sb("vp", [P, TILES, H, HV])
        g32 = sb("g32", [P, TILES, 2 * H])
        fg = sb("fg", [P, TILES, H])
        cumT = sb("cumT", [H, TILES, P])
        decay = sb("decay", [P, TILES * H + DC * TILES])
        dm = sb("dm", [P, NQ, QUAD * P])
        arena = sb("arena", [P, 2, H * BLOCK // 4])
        qs, ks = (arena[0:STACK, n].bitcast(BF16).rearrange("k (h t) -> k h t", h=H) for n in range(2))
        pt = sb("pt", [P, 2, QUAD * P])
        wv = sb("wv", [P, H, HV])
        cb = sb("cb", [P, DC, HH * HV])
        cm = sb("cm", [P, DC, HH * HV])
        keep = sb("keep", [P, 1])
        o1 = sb("o1", [P, H, HV])
        den = sb("den", [P, 3, H])
        y = sb("y", [P, 2, D])
        yT_h, yT_l = pair("yT", [P, DC, P])
        th, gm = pt[:, 0], pt[:, 1]
        m_h = sb("m_h", [P, 2, BLOCK], F32R)
        m_l = sb("m_l", [P, 2, BLOCK], F32R)

        wo_b = y[:, 0]
        psum = [ctx.enter_context(nc.psum_tensor(f"bank{n}", [P, 512], F32)) for n in range(8)]
        T, U, A = psum[0:2], psum[2:4], psum[4:8]

        parts_d = nc.dram_tensor("parts_scratch", (2, 3, H, HD, BLOCK), BF16).ap()
        f_d = nc.dram_tensor("f_scratch", (TILES, NQ, QUAD * P), F32).ap()

        s_const = sig("const_loaded", 1, 16)
        s_early = [sig(f"early_loaded{n}", 1, 16) for n in range(5)]
        s_early_hi, s_early_lo = sig("early_hi"), sig("early_lo")
        s_late = [sig(f"late_loaded{n}", 1, 16) for n in range(2)]
        s_late_hi, s_late_lo = sig("late_hi"), sig("late_lo")
        s_setup = sig("setup_done")
        n_setup = 7
        s_xin = sig("x_loaded", 1, 16)
        s_xout = sig("x_stored", 1, 16)
        f_stats, f_mean, f_var = sig("f_stats", TILES), sig("f_mean", 6), sig("f_var")
        f_rstd, f_xn, f_xb = sig("f_rstd"), sig("f_xn", TILES), sig("f_xb")
        f_tr, f_x32, f_xh, f_xl = sig("f_tr", DC), sig("f_x32", DC), sig("f_xh", DC), sig("f_xl", DC)
        f_route, f_sel, f_u = sig("f_route"), sig("f_sel", 6), sig("f_u", 3)
        f_uT, f_uh, f_ul = sig("f_uT"), sig("f_uh", 2), sig("f_ul")
        f_up, f_rh, f_rl, f_dn, f_y = sig("f_up", FT), sig("f_rh", FT), sig("f_rl", FT), sig("f_dn", FT), sig("f_y", TILES)
        a_stats, a_mean, a_small = sig("a_stats", 2 * TILES), sig("a_mean", 11), sig("a_small", 7)
        a_pow = sig("a_pow", 3)
        a_z, a_h, a_xc, a_xx = sig("a_z", TILES), sig("a_h", 2 * TILES), sig("a_xc"), sig("a_xx")
        a_tr, a_hh, a_hl = sig("a_tr", 2 * DC), sig("a_hh", 2 * DC), sig("a_hl", 2 * DC)
        a_q, a_q32 = sig("a_q", DC), sig("a_q32", DC)
        a_pa, a_r1, a_pb, a_pc = sig("a_pa", 2 * DC), sig("a_r1", 2 * DC), sig("a_pb", 2 * DC), sig("a_pc", 2 * DC)
        a_kv, a_k32, a_g, a_clip = sig("a_kv", 2 * TILES), sig("a_k32", TILES), sig("a_g", TILES), sig("a_clip", TILES)
        a_i, a_tf, a_v, a_f = sig("a_i", TILES), sig("a_tf", TILES), sig("a_v", TILES), sig("a_f", TILES)
        a_kT, a_fT, a_fTs, a_cum = sig("a_kT", DC), sig("a_fT"), sig("a_fTs", 2), sig("a_cum", TILES)
        a_dT, a_dec = sig("a_dT"), sig("a_dec")
        d_parts = sig("d_parts", 2 * 3 * DC, 16)
        d_f = sig("d_f", NQ, 16)
        d_stack = sig("d_stack", 3 * 2 * SLOTS, 16)
        d_fb = [sig(f"d_fb{n}", TILES, 16) for n in range(NQ)]
        a_D, a_S, a_P, a_wv, a_O = (sig(n, TILES * NQ) for n in ("a_D", "a_S", "a_P", "a_wv", "a_O"))
        a_oi, a_t1, a_o, a_den, a_y = sig("a_oi", TILES), sig("a_t1", TILES), sig("a_o", TILES), sig("a_den", 3 * TILES), sig("a_y", TILES)
        a_state, a_cm, a_cb = sig("a_state", TILES), sig("a_cm", TILES), sig("a_cb", 2 * TILES + 2)
        a_yT, a_yh, a_yl, a_wo, a_x2 = (sig(n, TILES) for n in ("a_yT", "a_yh", "a_yl", "a_wo", "a_x2"))
        a_gu, a_th, a_m1, a_m, a_mh, a_ml, a_md = sig("a_gu", 2 * IT), sig("a_th", IT), sig("a_m1", IT), sig("a_m", IT), sig("a_mh", IT), sig("a_ml", IT), sig("a_md", IT)
        a_x3 = sig("a_x3", TILES)


        woT = a["wo"].rearrange("(c p) n -> p c n", p=P)
        half_ft = FT // 2
        early = [(z, a["wi"][0:P], wi_h[:, 0], wi_l[:, 0]), (xc, a["wi"][P:D], wi_h[:, 1], wi_l[:, 1]),
                 (x_mid, a["lora"], lora_b[0:LS2], None),
                 (hn, woT[:, 0:half_ft], wo_h[:, 0:half_ft], wo_l[:, 0:half_ft]),
                 (q32, woT[:, half_ft:FT], wo_h[:, half_ft:FT], wo_l[:, half_ft:FT])]
        n_early_lo = len(early) + 1

        wgu_in = [(a["wgu"][c * P:(c + 1) * P].unsqueeze(1), wgu_h[:, c:c + 1], wgu_l[:, c:c + 1], ln2[:, c:c + 1], 1.0)
                  for c in range(DC)]
        rows_of = lambda name: a[name].rearrange("(c p) n -> p c n", p=P)
        last_rows = I - (IT - 1) * P
        late = [(rows_of("wq"), wq_h, wq_l, ln1, 1.0), (rows_of("wkv"), wkv_h, wkv_l, ln1, 1.0),
                (rows_of("wao"), wao_h, wao_l, None, 1.0), *wgu_in,
                (a["wd"][0:(IT - 1) * P].rearrange("(c p) n -> p c n", p=P), wd_h[:, 0:IT - 1], wd_l[:, 0:IT - 1], None, 0.5),
                (a["wd"][(IT - 1) * P:I].unsqueeze(1), wd_h[0:last_rows, IT - 1:IT], wd_l[0:last_rows, IT - 1:IT], None, 0.5)]

        def late_count(n):
            return sum(hi.shape[1] for _, hi, *_ in late[:n])

        def late_stage(n):
            hi = late[n][1]
            rows, c, cols = hi.shape
            return arena[0:rows, n % 2, 0:c * cols].rearrange("p (c n) -> p c n", c=c)

        consts = [(ident[:], a["ident"]), (ident4[:], a["ident4"]), (headmask[:], a["headmask"]),
                  (headsel[:], a["headsel"]), (prio[:], a["prio"]),
                  (route_w[:], a["route_w"].rearrange("(c p) n -> p c n", p=P)),
                  (route_b[:], a["route_b"].partition_broadcast(P)),
                  (wo_b, a["wo_b"].partition_broadcast(P)),
                  (gate_bias[:], a["gate_bias"].partition_broadcast(P)),
                  (ln1[:], a["ln1"]), (ln2[:], a["ln2"])]

        def flat(ap):
            return ap.rearrange("p a b -> p (a b)") if len(ap.shape) == 3 else ap

        def held(engine, value):
            return value if isinstance(value, int) else engine.snap(value)

        def ffn1_run(b):
            return 0 if isinstance(b, int) and b == 0 else b * 2 - 1

        def schedule(engine, steps):
            def play(t, run2, att, run1, run_next):
                runs = {"1": (run1, t, True), "2": (run2, t - 2, False), "n": (run_next, t - 1, False), "a": (att,), "m": (t,)}
                for group in iteration(run2 is not None, att is not None, run1 is not None, run_next is not None):
                    named = [(steps.get(("a_" if stage in "am" else "f_") + name), stage, k) for stage, name, k in group]
                    running = [step(*runs[stage], k) for step, stage, k in named if step]
                    while running:
                        running = [step for step in running if step is not None and next(step, ended) is not ended]
                    if t is first and group[0][:2] == ("1", "normal") and "setup" in steps:
                        steps["setup"]()
                    if t is first and group[0][:2] == ("1", "act") and group[0][2] < len(late) and "late" in steps:
                        steps["late"](group[0][2])

            ended = object()
            first = 0
            play(first, None, None, 0, None)
            first = None
            play(1, None, 0, 1, 2)
            with engine.Fori(2, BLOCKS) as t:
                play(t, t * 2 - 2, t - 1, t * 2 - 1, t * 2)
            play(BLOCKS, 2 * BLOCKS - 2, BLOCKS - 1, None, 2 * BLOCKS - 1)
            play(BLOCKS + 1, 2 * BLOCKS - 1, None, None, None)

        block = ctx.enter_context(nc.Block())

        @block.sync
        def _(sp):
            def load_x(b):
                sp.dma_start(x_in[:], a["x"][bass.ds(b, 1)].rearrange("a j p d -> p (a j) d")).then_inc(s_xin.sem, 16)

            sp.dma_start(x_in[:], a["x"][0].rearrange("j p d -> p j d")).then_inc(s_xin.sem, 16)
            for n, (stage, src, hi, lo) in enumerate(early):
                dst = stage[0:hi.shape[0]]
                if len(src.shape) == 2:
                    dst = flat(dst)
                sp.dma_start(dst, src).then_inc(s_early[n].sem, 16)
                if n == 0:
                    for to, of in consts:
                        sp.dma_start(to, of).then_inc(s_const.sem, 16)
            for n, (src, hi, lo, _, _) in enumerate(late):
                sp.wait_ge(s_late_lo.sem, s_late_lo.at(0, late_count(n - 1) if n > 1 else 0))
                sp.dma_start(late_stage(n), src).then_inc(s_late[n % 2].sem, 16)

            def load(run, b, first, k):
                if isinstance(b, int) and b == 0:
                    return
                value = held(sp, f_y.at(ffn1_run(b - 1), TILES))
                sp.wait_ge(s_const.sem, s_const.at(len(consts), 0))
                sp.wait_ge(f_y.sem, value)
                load_x(b)

            def fin(run, b, first, k):
                if not first:
                    value = held(sp, f_y.at(run, TILES))
                    sp.wait_ge(s_const.sem, s_const.at(len(consts), 0))
                    sp.wait_ge(f_y.sem, value)
                    sp.dma_start(out[bass.ds(b, 1)].rearrange("a j p d -> p (a j) d"), x_out[:]).then_inc(s_xout.sem, 16)

            def store_parts(b, u):
                for n, (sem, part) in enumerate(((a_pa, pa), (a_pb, pb), (a_pc, pc))):
                    sp.wait_ge(sem.sem, sem.at(b, DC * (u + 1)))
                    for m in range(DC):
                        sp.dma_start(parts_d[u, n, m * HH:(m + 1) * HH].rearrange("h e t -> (h e) t"), part[:, m]
                                     ).then_inc(d_parts.sem, 16)

            def q(b, m):
                if m == DC - 1:
                    sp.wait_ge(d_stack.sem, d_stack.at(b - 1, 3 * 2 * SLOTS))
                    store_parts(b, 0)

            def load_stack(b, j):
                value = held(sp, d_parts.at(b, 2 * 3 * DC))
                sp.wait_ge(s_const.sem, s_const.at(len(consts), 0))
                sp.wait_ge(d_parts.sem, value)
                if j:
                    sp.wait_ge(a_S.sem, a_S.at(b, (j - 1) * NQ))
                else:
                    sp.wait_ge(a_S.sem, a_S.at(b - 1, TILES * NQ))
                tokens = slice(j * P, (j + 1 if j else 2) * P)
                to = slice(j % 2 * P, (j % 2 + 1 if j else 2) * P)
                for u, (dst, order) in enumerate(((qs, (0, 0, 1, 1, 0, 2)), (ks, (0, 1, 0, 1, 2, 0)))):
                    for slot, n in enumerate(order):
                        sp.dma_start(dst[slot * HD:(slot + 1) * HD, :, to],
                                     parts_d[u, n, :, :, tokens].rearrange("h e t -> e h t")).then_inc(d_stack.sem, 16)

            def load_f(b, u):
                j, g = divmod(u, NQ)
                value = held(sp, d_f.at(b, NQ))
                sp.wait_ge(s_const.sem, s_const.at(len(consts), 0))
                sp.wait_ge(d_f.sem, value)
                sp.wait_ge(a_P.sem, a_P.at(b, u - NQ + 1))
                sp.wait_ge(a_wv.sem, a_wv.at(b, u - NQ + 1))
                sp.dma_start(dm[:, g], f_d[j, g].partition_broadcast(P)).then_inc(d_fb[g].sem, 16)

            def fT_(b, k):
                store_parts(b, 1)
                sp.wait_ge(a_fTs.sem, a_fTs.at(b, 1))
                for g in range(NQ):
                    sp.wait_ge(d_fb[g].sem, d_fb[g].at(b - 1, TILES))
                for g in range(NQ):
                    sp.dma_start(f_d[:, g].rearrange("j (h t) -> h j t", h=QUAD), fTz[QUAD * g:QUAD * (g + 1)]).then_inc(d_f.sem, 16)
                for u in range(NQ):
                    load_f(b, u)

            def mix(b, u):
                if u + NQ < TILES * NQ:
                    load_f(b, u + NQ)

            schedule(sp, {"f_load": load, "f_fin": fin, "a_q": q, "a_fT": fT_, "a_stack": load_stack, "a_mix": mix})
            sp.wait_ge(s_xout.sem, s_xout.at(BLOCKS, 0))

        @block.gpsimd
        def _(pool):
            nc.gpsimd.memset(minus_half[:], -0.5).then_inc(s_setup.sem, 1)

            def stats(run, b, first, k):
                if isinstance(run, int) and run == 0:
                    pool.wait_ge(s_setup.sem, s_setup.at(n_setup, 0))
                pool.wait_ge(f_var.sem, f_var.at(run, 1))
                nc.gpsimd.tensor_tensor(f_rs[:], f_ve[:], minus_half[:], ALU.pow).then_inc(f_rstd.sem, 1)

            def normal(run, b, first, k):
                pool.wait_ge(f_xn.sem, f_xn.at(run, TILES))
                x = x_in if first else x_out
                bias = half_wo_b[:].unsqueeze(1).to_broadcast([P, TILES, D])
                nc.gpsimd.tensor_tensor(x[:], x[:], bias, ALU.add).then_inc(f_xb.sem, 1)

            def tr(run, b, first, k):
                pool.wait_ge(f_route.sem, f_route.at(run - 1, 1))
                for c in range(DC):
                    pool.wait_ge(f_xh.sem, f_xh.at(run, c + 1))
                    pool.wait_ge(f_xl.sem, f_xl.at(run, c + 1))
                    nc.gpsimd.tensor_tensor(xT[:, c], xT_h[:, c].bitcast(F32), xT_l[:, c].bitcast(F32), ALU.add
                                            ).then_inc(f_x32.sem, 1)

            def astats(b, k):
                pool.wait_ge(a_small.sem, a_small.at(b, 1))
                nc.gpsimd.tensor_tensor(a_sm[:, 1], a_sm[:, 0], minus_half[:], ALU.pow).then_inc(a_pow.sem, 1)

            def az(b, k):
                pool.wait_ge(a_small.sem, a_small.at(b, 6))
                nc.gpsimd.tensor_tensor(a_sm[:, 2], a_sm[:, 0], minus_half[:], ALU.pow).then_inc(a_pow.sem, 1)

            def split(b, u):
                for m in range(DC):
                    n = DC * u + m
                    pool.wait_ge(a_pb.sem, a_pb.at(b, n + 1))
                    nc.gpsimd.tensor_tensor(pc[:, m], r1[:, m], pb[:, m], ALU.subtract).then_inc(a_pc.sem, 1)

            def mix(b, u):
                j, g = divmod(u, NQ)
                pool.wait_ge(a_D.sem, a_D.at(b, u + 1))
                if j:
                    pool.wait_ge(a_state.sem, a_state.at(b, j))
                else:
                    pool.wait_ge(a_state.sem, a_state.at(b - 1, TILES))
                w = dm[:, g].rearrange("p (h t) -> p h t", h=QUAD)[:, :, P - 1:P].to_broadcast([P, QUAD, HV])
                heads = slice(QUAD * g, QUAD * (g + 1))
                pool.wait_ge(a_v.sem, a_v.at(b, j + 1))
                nc.gpsimd.tensor_tensor(wv[:, heads], vp[:, j, heads], w, ALU.mult).then_inc(a_wv.sem, 1)

            def aln2(b, k):
                pool.wait_ge(a_x2.sem, a_x2.at(b, TILES))
                pool.wait_ge(a_small.sem, a_small.at(b, 7))
                nc.gpsimd.tensor_tensor(a_sm[:, 4], a_sm[:, 3], minus_half[:], ALU.pow).then_inc(a_pow.sem, 1)
                pool.wait_ge(a_xc.sem, a_xc.at(b, 1))
                nc.gpsimd.tensor_tensor(xc[:], xc[:], z[:], ALU.add).then_inc(a_xx.sem, 1)

            def gu(b, i):
                rows = P if i < IT - 1 else last_rows
                pool.wait_ge(a_mh.sem, a_mh.at(b, i + 1))
                if i > 1:
                    pool.wait_ge(a_md.sem, a_md.at(b, i - 1))
                nc.gpsimd.tensor_tensor(m_l[:rows, i % 2], gm[:rows], m_h[:rows, i % 2].bitcast(F32), ALU.subtract
                                        ).then_inc(a_ml.sem, 1)

            schedule(pool, {"f_stats": stats, "f_normal": normal, "f_tr": tr, "a_stats": astats, "a_z": az, "a_q": lambda b, m: split(b, 0) if m else None,
                            "a_kT": lambda b, k: split(b, 1), "a_mix": mix, "a_ln2": aln2, "a_gu": gu})

        @block.scalar
        def _(act):
            act.wait_ge(s_const.sem, s_const.at(len(consts), 0))
            nc.scalar.mul(half_wo_b[:], wo_b, 0.5).then_inc(s_setup.sem, 1)
            for n, (stage, src, hi, lo) in enumerate(early):
                act.wait_ge(s_early[n].sem, s_early[n].at(1, 0))
                nc.scalar.copy(flat(hi), flat(stage[0:hi.shape[0]])).then_inc(s_early_hi.sem, 1)
                if lo is None:
                    act.wait_ge(s_early_lo.sem, s_early_lo.at(n + 1, 0))
                    nc.scalar.copy(hi[LS:LS + 1], flat(stage[LS:LS + 1])).then_inc(s_early_hi.sem, 1)

            def late_hi(n):
                src, hi, lo, factors, const = late[n]
                act.wait_ge(s_early_lo.sem, s_early_lo.at(n_early_lo, 0))
                act.wait_ge(s_late[n % 2].sem, s_late[n % 2].at(n // 2 + 1, 0))
                for c in range(hi.shape[1]):
                    nc.scalar.activation(hi[:, c], late_stage(n)[:, c], ACT.Copy, scale=const if factors is None else factors[:, c:c + 1]
                                         ).then_inc(s_late_hi.sem, 1)

            def tr(run, b, first, k):
                for c in range(DC):
                    act.wait_ge(f_tr.sem, f_tr.at(run, c + 1))
                    act.wait_ge(f_up.sem, f_up.at(run - 1, FT))
                    nc.scalar.copy(xT_h[:, c], T[c][:]).then_inc(f_xh.sem, 1)

            def lora(run, b, first, k):
                act.wait_ge(f_uT.sem, f_uT.at(run, 1))
                nc.scalar.copy(u_st[0:2 * ER], T[1][0:2 * ER]).then_inc(f_uh.sem, 1)
                act.wait_ge(f_ul.sem, f_ul.at(run - 1, 1))
                nc.scalar.copy(u_hi.bitcast(F32R), T[1][2 * ER:LS]).then_inc(f_uh.sem, 1)

            def relu(run, b, first, f):
                act.wait_ge(f_up.sem, f_up.at(run, f + 1))
                act.wait_ge(f_dn.sem, f_dn.at(run, f - 1))
                nc.scalar.activation(r_h[:, f % 2], U[f % 2][:], ACT.Relu).then_inc(f_rh.sem, 1)

            def atr(b, k):
                for c in range(DC):
                    act.wait_ge(a_tr.sem, a_tr.at(b, c + 1))
                    act.wait_ge(a_gu.sem, a_gu.at(b - 1, 2 * IT))
                    nc.scalar.copy(hT_h[:, c], U[c][:]).then_inc(a_hh.sem, 1)

            def acopy(b, k):
                act.wait_ge(a_x3.sem, a_x3.at(b - 1, TILES))
                act.wait_ge(f_y.sem, f_y.at(ffn1_run(b), TILES))
                nc.scalar.copy(xc[:], x_mid[:]).then_inc(a_xc.sem, 1)

            def atr2(b, k):
                for c in range(DC):
                    act.wait_ge(a_tr.sem, a_tr.at(b, DC + c + 1))
                    act.wait_ge(a_kv.sem, a_kv.at(b, 2 * TILES))
                    nc.scalar.copy(hT_h[:, c], A[c][:]).then_inc(a_hh.sem, 1)

            def q(b, m):
                act.wait_ge(a_q.sem, a_q.at(b, m + 1))
                act.wait_ge(a_oi.sem, a_oi.at(b - 1, TILES))
                nc.scalar.copy(q32[:, m], A[2 + m][:]).then_inc(a_q32.sem, 1)
                act.wait_ge(d_parts.sem, d_parts.at(b - 1, 6 * DC))
                nc.scalar.copy(pa[:, m], A[2 + m][:]).then_inc(a_pa.sem, 1)
                second_part(b, m)

            def second_part(b, n):
                act.wait_ge(a_r1.sem, a_r1.at(b, n + 1))
                nc.scalar.copy(pb[:, n % DC], r1[:, n % DC]).then_inc(a_pb.sem, 1)

            def kv(b, j):
                act.wait_ge(a_kv.sem, a_kv.at(b, 2 * j + 1))
                act.wait_ge(a_state.sem, a_state.at(b - 1, TILES))
                nc.scalar.copy(k32[:, j], A[0][:, 0:D]).then_inc(a_k32.sem, 1)
                act.wait_ge(a_clip.sem, a_clip.at(b, j + 1))
                act.wait_ge(a_wv.sem, a_wv.at(b - 1, TILES * NQ))
                act.wait_ge(a_O.sem, a_O.at(b - 1, TILES * NQ))
                nc.scalar.activation(vp[:, j, :, HD], g32[:, j, 0:H], ACT.Exp).then_inc(a_i.sem, 1)
                nc.scalar.activation(fg[:, j], g32[:, j, H:2 * H], ACT.Tanh, scale=0.5).then_inc(a_tf.sem, 1)

            def kT(b, k):
                act.wait_ge(d_parts.sem, d_parts.at(b, 3 * DC))
                for m in range(DC):
                    act.wait_ge(a_kT.sem, a_kT.at(b, m + 1))
                    nc.scalar.copy(pa[:, m], A[2 + m][:]).then_inc(a_pa.sem, 1)
                for m in range(DC):
                    second_part(b, DC + m)

            def fT_(b, k):
                act.wait_ge(a_fT.sem, a_fT.at(b, 1))
                act.wait_ge(d_f.sem, d_f.at(b - 1, NQ))
                src = A[0][0:H].rearrange("h (j t) -> h j t", j=TILES)
                nc.scalar.copy(fTz[:, :, 1:P], src[:, :, 1:P]).then_inc(a_fTs.sem, 1)
                nc.scalar.copy(fT[:], src).then_inc(a_fTs.sem, 1)

            def dec(b, k):
                act.wait_ge(a_dT.sem, a_dT.at(b, 1))
                act.wait_ge(a_cb.sem, a_cb.at(b, 0))
                nc.scalar.copy(decay[:], A[1][:, 0:TILES * H + DC * TILES]).then_inc(a_dec.sem, 1)

            def yT_(b, j):
                act.wait_ge(a_yT.sem, a_yT.at(b, j + 1))
                if j:
                    act.wait_ge(a_wo.sem, a_wo.at(b, j))
                else:
                    act.wait_ge(a_wo.sem, a_wo.at(b - 1, TILES))
                nc.scalar.copy(flat(yT_h[:]), A[0][:, 0:D]).then_inc(a_yh.sem, 1)

            def gu(b, i):
                rows = P if i < IT - 1 else last_rows
                act.wait_ge(a_gu.sem, a_gu.at(b, 2 * i + 1))
                nc.scalar.activation(th[:rows], A[2][:rows], ACT.Tanh, scale=0.5).then_inc(a_th.sem, 1)
                act.wait_ge(a_m.sem, a_m.at(b, i + 1))
                if i > 1:
                    act.wait_ge(a_md.sem, a_md.at(b, i - 1))
                nc.scalar.copy(m_h[:rows, i % 2], gm[:rows]).then_inc(a_mh.sem, 1)

            schedule(act, {"late": late_hi, "f_tr": tr, "a_copy": acopy, "f_lora": lora, "f_act": relu, "a_tr": atr, "a_q": q, "a_kv": kv, "a_kT": kT,
                           "a_fT": fT_, "a_decay": dec, "a_yT": yT_, "a_tr2": atr2, "a_gu": gu})

        @block.vector
        def _(dve):
            v = nc.vector
            v.memset(cb[:], 0.0).then_inc(s_setup.sem, 1)
            v.memset(keep[:], 1.0).then_inc(s_setup.sem, 1)
            v.memset(zeros[:], 0.0).then_inc(s_setup.sem, 1)
            v.memset(fTz[:], 0.0).then_inc(s_setup.sem, 1)
            v.memset(u_st[LS:P].bitcast(F32), 1.0).then_inc(s_setup.sem, 1)

            def split_early():
                count = 0
                for n, (stage, src, hi, lo) in enumerate(early):
                    s = flat(stage[0:hi.shape[0]])
                    dve.wait_ge(s_early[n].sem, s_early[n].at(1, 0))
                    dve.wait_ge(s_early_hi.sem, s_early_hi.at(n + 1 + (n > 2), 0))
                    if lo is not None:
                        v.tensor_tensor(flat(lo), s, flat(hi).bitcast(F32), ALU.subtract).then_inc(s_early_lo.sem, 1)
                        continue
                    v.tensor_tensor(hi[LS:LS2], s[LS:LS2], hi[LS:LS2].bitcast(F32), ALU.subtract).then_inc(s_early_lo.sem, 1)
                    v.tensor_tensor(hi[ER:2 * ER], s[ER:2 * ER], hi[ER:2 * ER].bitcast(F32), ALU.subtract
                                    ).then_inc(s_early_lo.sem, 1)

            def late_lo(n):
                src, hi, lo, factors, const = late[n]
                dve.wait_ge(s_late[n % 2].sem, s_late[n % 2].at(n // 2 + 1, 0))
                for c in range(hi.shape[1]):
                    dve.wait_ge(s_late_hi.sem, s_late_hi.at(late_count(n) + c + 1, 0))
                    v.scalar_tensor_tensor(lo[:, c], late_stage(n)[:, c], const if factors is None else factors[:, c:c + 1],
                                           hi[:, c].bitcast(F32), ALU.mult, ALU.subtract).then_inc(s_late_lo.sem, 1)

            def moments(st, mv, done, run, before, eps):
                means, squares = (st[:, :, 1], st[:, :, 4]), (st[:, :, 2], st[:, :, 5])
                v.tensor_tensor(mv[:, 0], *means, ALU.add).then_inc(done.sem, 1)
                v.tensor_tensor(mv[:, 1], *means, ALU.subtract).then_inc(done.sem, 1)
                v.tensor_tensor(mv[:, 2], *squares, ALU.add).then_inc(done.sem, 1)
                dve.wait_ge(done.sem, done.at(run, before + 1))
                v.tensor_scalar(mv[:, 3], mv[:, 0], 0.5, None, ALU.mult).then_inc(done.sem, 1)
                dve.wait_ge(done.sem, done.at(run, before + 2))
                v.tensor_tensor(mv[:, 4], mv[:, 1], mv[:, 1], ALU.mult).then_inc(done.sem, 1)
                dve.wait_ge(done.sem, done.at(run, before + 3))
                v.tensor_scalar(mv[:, 5], mv[:, 2], 1.0 / D, eps, ALU.mult, ALU.add).then_inc(done.sem, 1)
                dve.wait_ge(done.sem, done.at(run, before + 6))

            def stats(run, b, first, k):
                if first:
                    dve.wait_ge(s_xin.sem, s_xin.at(b, 1))
                    x = x_in
                else:
                    dve.wait_ge(a_x3.sem, a_x3.at(b, TILES))
                    x = x_out
                for j in range(TILES):
                    v.bn_stats(f_st[:, j], x[:, j]).then_inc(f_stats.sem, 1)
                dve.wait_ge(f_stats.sem, f_stats.at(run, TILES))
                moments(f_st, f_mv, f_mean, run, 0, 1e-5)
                v.scalar_tensor_tensor(f_ve[:], f_mv[:, 4], 0.25, f_mv[:, 5], ALU.mult, ALU.add).then_inc(f_var.sem, 1)

            def normal(run, b, first, k):
                x = x_in if first else x_out
                dve.wait_ge(f_rstd.sem, f_rstd.at(run, 1))
                dve.wait_ge(f_tr.sem, f_tr.at(run - 1, DC))
                for j in range(TILES):
                    v.tensor_scalar(xn[:, j], x[:, j], f_mv[:, 3, j:j + 1], f_rs[:, j:j + 1], ALU.subtract, ALU.mult
                                    ).then_inc(f_xn.sem, 1)

            def tr(run, b, first, k):
                for c in range(DC):
                    dve.wait_ge(f_xh.sem, f_xh.at(run, c + 1))
                    v.tensor_tensor(xT_l[:, c], T[c][:], xT_h[:, c].bitcast(F32), ALU.subtract).then_inc(f_xl.sem, 1)

            def gate(run, b, first, k):
                dve.wait_ge(f_route.sem, f_route.at(run, 1))
                routed = T[0][:, 0:TILES * GW].rearrange("p (j n) -> p j n", j=TILES)
                each = lambda t: t[:].unsqueeze(2).to_broadcast([P, TILES, E])
                v.tensor_tensor(lg[:], routed[:, :, 0:E], route_b[:].unsqueeze(1).to_broadcast([P, TILES, E]), ALU.add
                                ).then_inc(f_sel.sem, 1)
                dve.wait_ge(f_sel.sem, f_sel.at(run, 1))
                v.tensor_reduce(lmax[:], lg[:], AX_X, ALU.max).then_inc(f_sel.sem, 1)
                dve.wait_ge(f_sel.sem, f_sel.at(run, 2))
                v.tensor_tensor(won[:], lg[:], each(lmax), ALU.is_ge).then_inc(f_sel.sem, 1)
                dve.wait_ge(f_sel.sem, f_sel.at(run, 3))
                v.tensor_tensor(won2[:], won[:], prio[:], ALU.mult).then_inc(f_sel.sem, 1)
                dve.wait_ge(f_sel.sem, f_sel.at(run, 4))
                v.tensor_reduce(wmax[:], won2[:], AX_X, ALU.max).then_inc(f_sel.sem, 1)
                dve.wait_ge(f_sel.sem, f_sel.at(run, 5))
                v.tensor_tensor(onehot[:], won2[:], each(wmax), ALU.is_equal).then_inc(f_sel.sem, 1)
                dve.wait_ge(f_sel.sem, f_sel.at(run, 6))
                dve.wait_ge(f_uT.sem, f_uT.at(run - 1, 1))
                for n in range(3):
                    v.tensor_tensor(u_rep[:, :, n].rearrange("p j (e r) -> p j e r", e=E),
                                    routed[:, :, E:GW].rearrange("p j (e r) -> p j e r", e=E),
                                    onehot[:].unsqueeze(3).to_broadcast([P, TILES, E, R]), ALU.mult).then_inc(f_u.sem, 1)

            def lora(run, b, first, k):
                dve.wait_ge(f_uh.sem, f_uh.at(run, 2))
                v.tensor_tensor(u_st[2 * ER:LS], T[1][2 * ER:LS], u_hi, ALU.subtract).then_inc(f_ul.sem, 1)

            def relu(run, b, first, f):
                dve.wait_ge(f_rh.sem, f_rh.at(run, f + 1))
                dve.wait_ge(f_dn.sem, f_dn.at(run, f - 1))
                v.scalar_tensor_tensor(r_l[:, f % 2], U[f % 2][:], 0.0, r_h[:, f % 2].bitcast(F32), ALU.max, ALU.subtract
                                       ).then_inc(f_rl.sem, 1)

            def fin(run, b, first, k):
                dve.wait_ge(f_dn.sem, f_dn.at(run, FT))
                dve.wait_ge(f_xb.sem, f_xb.at(run, 1))
                if first:
                    dve.wait_ge(a_xc.sem, a_xc.at(b - 1, 1))
                x, to = (x_in, x_mid) if first else (x_out, x_out)
                for j in range(TILES):
                    v.scalar_tensor_tensor(to[:, j], T[j // 2][:, (j % 2) * D:(j % 2 + 1) * D], 0.5, x[:, j],
                                           ALU.mult, ALU.add).then_inc(f_y.sem, 1)

            def astats(b, k):
                dve.wait_ge(f_y.sem, f_y.at(ffn1_run(b), TILES))
                for j in range(TILES):
                    v.bn_stats(a_st[:, j], x_mid[:, j]).then_inc(a_stats.sem, 1)
                dve.wait_ge(a_stats.sem, a_stats.at(b, TILES))
                moments(a_st, a_mv, a_mean, b, 0, 1e-5)
                v.scalar_tensor_tensor(a_sm[:, 0], a_mv[:, 4], 0.25, a_mv[:, 5], ALU.mult, ALU.add).then_inc(a_small.sem, 1)
                v.tensor_scalar(a_sm[:, 5], a_mv[:, 2], 1.0 / D, None, ALU.mult).then_inc(a_small.sem, 1)
                dve.wait_ge(a_small.sem, a_small.at(b, 2))
                v.scalar_tensor_tensor(a_sm[:, 5], a_mv[:, 4], 0.25, a_sm[:, 5], ALU.mult, ALU.add).then_inc(a_small.sem, 1)

            def az(b, k):
                dve.wait_ge(a_pow.sem, a_pow.at(b, 1))
                dve.wait_ge(a_xx.sem, a_xx.at(b - 1, 1))
                v.tensor_tensor(a_sm[:, 3], a_sm[:, 1], a_sm[:, 1], ALU.mult).then_inc(a_small.sem, 1)
                for j in range(TILES):
                    v.tensor_scalar(z[:, j], x_mid[:, j], a_mv[:, 3, j:j + 1], a_sm[:, 1, j:j + 1], ALU.subtract, ALU.mult
                                    ).then_inc(a_z.sem, 1)
                dve.wait_ge(a_small.sem, a_small.at(b, 4))
                v.tensor_tensor(a_sm[:, 3], a_sm[:, 3], a_sm[:, 5], ALU.mult).then_inc(a_small.sem, 1)
                dve.wait_ge(a_small.sem, a_small.at(b, 5))
                v.tensor_scalar(a_sm[:, 0], a_sm[:, 3], 1e-6, None, ALU.add).then_inc(a_small.sem, 1)

            def anormal(b, k):
                dve.wait_ge(a_pow.sem, a_pow.at(b, 2))
                dve.wait_ge(a_tr.sem, a_tr.at(b, 0))
                for j in range(TILES):
                    dve.wait_ge(a_z.sem, a_z.at(b, j + 1))
                    v.tensor_scalar(hn[:, j], z[:, j], a_sm[:, 2, j:j + 1], None, ALU.mult).then_inc(a_h.sem, 1)

            def atr(b, k):
                for c in range(DC):
                    dve.wait_ge(a_hh.sem, a_hh.at(b, c + 1))
                    v.tensor_tensor(hT_l[:, c], U[c][:], hT_h[:, c].bitcast(F32), ALU.subtract).then_inc(a_hl.sem, 1)

            def atr2(b, k):
                for c in range(DC):
                    dve.wait_ge(a_hh.sem, a_hh.at(b, DC + c + 1))
                    v.tensor_tensor(hT_l[:, c], A[c][:], hT_h[:, c].bitcast(F32), ALU.subtract).then_inc(a_hl.sem, 1)

            def q(b, m):
                dve.wait_ge(a_pa.sem, a_pa.at(b, m + 1))
                dve.wait_ge(a_pc.sem, a_pc.at(b, 0))
                v.tensor_tensor(r1[:, m], A[2 + m][:], pa[:, m], ALU.subtract).then_inc(a_r1.sem, 1)

            def kv(b, j):
                dve.wait_ge(a_k32.sem, a_k32.at(b, j + 1))
                dve.wait_ge(a_tf.sem, a_tf.at(b, 0))
                v.tensor_tensor(g32[:, j], A[0][:, D:D + 2 * H], gate_bias[:], ALU.add).then_inc(a_g.sem, 1)
                dve.wait_ge(a_g.sem, a_g.at(b, j + 1))
                v.tensor_scalar(g32[:, j, 0:H], g32[:, j, 0:H], -10.0, 10.0, ALU.max, ALU.min).then_inc(a_clip.sem, 1)
                dve.wait_ge(a_i.sem, a_i.at(b, j + 1))
                dve.wait_ge(a_kv.sem, a_kv.at(b, 2 * j + 2))
                v.tensor_tensor(vp[:, j, :, 0:HD], A[1][:, 0:D].rearrange("p (h d) -> p h d", h=H),
                                vp[:, j, :, HD:HV].to_broadcast([P, H, HD]), ALU.mult).then_inc(a_v.sem, 1)
                dve.wait_ge(a_tf.sem, a_tf.at(b, j + 1))
                v.tensor_scalar(fg[:, j], fg[:, j], 0.5, 0.5, ALU.mult, ALU.add).then_inc(a_f.sem, 1)

            def kT(b, k):
                for m in range(DC):
                    dve.wait_ge(a_pa.sem, a_pa.at(b, DC + m + 1))
                    dve.wait_ge(a_pc.sem, a_pc.at(b, m + 1))
                    v.tensor_tensor(r1[:, m], A[2 + m][:], pa[:, m], ALU.subtract).then_inc(a_r1.sem, 1)

            def fT_(b, k):
                dve.wait_ge(a_fTs.sem, a_fTs.at(b, 2))
                dve.wait_ge(a_dT.sem, a_dT.at(b, 0))
                for j in range(TILES):
                    v.tensor_tensor_scan(cumT[:, j], fT[:, j], zeros[:], 1.0, ALU.mult, ALU.add).then_inc(a_cum.sem, 1)

            def scan(b, u):
                j, g = divmod(u, NQ)
                dve.wait_ge(d_fb[g].sem, d_fb[g].at(b, j + 1))
                v.tensor_tensor_scan(dm[:, g], dm[:, g], ident4[:], 0.0, ALU.mult, ALU.add).then_inc(a_D.sem, 1)

            def score(b, u):
                g = u % NQ
                dve.wait_ge(a_D.sem, a_D.at(b, u + 1))
                dve.wait_ge(a_S.sem, a_S.at(b, u + 1))
                dve.wait_ge(a_O.sem, a_O.at(b, u - 1))
                v.tensor_tensor(pt[:, u % 2], A[2 + u % 2][:], dm[:, g], ALU.mult).then_inc(a_P.sem, 1)

            heads = lambda bank: bank[:, 0:H * HV].rearrange("p (h d) -> p h d", h=H)

            def carry(b, j):
                dve.wait_ge(a_oi.sem, a_oi.at(b, j + 1))
                cum = decay[:, j * H:(j + 1) * H].unsqueeze(2).to_broadcast([P, H, HV])
                v.tensor_tensor(o1[:], heads(A[1]), cum, ALU.mult).then_inc(a_t1.sem, 1)

            def sum_(b, j):
                dve.wait_ge(a_t1.sem, a_t1.at(b, j + 1))
                dve.wait_ge(a_O.sem, a_O.at(b, NQ * (j + 1)))
                v.tensor_tensor(o1[:], heads(A[0]), o1[:], ALU.add).then_inc(a_o.sem, 1)
                dve.wait_ge(a_o.sem, a_o.at(b, j + 1))
                v.tensor_scalar(den[:, 0], o1[:, :, HD], 1.0, None, ALU.max).then_inc(a_den.sem, 1)
                dve.wait_ge(a_den.sem, a_den.at(b, 3 * j + 1))
                v.scalar_tensor_tensor(den[:, 1], o1[:, :, HD], -1.0, den[:, 0], ALU.mult, ALU.max).then_inc(a_den.sem, 1)
                dve.wait_ge(a_den.sem, a_den.at(b, 3 * j + 2))
                v.reciprocal(den[:, 2], den[:, 1]).then_inc(a_den.sem, 1)
                dve.wait_ge(a_den.sem, a_den.at(b, 3 * j + 3))
                if j > 1:
                    dve.wait_ge(a_yT.sem, a_yT.at(b, j - 1))
                else:
                    dve.wait_ge(a_yT.sem, a_yT.at(b, 0))
                v.tensor_tensor(y[:, j % 2].rearrange("p (h d) -> p h d", h=H), o1[:, :, 0:HD],
                                den[:, 2].unsqueeze(2).to_broadcast([P, H, HD]), ALU.mult).then_inc(a_y.sem, 1)

            def state(b, j):
                dve.wait_ge(a_state.sem, a_state.at(b, j + 1))
                v.tensor_tensor(flat(cm[:]), A[1][:, 0:DC * HH * HV], headmask[:], ALU.mult).then_inc(a_cm.sem, 1)
                dve.wait_ge(a_cm.sem, a_cm.at(b, j + 1))
                for m in range(DC):
                    last = TILES * H + m * TILES + j
                    v.scalar_tensor_tensor(cb[:, m], cb[:, m], decay[:, last:last + 1], cm[:, m], ALU.mult, ALU.add
                                           ).then_inc(a_cb.sem, 1)
                dve.wait_ge(a_cb.sem, a_cb.at(b, 2 * j + 2))
                if j == TILES - 1:
                    v.tensor_scalar(flat(cb[:]), flat(cb[:]), keep[:, 0:1], None, ALU.mult).then_inc(a_cb.sem, 1)
                    v.tensor_scalar(keep[:], keep[:], -1.0, 1.0, ALU.mult, ALU.add).then_inc(a_cb.sem, 1)

            def yT_(b, j):
                dve.wait_ge(a_yh.sem, a_yh.at(b, j + 1))
                v.tensor_tensor(flat(yT_l[:]), A[0][:, 0:D], flat(yT_h[:]).bitcast(F32), ALU.subtract).then_inc(a_yl.sem, 1)

            def wo(b, j):
                dve.wait_ge(a_wo.sem, a_wo.at(b, j + 1))
                v.tensor_tensor(z[:, j], A[0][:, D:2 * D], z[:, j], ALU.add).then_inc(a_x2.sem, 1)
                dve.wait_ge(a_x2.sem, a_x2.at(b, j + 1))
                v.bn_stats(a_st[:, j], z[:, j]).then_inc(a_stats.sem, 1)

            def aln2(b, k):
                dve.wait_ge(a_stats.sem, a_stats.at(b, 2 * TILES))
                even, odd = a_st[:, :, 1], a_st[:, :, 4]
                v.tensor_tensor(a_mv[:, 0], even, even, ALU.mult).then_inc(a_mean.sem, 1)
                v.tensor_tensor(a_mv[:, 1], odd, odd, ALU.mult).then_inc(a_mean.sem, 1)
                v.tensor_tensor(a_mv[:, 2], a_st[:, :, 2], a_st[:, :, 5], ALU.add).then_inc(a_mean.sem, 1)
                dve.wait_ge(a_mean.sem, a_mean.at(b, 8))
                v.tensor_tensor(a_mv[:, 3], a_mv[:, 0], a_mv[:, 1], ALU.add).then_inc(a_mean.sem, 1)
                dve.wait_ge(a_mean.sem, a_mean.at(b, 9))
                v.tensor_scalar(a_mv[:, 5], a_mv[:, 2], 1.0 / D, 1e-6, ALU.mult, ALU.add).then_inc(a_mean.sem, 1)
                dve.wait_ge(a_mean.sem, a_mean.at(b, 11))
                v.scalar_tensor_tensor(a_sm[:, 3], a_mv[:, 3], 0.5, a_mv[:, 5], ALU.mult, ALU.add).then_inc(a_small.sem, 1)
                dve.wait_ge(a_pow.sem, a_pow.at(b, 3))
                dve.wait_ge(a_tr.sem, a_tr.at(b, DC))
                dve.wait_ge(a_pc.sem, a_pc.at(b, 2 * DC))
                for j in range(TILES):
                    v.tensor_scalar(hn[:, j], z[:, j], a_sm[:, 4, j:j + 1], None, ALU.mult).then_inc(a_h.sem, 1)

            def gu(b, i):
                rows = P if i < IT - 1 else last_rows
                dve.wait_ge(a_th.sem, a_th.at(b, i + 1))
                dve.wait_ge(a_ml.sem, a_ml.at(b, i))
                v.scalar_tensor_tensor(gm[:rows], th[:rows], 1.0, A[2][:rows], ALU.add, ALU.mult).then_inc(a_m1.sem, 1)
                dve.wait_ge(a_m1.sem, a_m1.at(b, i + 1))
                dve.wait_ge(a_gu.sem, a_gu.at(b, 2 * i + 2))
                v.tensor_tensor(gm[:rows], A[3][:rows], gm[:rows], ALU.mult).then_inc(a_m.sem, 1)

            def mfin(b, k):
                dve.wait_ge(a_md.sem, a_md.at(b, IT))
                dve.wait_ge(a_xx.sem, a_xx.at(b, 1))
                dve.wait_ge(s_xout.sem, s_xout.at(b, 0))
                for j in range(TILES):
                    v.tensor_tensor(x_out[:, j], A[j // 2][:, (j % 2) * D:(j % 2 + 1) * D], xc[:, j], ALU.add
                                    ).then_inc(a_x3.sem, 1)

            dve.wait_ge(s_setup.sem, s_setup.at(n_setup, 0))
            dve.wait_ge(s_const.sem, s_const.at(len(consts), 0))
            schedule(dve, {"setup": split_early, "late": late_lo, "f_stats": stats, "f_normal": normal, "f_tr": tr, "f_gate": gate, "f_lora": lora,
                           "f_act": relu, "f_fin": fin, "a_stats": astats, "a_z": az, "a_normal": anormal, "a_tr": atr, "a_q": q, "a_kv": kv, "a_kT": kT, "a_fT": fT_,
                           "a_scan": scan, "a_score": score, "a_carry": carry, "a_sum": sum_, "a_state": state, "a_yT": yT_,
                           "a_wo": wo, "a_ln2": aln2,
                           "a_tr2": atr2, "a_gu": gu, "a_mfin": mfin})

        @block.tensor
        def _(pe):
            def product(dst, left, right, first=True, last=True, **more):
                (lh, ll), (rh, rl) = left, right
                nc.tensor.matmul(dst, lh, rh, start=first, stop=False, **more)
                yield
                nc.tensor.matmul(dst, ll, rh, start=False, stop=False, **more)
                yield
                return nc.tensor.matmul(dst, lh, rl, start=False, stop=last, **more)

            def tiles(j):
                return slice((j % 2) * D, (j % 2 + 1) * D)

            def tr(run, b, first, k):
                pe.wait_ge(f_y.sem, f_y.at(run - 1, TILES))
                for c in range(DC):
                    for j in range(TILES):
                        pe.wait_ge(f_xn.sem, f_xn.at(run, j + 1))
                        done = nc.tensor.transpose(T[c][:, j * P:(j + 1) * P], xn[:, j, c * P:(c + 1) * P], ident[:])
                        if j == TILES - 1:
                            done.then_inc(f_tr.sem, 1)
                        yield

            def gate(run, b, first, k):
                pe.wait_ge(f_x32.sem, f_x32.at(run, DC))
                for j in range(TILES):
                    for c in range(DC):
                        done = nc.tensor.matmul(T[0][:, j * GW:(j + 1) * GW], xT[:, c, j * P:(j + 1) * P], route_w[:, c],
                                                start=c == 0, stop=c == DC - 1)
                        if j == TILES - 1 and c == DC - 1:
                            done.then_inc(f_route.sem, 1)
                        yield

            def up(run, b, first, f):
                if isinstance(run, int) and run == 0 and f == 0:
                    pe.wait_ge(s_early_hi.sem, s_early_hi.at(len(early) + 1, 0))
                    pe.wait_ge(s_early_lo.sem, s_early_lo.at(n_early_lo, 0))
                pe.wait_ge(f_rl.sem, f_rl.at(run, f - 1))
                cols = slice(f * P, (f + 1) * P)
                for c in range(DC):
                    pe.wait_ge(f_xl.sem, f_xl.at(run, c + 1))
                    yield from product(U[f % 2][:], (wi_h[:, c, cols], wi_l[:, c, cols]), (xT_h[:, c], xT_l[:, c]), c == 0, False)
                    yield

            def lora(run, b, first, k):
                pe.wait_ge(f_u.sem, f_u.at(run, 3))
                pe.wait_ge(f_xl.sem, f_xl.at(run, DC))
                for j in range(TILES):
                    done = nc.tensor.transpose(T[1][0:LS, j * P:(j + 1) * P], flat(u_rep[:, j]), ident[:])
                    if j == TILES - 1:
                        done.then_inc(f_uT.sem, 1)
                    yield

            def act_(run, b, first, f):
                pe.wait_ge(f_ul.sem, f_ul.at(run, 1))
                pe.wait_ge(f_uh.sem, f_uh.at(run, 1))
                nc.tensor.matmul(U[f % 2][:], lora_b[0:LS2, f * P:(f + 1) * P], u_st[0:LS2], start=False, stop=True
                                 ).then_inc(f_up.sem, 1)
                yield

            def down(run, b, first, f):
                if f == 0:
                    pe.wait_ge(f_u.sem, f_u.at(run, 3))
                    pe.wait_ge(f_ul.sem, f_ul.at(run, 1))
                pe.wait_ge(f_rl.sem, f_rl.at(run, f + 1))
                for j in range(TILES):
                    t = slice(j * P, (j + 1) * P)
                    done = yield from product(T[j // 2][:, tiles(j)], (r_h[:, f % 2, t], r_l[:, f % 2, t]), (wo_h[:, f], wo_l[:, f]),
                                              f == 0 and j % 2 == 0, f == FT - 1, skip_group_check=True)
                    if j == TILES - 1:
                        done.then_inc(f_dn.sem, 1)
                    yield

            def atr(b, k):
                pe.wait_ge(f_rl.sem, f_rl.at(ffn1_run(b), FT))
                pe.wait_ge(a_h.sem, a_h.at(b, TILES))
                for c in range(DC):
                    for j in range(TILES):
                        done = nc.tensor.transpose(U[c][:, j * P:(j + 1) * P], hn[:, j, c * P:(c + 1) * P], ident[:])
                        if j == TILES - 1:
                            done.then_inc(a_tr.sem, 1)
                        yield

            def atr2(b, k):
                pe.wait_ge(a_x2.sem, a_x2.at(b, TILES))
                pe.wait_ge(a_cb.sem, a_cb.at(b, 2 * TILES))
                for c in range(DC):
                    for j in range(TILES):
                        pe.wait_ge(a_h.sem, a_h.at(b, TILES + j + 1))
                        done = nc.tensor.transpose(A[c][:, j * P:(j + 1) * P], hn[:, j, c * P:(c + 1) * P], ident[:])
                        if j == TILES - 1:
                            done.then_inc(a_tr.sem, 1)
                        yield

            def q(b, m):
                if isinstance(b, int) and b == 0 and m == 0:
                    pe.wait_ge(s_late_lo.sem, s_late_lo.at(late_count(len(late)), 0))
                pe.wait_ge(a_m.sem, a_m.at(b - 1, IT))
                cols = slice(m * P, (m + 1) * P)
                for c in range(DC):
                    pe.wait_ge(a_hl.sem, a_hl.at(b, c + 1))
                    done = yield from product(A[2 + m][:], (wq_h[:, c, cols], wq_l[:, c, cols]), (hT_h[:, c], hT_l[:, c]),
                                              c == 0, c == DC - 1)
                    if c == DC - 1:
                        done.then_inc(a_q.sem, 1)
                    yield

            def kv(b, j):
                if j == 0:
                    pe.wait_ge(a_x3.sem, a_x3.at(b - 1, TILES))
                pe.wait_ge(a_g.sem, a_g.at(b, j))
                t = slice(j * P, (j + 1) * P)
                for n, (lo_col, hi_col) in enumerate(((0, KI), (KI, KI + D))):
                    if n:
                        pe.wait_ge(a_v.sem, a_v.at(b, j))
                        pe.wait_ge(a_hl.sem, a_hl.at(b, DC))
                    for c in range(DC):
                        done = yield from product(A[n][:, 0:hi_col - lo_col], (hT_h[:, c, t], hT_l[:, c, t]),
                                                  (wkv_h[:, c, lo_col:hi_col], wkv_l[:, c, lo_col:hi_col]), c == 0, c == DC - 1)
                        if c == DC - 1:
                            done.then_inc(a_kv.sem, 1)
                        yield

            def kT(b, k):
                pe.wait_ge(a_k32.sem, a_k32.at(b, TILES))
                for m in range(DC):
                    pe.wait_ge(a_r1.sem, a_r1.at(b, m + 1))
                    for j in range(TILES):
                        done = nc.tensor.transpose(A[2 + m][:, j * P:(j + 1) * P], k32[:, j, m * P:(m + 1) * P], ident[:])
                        if j == TILES - 1:
                            done.then_inc(a_kT.sem, 1)
                        yield

            def fT_(b, k):
                pe.wait_ge(a_f.sem, a_f.at(b, TILES))
                pe.wait_ge(a_g.sem, a_g.at(b, TILES))
                for j in range(TILES):
                    done = nc.tensor.transpose(A[0][0:H, j * P:(j + 1) * P], fg[:, j], ident[:])
                    if j == TILES - 1:
                        done.then_inc(a_fT.sem, 1)
                    yield

            def dec(b, k):
                value = held(pe, a_cum.at(b, TILES))
                pe.wait_ge(s_const.sem, s_const.at(len(consts), 0))
                pe.wait_ge(a_cum.sem, value)
                pe.wait_ge(a_v.sem, a_v.at(b, TILES))
                for j in range(TILES):
                    nc.tensor.transpose(A[1][:, j * H:(j + 1) * H], cumT[:, j], ident[0:H, 0:H])
                    yield
                for m in range(DC):
                    at = TILES * H + m * TILES
                    done = nc.tensor.matmul(A[1][:, at:at + TILES], headsel[:, m], cumT[:, :, P - 1], start=True, stop=True)
                    if m == DC - 1:
                        done.then_inc(a_dT.sem, 1)
                    yield

            def score(b, u):
                j, g = divmod(u, NQ)
                pe.wait_ge(d_stack.sem, d_stack.at(b, 2 * SLOTS * max(j, 1)))
                if u < 2:
                    pe.wait_ge(a_r1.sem, a_r1.at(b, 2 * DC))
                else:
                    pe.wait_ge(a_P.sem, a_P.at(b, u - 1))
                t = slice((j % 2) * P, (j % 2 + 1) * P)
                for n in range(QUAD):
                    h = QUAD * g + n
                    done = nc.tensor.matmul(A[2 + u % 2][:, n * P:(n + 1) * P], ks[:, h, t], qs[:, h, t], start=True, stop=True)
                    if n == QUAD - 1:
                        done.then_inc(a_S.sem, 1)
                    yield

            def mix(b, u):
                j, g = divmod(u, NQ)
                pe.wait_ge(a_P.sem, a_P.at(b, u + 1))
                if u == 0:
                    pe.wait_ge(a_fTs.sem, a_fTs.at(b, 2))
                elif g == 0:
                    pe.wait_ge(a_x2.sem, a_x2.at(b, j))
                for n in range(QUAD):
                    h = QUAD * g + n
                    done = nc.tensor.matmul(A[0][:, h * HV:(h + 1) * HV], pt[:, u % 2, n * P:(n + 1) * P], vp[:, j, h],
                                            start=True, stop=True)
                    if n == QUAD - 1:
                        done.then_inc(a_O.sem, 1)
                    yield

            def carry(b, j):
                if j == 0:
                    pe.wait_ge(a_dec.sem, a_dec.at(b, 1))
                pe.wait_ge(a_cb.sem, a_cb.at(b, 2 * j))
                t = slice(j * P, (j + 1) * P)
                for m in range(DC):
                    done = nc.tensor.matmul(A[1][:, m * HH * HV:(m + 1) * HH * HV], q32[:, m, t], cb[:, m], start=True, stop=True)
                    if m == DC - 1:
                        done.then_inc(a_oi.sem, 1)
                    yield

            def state(b, j):
                pe.wait_ge(a_t1.sem, a_t1.at(b, j + 1))
                pe.wait_ge(a_wv.sem, a_wv.at(b, NQ * (j + 1)))
                for m in range(DC):
                    done = nc.tensor.matmul(A[1][:, m * HH * HV:(m + 1) * HH * HV], k32[:, j, m * P:(m + 1) * P],
                                            flat(wv[:, m * HH:(m + 1) * HH]), start=True, stop=True)
                    if m == DC - 1:
                        done.then_inc(a_state.sem, 1)
                    yield

            def yT_(b, j):
                pe.wait_ge(a_y.sem, a_y.at(b, j + 1))
                pe.wait_ge(a_o.sem, a_o.at(b, j + 1))
                for c in range(DC):
                    done = nc.tensor.transpose(A[0][:, c * P:(c + 1) * P], y[:, j % 2, c * P:(c + 1) * P], ident[:])
                    if c == DC - 1:
                        done.then_inc(a_yT.sem, 1)
                    yield

            def wo(b, j):
                pe.wait_ge(a_yl.sem, a_yl.at(b, j + 1))
                for c in range(DC):
                    done = yield from product(A[0][:, D:2 * D], (yT_h[:, c], yT_l[:, c]), (wao_h[:, c], wao_l[:, c]), c == 0, c == DC - 1)
                    if c == DC - 1:
                        done.then_inc(a_wo.sem, 1)
                    yield

            def gu(b, i):
                rows = P if i < IT - 1 else last_rows
                if i:
                    pe.wait_ge(a_m.sem, a_m.at(b, i))
                else:
                    pe.wait_ge(a_P.sem, a_P.at(b, TILES * NQ))
                for n in range(2):
                    cols = slice(n * I + i * P, n * I + i * P + rows)
                    for c in range(DC):
                        pe.wait_ge(a_hl.sem, a_hl.at(b, DC + c + 1))
                        done = yield from product(A[2 + n][:rows], (wgu_h[:, c, cols], wgu_l[:, c, cols]), (hT_h[:, c], hT_l[:, c]),
                                                  c == 0, c == DC - 1)
                        if c == DC - 1:
                            done.then_inc(a_gu.sem, 1)
                        yield

            def mdown(b, i):
                rows = P if i < IT - 1 else last_rows
                pe.wait_ge(a_ml.sem, a_ml.at(b, i + 1))
                for j in range(TILES):
                    t = slice(j * P, (j + 1) * P)
                    done = yield from product(A[j // 2][:, tiles(j)], (m_h[:rows, i % 2, t], m_l[:rows, i % 2, t]),
                                              (wd_h[:rows, i], wd_l[:rows, i]), i == 0 and j % 2 == 0, i == IT - 1,
                                              skip_group_check=True)
                    if j == TILES - 1:
                        done.then_inc(a_md.sem, 1)
                    yield

            pe.wait_ge(s_const.sem, s_const.at(len(consts), 0))
            pe.wait_ge(s_setup.sem, s_setup.at(n_setup, 0))
            schedule(pe, {"f_tr": tr, "f_gate": gate, "f_up": up, "f_lora": lora, "f_act": act_, "f_down": down,
                          "a_tr": atr, "a_q": q, "a_kv": kv, "a_kT": kT, "a_fT": fT_, "a_decay": dec, "a_score": score,
                          "a_mix": mix, "a_carry": carry, "a_state": state, "a_yT": yT_, "a_wo": wo,
                          "a_tr2": atr2, "a_gu": gu, "a_mdown": mdown})


def kernel(**inputs):
    from concourse import bacc
    from concourse.bass_utils import run_bass_kernel_spmd

    g = {name: np.asarray(v) for name, v in inputs.items()}
    att = lambda name: g["L0_attn_" + name]
    ffn = lambda name: g["L0_ffn_" + name]
    cat = np.concatenate
    lora = ffn("lora_B").transpose(0, 2, 1).reshape(ER, F)
    bias = ffn("wi_b")[None]
    head = np.arange(P) // HD
    arrays = {
        "x": att("x").reshape(BLOCKS, TILES, P, D),
        "wi": ffn("wi_W").T, "wo": ffn("wo_W").T,
        "lora": cat([lora, lora, lora, bias, bias]),
        "wq": att("wq"), "wkv": cat([att("wk"), att("wi"), att("wf"), att("wv")], axis=1), "wao": att("wo"),
        "wgu": cat([att("w_gate"), att("w_up")], axis=1), "wd": att("w_down"),
        "route_w": cat([ffn("gate_W"), ffn("lora_A").reshape(ER, D)]).T,
        "route_b": ffn("gate_b"), "wo_b": ffn("wo_b"), "gate_bias": cat([att("bi"), att("bf")]),
        "ln1": att("ln1_w").reshape(DC, P).T, "ln2": att("ln2_w").reshape(DC, P).T,
        "ident": np.eye(P, dtype=np.float32), "ident4": np.tile(np.eye(P, dtype=np.float32), (1, QUAD)),
        "headmask": np.tile(np.repeat(head[:, None] == np.arange(HH), HV, axis=1), (1, DC)).astype(np.float32),
        "headsel": np.stack([np.arange(H)[:, None] == head + m * HH for m in range(DC)], axis=1).astype(np.float32),
        "prio": np.broadcast_to(np.arange(E, 0, -1, dtype=np.float32), (P, TILES, E)),
    }
    arrays = {k: np.ascontiguousarray(v) for k, v in arrays.items()}
    nc = bacc.Bacc("TRN2", target_bir_lowering=False, num_devices=1, dynamic_dma_scratch_size=1024)
    a = {k: nc.dram_tensor("in_" + k, v.shape, mybir.dt.from_np(v.dtype), kind="ExternalInput").ap() for k, v in arrays.items()}
    out = nc.dram_tensor("out", (BLOCKS, TILES, P, D), F32, kind="ExternalOutput").ap()
    build(nc, a, out)
    r = run_bass_kernel_spmd(nc, [{"in_" + k: v for k, v in arrays.items()}], core_ids=[0])
    return r.results[0]["out"].reshape(N_SEQ, SEQ, D)
```

```python
import numpy as np

import concourse.bass as bass
import concourse.mybir as mybir
from concourse.alu_op_type import AluOpType as ALU

P = 128
N_SEQ, SEQ, D = 4, 1024, 256
TILES = 4
BLOCK = TILES * P
BLOCKS = N_SEQ * SEQ // BLOCK
DC = D // P
F = 1024
FT = F // P
E, R = 8, 4
ER = E * R
GW = E + ER
H, HD = 16, 16
HV = HD + 1
HH = P // HD
I = 704
IT = -(-I // P)
KI = D + 2 * H
QUAD = 4
NQ = H // QUAD
SLOTS = 6
STACK = SLOTS * HD
SLOT_RUNS = (((0, 1), (0, 1), (0, 2), (1, 3)), ((0, 3), (0, 2), (0, 1)))
LOADS = sum(len(runs) for runs in SLOT_RUNS)
LS = 3 * ER
LS2 = LS + 2

F32, F32R, BF16 = mybir.dt.float32, mybir.dt.float32r, mybir.dt.bfloat16
ACT = mybir.ActivationFunctionType
AX_X = mybir.AxisListType.X


class Signal:

    def __init__(self, sem, per, step=1):
        self.sem, self.per, self.step = sem, per, step

    def at(self, run, count):
        value = (run * self.per + count) * self.step
        return max(value, 0) if isinstance(value, int) else value


def iteration(ffn1, ffn2, att, ffn1_next, att_next):
    present = {"1": ffn1, "2": ffn2, "a": att, "n": ffn1_next, "m": att_next}
    order = """
        a kv 0; 1 up 3; a stack 0; a kv 1; 2 stats; 1 down 1; 1 act 3; a kv 2; 1 up 4; 2 normal; a kv 3; a kT; 1 down 2; a fT; a k2; 1 act 4; 1 up 5;
        1 down 3; 1 act 5; a decay; 1 up 6; a stack_k; a copy; 1 down 4; 1 act 6; 1 up 7; 1 down 5; 1 act 7; a scan 0; a scan 1;
        1 down 6; 2 tr; a carry 0; a score 0; a score 1; 1 down 7; a scan 2;
        a mix 0; a score 2; a scan 3; 1 fin; a mix 1; a score 3; a stack 2; a scan 4; 2 up 0; a mix 2; a mix 3; n load;
        a sum 0; a state 0; a score 4; 2 up 1; a yT 0; a scan 5; 2 gate; a score 5; a carry 1; a wo 0; a scan 6;
        a mix 4; a score 6; 2 select; a scan 7; a mix 5; a score 7; a stack 3; a mix 6; 2 lora; a scan 8; a mix 7; 2 act 0; 2 act 1;
        a sum 1; a state 1; a score 8; 2 up 2; a yT 1; a scan 9; a score 9; 2 down 0; a carry 2; a wo 1; 2 act 2; 2 up 3;
        a scan 10; a mix 8; a score 10; a scan 11; 2 down 1; 2 act 3; a mix 9; a score 11; 2 up 4; a mix 10; 2 down 2; 2 act 4;
        a scan 12; a mix 11; a sum 2; a state 2; a score 12; 2 up 5; a yT 2; a scan 13; 2 down 3; a score 13; a carry 3;
        a wo 2; 2 act 5; n stats; 2 up 6; a scan 14; a mix 12; a score 14; 2 down 4; 2 act 6; a scan 15; a mix 13; a score 15; 2 up 7;
        n normal; a mix 14; a mix 15; a sum 3; a state 3; 2 down 5; 2 act 7; a yT 3; 2 down 6; a wo 3; a ln2; n tr; a normal2; 2 down 7; n up 0; a tr2;
        2 fin; n up 1; a gu 0; n gate; a gu 1; n select; a mdown 0; a gu 2; m stats; a mdown 1; n lora; a gu 3; m z;
        n act 0; n act 1; a mdown 2; a gu 4; m normal; a mdown 3; a gu 5; m tr; a mdown 4; n up 2; m q 0; a mdown 5; a mfin;
        m q 1; n down 0; n act 2"""
    for step in order.split(";"):
        stage, name, *index = step.split()
        if present[stage]:
            yield stage, name, int(index[0]) if index else 0


def build(nc, a, out):
    from contextlib import ExitStack

    ctx = ExitStack()
    with ctx:
        def sb(name, shape, dt=F32):
            return ctx.enter_context(nc.sbuf_tensor(name, shape, dt))

        def sig(name, per=1, step=1):
            return Signal(ctx.enter_context(nc.semaphore(name)), per, step)

        ident = sb("ident", [P, P])
        ident4 = sb("ident4", [P, QUAD * P])
        headmask = sb("headmask", [P, DC * HH * HV])
        headsel = sb("headsel", [H, DC, P])
        prio = sb("prio", [P, TILES, E])
        zeros = sb("zeros", [H, P])
        minus_half = sb("minus_half", [P, TILES])
        def pair(name, shape):
            return sb(name + "_hi", shape, F32R), sb(name + "_lo", shape, F32R)

        wi_h, wi_l = pair("wi", [P, DC, F])
        wo_h, wo_l = pair("wo", [P, FT, D])
        wq_h, wq_l = pair("wq", [P, DC, D])
        wkv_h, wkv_l = pair("wkv", [P, DC, KI + D])
        wao_h, wao_l = pair("wao", [P, DC, D])
        wgu_h, wgu_l = pair("wgu", [P, DC, 2 * I])
        wd_h, wd_l = pair("wd", [P, IT, D])
        lora_b = sb("lora_b", [P, F], F32R)
        route_w = sb("route_w", [P, DC, GW])
        route_b = sb("route_b", [P, E])
        half_wo_b = sb("half_wo_b", [P, D])
        gate_bias = sb("gate_bias", [P, 2 * H])
        ln1 = sb("ln1", [P, DC])
        ln2 = sb("ln2", [P, DC])
        x_in = sb("x_in", [P, TILES, D])
        x_mid = sb("x_mid", [P, TILES, D])
        x_out = sb("x_out", [P, TILES, D])
        f_st = sb("f_st", [P, TILES, 6])
        f_mv = sb("f_mv", [P, 6, TILES])
        f_ve = sb("f_ve", [P, TILES])
        f_rs = sb("f_rs", [P, TILES])
        xn = sb("xn", [P, TILES, D])
        xT = sb("xT", [P, DC, BLOCK])
        xT_h, xT_l = pair("xT", [P, DC, BLOCK])
        lg = sb("lg", [P, TILES, E])
        lmax = sb("lmax", [P, TILES])
        won = sb("won", [P, TILES, E])
        won2 = sb("won2", [P, TILES, E])
        wmax = sb("wmax", [P, TILES])
        onehot = sb("onehot", [P, TILES, E])
        u_rep = sb("u_rep", [P, TILES, 3, ER])
        u_st = sb("u_st", [P, BLOCK], F32R)
        narrow = sb("narrow", [P, BLOCK])
        fT = narrow[0:H].rearrange("h (j t) -> h j t", j=TILES)
        fTz = narrow[32:32 + H].rearrange("h (j t) -> h j t", j=TILES)
        u_hi = narrow[2 * ER:LS]
        r_h = sb("r_h", [P, 2, BLOCK], F32R)
        r_l = sb("r_l", [P, 2, BLOCK], F32R)
        a_st = sb("a_st", [P, TILES, 6])
        a_mv = sb("a_mv", [P, 6, TILES])
        a_sm = sb("a_sm", [P, 6, TILES])
        z = sb("z", [P, TILES, D])
        xc = sb("xc", [P, TILES, D])
        hn = sb("hn", [P, TILES, D])
        hT_h, hT_l = pair("hT", [P, DC, BLOCK])
        q32 = sb("q32", [P, DC, BLOCK])
        pa = sb("pa", [P, DC, BLOCK], BF16)
        pb = sb("pb", [P, DC, BLOCK], BF16)
        pc = sb("pc", [P, DC, BLOCK], BF16)
        r1 = hn[:].rearrange("p (c k) d -> p c (k d)", c=DC)
        k32 = sb("k32", [P, TILES, D])
        vp = sb("vp", [P, TILES, H, HV])
        g32 = sb("g32", [P, TILES, 2 * H])
        fg = sb("fg", [P, TILES, H])
        cumT = sb("cumT", [H, TILES, P])
        decay = sb("decay", [P, TILES * H + DC * TILES])
        dm = sb("dm", [P, NQ, QUAD * P])
        arena = sb("arena", [P, 2, H * BLOCK // 4])
        qs, ks = (arena[0:STACK, n].bitcast(BF16).rearrange("k (h t) -> k h t", h=H) for n in range(2))
        pt = sb("pt", [P, 2, QUAD * P])
        wv = sb("wv", [P, H, HV])
        cb = sb("cb", [P, DC, HH * HV])
        cm = sb("cm", [P, DC, HH * HV])
        keep = sb("keep", [P, 1])
        o1 = sb("o1", [P, H, HV])
        den = sb("den", [P, 3, H])
        y = sb("y", [P, 2, D])
        yT_h, yT_l = pair("yT", [P, DC, P])
        th, gm = pt[:, 0], pt[:, 1]
        m_h = sb("m_h", [P, 2, BLOCK], F32R)
        m_l = sb("m_l", [P, 2, BLOCK], F32R)

        wo_b = y[:, 0]
        psum = [ctx.enter_context(nc.psum_tensor(f"bank{n}", [P, 512], F32)) for n in range(8)]
        T, U, A = psum[0:2], psum[2:4], psum[4:8]

        parts_d = nc.dram_tensor("parts_scratch", (2, H, 3, HD, BLOCK), BF16).ap()
        f_d = nc.dram_tensor("f_scratch", (TILES, NQ, QUAD * P), F32).ap()

        s_const = sig("const_loaded", 1, 16)
        s_early = [sig(f"early_loaded{n}", 1, 16) for n in range(5)]
        s_early_hi, s_early_lo = sig("early_hi"), sig("early_lo")
        s_late = [sig(f"late_loaded{n}", 1, 16) for n in range(2)]
        s_late_hi, s_late_lo = sig("late_hi"), sig("late_lo")
        s_setup = sig("setup_done")
        n_setup = 7
        s_xin = sig("x_loaded", 1, 16)
        s_xout = sig("x_stored", 1, 16)
        f_stats, f_mean, f_var = sig("f_stats", TILES), sig("f_mean", 6), sig("f_var")
        f_rstd, f_xn, f_xb = sig("f_rstd"), sig("f_xn", TILES), sig("f_xb")
        f_tr, f_x32, f_xh, f_xl = sig("f_tr", DC), sig("f_x32", DC), sig("f_xh", DC), sig("f_xl", DC)
        f_route, f_sel, f_u = sig("f_route"), sig("f_sel", 6), sig("f_u", 3)
        f_uT, f_uh, f_ul = sig("f_uT"), sig("f_uh", 2), sig("f_ul")
        f_up, f_rh, f_rl, f_dn = sig("f_up", FT), sig("f_rh", FT), sig("f_rl", FT), sig("f_dn", FT)
        f_mid, f_out = sig("f_mid", TILES), sig("f_out", TILES)
        a_stats, a_mean, a_small = sig("a_stats", 2 * TILES), sig("a_mean", 11), sig("a_small", 7)
        a_pow = sig("a_pow", 3)
        a_z, a_h, a_xc, a_xx = sig("a_z", TILES), sig("a_h", 2 * TILES), sig("a_xc"), sig("a_xx")
        a_tr, a_hh, a_hl = sig("a_tr", 2 * DC), sig("a_hh", 2 * DC), sig("a_hl", 2 * DC)
        a_q, a_q32 = sig("a_q", DC), sig("a_q32", DC)
        a_pa, a_r1, a_pb, a_pc = sig("a_pa", 2 * DC), sig("a_r1", 2 * DC), sig("a_pb", 2 * DC), sig("a_pc", 2 * DC)
        a_kv, a_k32, a_g, a_clip = sig("a_kv", 2 * TILES), sig("a_k32", TILES), sig("a_g", TILES), sig("a_clip", TILES)
        a_i, a_tf, a_v, a_f = sig("a_i", TILES), sig("a_tf", TILES), sig("a_v", TILES), sig("a_f", TILES)
        a_kT, a_fT, a_fTs, a_cum = sig("a_kT", DC), sig("a_fT"), sig("a_fTs", 2), sig("a_cum", TILES)
        a_dT, a_dec = sig("a_dT"), sig("a_dec")
        d_parts = sig("d_parts", 2 * 3 * DC, 16)
        d_f = sig("d_f", 1, 16)
        d_stack = sig("d_stack", 3 * LOADS, 16)
        d_fb = [sig(f"d_fb{n}", TILES, 16) for n in range(NQ)]
        a_D, a_S, a_P, a_wv, a_O = (sig(n, TILES * NQ) for n in ("a_D", "a_S", "a_P", "a_wv", "a_O"))
        a_oi, a_t1, a_o, a_den, a_y = sig("a_oi", TILES), sig("a_t1", TILES), sig("a_o", TILES), sig("a_den", 3 * TILES), sig("a_y", TILES)
        a_state, a_cm, a_cb = sig("a_state", TILES), sig("a_cm", TILES), sig("a_cb", 2 * TILES + 2)
        a_yT, a_yh, a_yl, a_wo, a_x2 = (sig(n, TILES) for n in ("a_yT", "a_yh", "a_yl", "a_wo", "a_x2"))
        a_gu, a_th, a_m1, a_m, a_mh, a_ml, a_md = sig("a_gu", 2 * IT), sig("a_th", IT), sig("a_m1", IT), sig("a_m", IT), sig("a_mh", IT), sig("a_ml", IT), sig("a_md", IT)
        a_x3 = sig("a_x3", TILES)


        woT = a["wo"].rearrange("(c p) n -> p c n", p=P)
        half_ft = FT // 2
        early = [(z, a["wi"][0:P], wi_h[:, 0], wi_l[:, 0]), (xc, a["wi"][P:D], wi_h[:, 1], wi_l[:, 1]),
                 (x_mid, a["lora"], lora_b[0:LS2], None),
                 (hn, woT[:, 0:half_ft], wo_h[:, 0:half_ft], wo_l[:, 0:half_ft]),
                 (q32, woT[:, half_ft:FT], wo_h[:, half_ft:FT], wo_l[:, half_ft:FT])]
        n_early_lo = len(early) + 1

        wgu_in = [(a["wgu"][c * P:(c + 1) * P].unsqueeze(1), wgu_h[:, c:c + 1], wgu_l[:, c:c + 1], ln2[:, c:c + 1], 1.0)
                  for c in range(DC)]
        rows_of = lambda name: a[name].rearrange("(c p) n -> p c n", p=P)
        last_rows = I - (IT - 1) * P
        late = [(rows_of("wq"), wq_h, wq_l, ln1, 1.0), (rows_of("wkv"), wkv_h, wkv_l, ln1, 1.0),
                (rows_of("wao"), wao_h, wao_l, None, 1.0), *wgu_in,
                (a["wd"][0:(IT - 1) * P].rearrange("(c p) n -> p c n", p=P), wd_h[:, 0:IT - 1], wd_l[:, 0:IT - 1], None, 0.5),
                (a["wd"][(IT - 1) * P:I].unsqueeze(1), wd_h[0:last_rows, IT - 1:IT], wd_l[0:last_rows, IT - 1:IT], None, 0.5)]

        def late_count(n):
            return sum(hi.shape[1] for _, hi, *_ in late[:n])

        def late_stage(n):
            hi = late[n][1]
            rows, c, cols = hi.shape
            return arena[0:rows, n % 2, 0:c * cols].rearrange("p (c n) -> p c n", c=c)

        consts = [(ident[:], a["ident"]), (ident4[:], a["ident4"]), (headmask[:], a["headmask"]),
                  (headsel[:], a["headsel"]), (prio[:], a["prio"]),
                  (route_w[:], a["route_w"].rearrange("(c p) n -> p c n", p=P)),
                  (route_b[:], a["route_b"].partition_broadcast(P)),
                  (wo_b, a["wo_b"].partition_broadcast(P)),
                  (gate_bias[:], a["gate_bias"].partition_broadcast(P)),
                  (ln1[:], a["ln1"]), (ln2[:], a["ln2"])]

        def flat(ap):
            return ap.rearrange("p a b -> p (a b)") if len(ap.shape) == 3 else ap

        def held(engine, value):
            return value if isinstance(value, int) else engine.snap(value)

        def schedule(engine, steps):

            def play(t, run1, run2, run_next):
                att = not isinstance(t, int) or 1 <= t <= BLOCKS
                runs = {"1": (run1, t, True), "2": (run2, t - 2, False), "n": (run_next, t + 1, True),
                        "a": (t - 1,), "m": (t,)}
                for stage, name, k in iteration(run1 is not None, run2 is not None, att, run_next is not None, run1 is not None):
                    step = steps.get(("a_" if stage in "am" else "f_") + name)
                    if step:
                        step(*runs[stage], k)
                    if isinstance(t, int) and t == -1 and "early" in steps:
                        for n in {"normal": (0, 1), "gate": (2,), "select": (3, 4)}.get(name, ()):
                            steps["early"](n)
                    if isinstance(t, int) and (t, stage, name) in ((-1, "n", "down"), (0, "1", "down")) and k < len(late):
                        if "late" in steps:
                            steps["late"](k)

            play(-1, None, None, 0)
            play(0, 0, None, 1)
            play(1, 1, None, 2)
            with engine.Fori(2, BLOCKS - 1) as t:
                play(t, t * 2 - 2, t * 2 - 1, t * 2)
            play(BLOCKS - 1, 2 * BLOCKS - 4, 2 * BLOCKS - 3, None)
            play(BLOCKS, None, 2 * BLOCKS - 2, None)
            play(BLOCKS + 1, None, 2 * BLOCKS - 1, None)

        block = ctx.enter_context(nc.Block())

        @block.sync
        def _(sp):
            def load_x(b):
                sp.dma_start(x_in[:], a["x"][bass.ds(b, 1)].rearrange("a j p d -> p (a j) d")).then_inc(s_xin.sem, 16)

            sp.dma_start(x_in[:], a["x"][0].rearrange("j p d -> p j d")).then_inc(s_xin.sem, 16)
            for n, (stage, src, hi, lo) in enumerate(early):
                dst = stage[0:hi.shape[0]]
                if len(src.shape) == 2:
                    dst = flat(dst)
                sp.dma_start(dst, src).then_inc(s_early[n].sem, 16)
                if n == 0:
                    for to, of in consts:
                        sp.dma_start(to, of).then_inc(s_const.sem, 16)
            for n, (src, hi, lo, _, _) in enumerate(late):
                sp.wait_ge(s_late_lo.sem, s_late_lo.at(0, late_count(n - 1) if n > 1 else 0))
                sp.dma_start(late_stage(n), src).then_inc(s_late[n % 2].sem, 16)

            def load(run, b, first, k):
                if isinstance(b, int) and b == 0:
                    return
                value = held(sp, f_mid.at(b - 1, TILES))
                sp.wait_ge(s_const.sem, s_const.at(len(consts), 0))
                sp.wait_ge(f_mid.sem, value)
                load_x(b)

            def fin(run, b, first, k):
                if not first:
                    value = held(sp, f_out.at(b, TILES))
                    sp.wait_ge(s_const.sem, s_const.at(len(consts), 0))
                    sp.wait_ge(f_out.sem, value)
                    sp.dma_start(out[bass.ds(b, 1)].rearrange("a j p d -> p (a j) d"), x_out[:]).then_inc(s_xout.sem, 16)

            def store_parts(b, u, parts):
                for n in parts:
                    sem, part = ((a_pa, pa), (a_pb, pb), (a_pc, pc))[n]
                    sp.wait_ge(sem.sem, sem.at(b, DC * (u + 1)))
                    for m in range(DC):
                        sp.dma_start(parts_d[u, m * HH:(m + 1) * HH, n], part[:, m]).then_inc(d_parts.sem, 16)

            def q(b, m):
                if m == DC - 1:
                    store_parts(b, 0, (0, 1, 2))

            def kT(b, k):
                store_parts(b, 1, (0,))

            def load_slots(u, j):
                tokens = slice(j * P, (j + 1 if j else 2) * P)
                to = slice(j % 2 * P, (j % 2 + 1 if j else 2) * P)
                slot = 0
                for first, last in SLOT_RUNS[u]:
                    rows = slice(slot * HD, (slot + last - first) * HD)
                    src = parts_d[u, :, first:last].rearrange("h n e t -> (n e) h t")
                    sp.dma_start((qs, ks)[u][rows, :, to], src[:, :, tokens]).then_inc(d_stack.sem, 16)
                    slot += last - first

            def load_stack(b, j):
                value = held(sp, d_parts.at(b, (2 if j else 1) * 3 * DC))
                sp.wait_ge(s_const.sem, s_const.at(len(consts), 0))
                sp.wait_ge(d_parts.sem, value)
                if j:
                    sp.wait_ge(a_S.sem, a_S.at(b, (j - 1) * NQ))
                    load_slots(0, j)
                    load_slots(1, j)
                else:
                    sp.wait_ge(a_S.sem, a_S.at(b - 1, TILES * NQ))
                    load_slots(0, 0)

            def load_stack_k(b, j):
                value = held(sp, d_parts.at(b, 2 * 3 * DC))
                sp.wait_ge(s_const.sem, s_const.at(len(consts), 0))
                sp.wait_ge(d_parts.sem, value)
                load_slots(1, 0)

            def load_f(b, u):
                j, g = divmod(u, NQ)
                value = held(sp, d_f.at(b, 1))
                sp.wait_ge(s_const.sem, s_const.at(len(consts), 0))
                sp.wait_ge(d_f.sem, value)
                sp.wait_ge(a_P.sem, a_P.at(b, u - NQ + 1))
                sp.wait_ge(a_wv.sem, a_wv.at(b, u - NQ + 1))
                sp.dma_start(dm[:, g], f_d[j, g].partition_broadcast(P)).then_inc(d_fb[g].sem, 16)

            def fT_(b, k):
                sp.wait_ge(a_fTs.sem, a_fTs.at(b, 1))
                for g in range(NQ):
                    sp.wait_ge(d_fb[g].sem, d_fb[g].at(b - 1, TILES))
                sp.dma_start(f_d.rearrange("j g (h t) -> (g h) j t", h=QUAD), fTz[:]).then_inc(d_f.sem, 16)

            def k2(b, k):
                store_parts(b, 1, (1, 2))
                for u in range(NQ):
                    load_f(b, u)

            def mix(b, u):
                if u + NQ < TILES * NQ:
                    load_f(b, u + NQ)

            schedule(sp, {"f_load": load, "f_fin": fin, "a_q": q, "a_kT": kT, "a_fT": fT_, "a_k2": k2, "a_stack": load_stack, "a_stack_k": load_stack_k, "a_mix": mix})
            sp.wait_ge(s_xout.sem, s_xout.at(BLOCKS, 0))

        @block.gpsimd
        def _(pool):
            nc.gpsimd.memset(minus_half[:], -0.5).then_inc(s_setup.sem, 1)

            def stats(run, b, first, k):
                if isinstance(run, int) and run == 0:
                    pool.wait_ge(s_setup.sem, s_setup.at(n_setup, 0))
                pool.wait_ge(f_var.sem, f_var.at(run, 1))
                nc.gpsimd.tensor_tensor(f_rs[:], f_ve[:], minus_half[:], ALU.pow).then_inc(f_rstd.sem, 1)

            def lora(run, b, first, k):
                pool.wait_ge(f_xn.sem, f_xn.at(run, TILES))
                x = x_in if first else x_out
                bias = half_wo_b[:].unsqueeze(1).to_broadcast([P, TILES, D])
                nc.gpsimd.tensor_tensor(x[:], x[:], bias, ALU.add).then_inc(f_xb.sem, 1)

            def tr(run, b, first, k):
                pool.wait_ge(f_route.sem, f_route.at(run - 1, 1))
                for c in range(DC):
                    pool.wait_ge(f_xh.sem, f_xh.at(run, c + 1))
                    pool.wait_ge(f_xl.sem, f_xl.at(run, c + 1))
                    nc.gpsimd.tensor_tensor(xT[:, c], xT_h[:, c].bitcast(F32), xT_l[:, c].bitcast(F32), ALU.add
                                            ).then_inc(f_x32.sem, 1)

            def astats(b, k):
                pool.wait_ge(a_small.sem, a_small.at(b, 1))
                nc.gpsimd.tensor_tensor(a_sm[:, 1], a_sm[:, 0], minus_half[:], ALU.pow).then_inc(a_pow.sem, 1)

            def az(b, k):
                pool.wait_ge(a_small.sem, a_small.at(b, 6))
                nc.gpsimd.tensor_tensor(a_sm[:, 2], a_sm[:, 0], minus_half[:], ALU.pow).then_inc(a_pow.sem, 1)

            def split(b, u):
                for m in range(DC):
                    n = DC * u + m
                    pool.wait_ge(a_pb.sem, a_pb.at(b, n + 1))
                    nc.gpsimd.tensor_tensor(pc[:, m], r1[:, m], pb[:, m], ALU.subtract).then_inc(a_pc.sem, 1)

            def mix(b, u):
                j, g = divmod(u, NQ)
                pool.wait_ge(a_D.sem, a_D.at(b, u + 1))
                if j:
                    pool.wait_ge(a_state.sem, a_state.at(b, j))
                else:
                    pool.wait_ge(a_state.sem, a_state.at(b - 1, TILES))
                w = dm[:, g].rearrange("p (h t) -> p h t", h=QUAD)[:, :, P - 1:P].to_broadcast([P, QUAD, HV])
                heads = slice(QUAD * g, QUAD * (g + 1))
                pool.wait_ge(a_v.sem, a_v.at(b, j + 1))
                nc.gpsimd.tensor_tensor(wv[:, heads], vp[:, j, heads], w, ALU.mult).then_inc(a_wv.sem, 1)

            def aln2(b, k):
                pool.wait_ge(a_x2.sem, a_x2.at(b, TILES))
                pool.wait_ge(a_small.sem, a_small.at(b, 7))
                nc.gpsimd.tensor_tensor(a_sm[:, 4], a_sm[:, 3], minus_half[:], ALU.pow).then_inc(a_pow.sem, 1)
                pool.wait_ge(a_xc.sem, a_xc.at(b, 1))
                nc.gpsimd.tensor_tensor(xc[:], xc[:], z[:], ALU.add).then_inc(a_xx.sem, 1)

            def gu(b, i):
                rows = P if i < IT - 1 else last_rows
                pool.wait_ge(a_mh.sem, a_mh.at(b, i + 1))
                if i > 1:
                    pool.wait_ge(a_md.sem, a_md.at(b, i - 1))
                nc.gpsimd.tensor_tensor(m_l[:rows, i % 2], gm[:rows], m_h[:rows, i % 2].bitcast(F32), ALU.subtract
                                        ).then_inc(a_ml.sem, 1)

            schedule(pool, {"f_stats": stats, "f_lora": lora, "f_tr": tr, "a_stats": astats, "a_z": az, "a_q": lambda b, m: split(b, 0) if m else None,
                            "a_k2": lambda b, k: split(b, 1), "a_mix": mix, "a_ln2": aln2, "a_gu": gu})

        @block.scalar
        def _(act):
            act.wait_ge(s_const.sem, s_const.at(len(consts), 0))
            nc.scalar.mul(half_wo_b[:], wo_b, 0.5).then_inc(s_setup.sem, 1)

            def early_hi(n):
                stage, src, hi, lo = early[n]
                act.wait_ge(s_early[n].sem, s_early[n].at(1, 0))
                nc.scalar.copy(flat(hi), flat(stage[0:hi.shape[0]])).then_inc(s_early_hi.sem, 1)
                if lo is None:
                    act.wait_ge(s_early_lo.sem, s_early_lo.at(n + 1, 0))
                    nc.scalar.copy(hi[LS:LS + 1], flat(stage[LS:LS + 1])).then_inc(s_early_hi.sem, 1)

            def late_hi(n):
                src, hi, lo, factors, const = late[n]
                act.wait_ge(s_early_lo.sem, s_early_lo.at(n_early_lo, 0))
                act.wait_ge(s_late[n % 2].sem, s_late[n % 2].at(n // 2 + 1, 0))
                for c in range(hi.shape[1]):
                    nc.scalar.activation(hi[:, c], late_stage(n)[:, c], ACT.Copy, scale=const if factors is None else factors[:, c:c + 1]
                                         ).then_inc(s_late_hi.sem, 1)

            def tr(run, b, first, k):
                for c in range(DC):
                    act.wait_ge(f_tr.sem, f_tr.at(run, c + 1))
                    act.wait_ge(f_up.sem, f_up.at(run - 1, FT))
                    nc.scalar.copy(xT_h[:, c], U[c][:]).then_inc(f_xh.sem, 1)

            def lora(run, b, first, k):
                act.wait_ge(f_uT.sem, f_uT.at(run, 1))
                nc.scalar.copy(u_st[0:2 * ER], T[1][0:2 * ER]).then_inc(f_uh.sem, 1)
                act.wait_ge(f_ul.sem, f_ul.at(run - 1, 1))
                nc.scalar.copy(u_hi.bitcast(F32R), T[1][2 * ER:LS]).then_inc(f_uh.sem, 1)

            def relu(run, b, first, f):
                act.wait_ge(f_up.sem, f_up.at(run, f + 1))
                act.wait_ge(f_dn.sem, f_dn.at(run, f - 1))
                nc.scalar.activation(r_h[:, f % 2], U[f % 2][:], ACT.Relu).then_inc(f_rh.sem, 1)

            def atr(b, k):
                for c in range(DC):
                    act.wait_ge(a_tr.sem, a_tr.at(b, c + 1))
                    act.wait_ge(a_gu.sem, a_gu.at(b - 1, 2 * IT))
                    nc.scalar.copy(hT_h[:, c], T[c][:]).then_inc(a_hh.sem, 1)

            def acopy(b, k):
                act.wait_ge(a_x3.sem, a_x3.at(b - 1, TILES))
                act.wait_ge(f_mid.sem, f_mid.at(b, TILES))
                nc.scalar.copy(xc[:], x_mid[:]).then_inc(a_xc.sem, 1)

            def atr2(b, k):
                for c in range(DC):
                    act.wait_ge(a_tr.sem, a_tr.at(b, DC + c + 1))
                    act.wait_ge(a_kv.sem, a_kv.at(b, 2 * TILES))
                    nc.scalar.copy(hT_h[:, c], A[c][:]).then_inc(a_hh.sem, 1)

            def q(b, m):
                act.wait_ge(a_q.sem, a_q.at(b, m + 1))
                act.wait_ge(a_oi.sem, a_oi.at(b - 1, TILES))
                nc.scalar.copy(q32[:, m], A[2 + m][:]).then_inc(a_q32.sem, 1)
                act.wait_ge(d_parts.sem, d_parts.at(b - 1, 6 * DC))
                nc.scalar.copy(pa[:, m], A[2 + m][:]).then_inc(a_pa.sem, 1)
                second_part(b, m)

            def second_part(b, n):
                act.wait_ge(a_r1.sem, a_r1.at(b, n + 1))
                nc.scalar.copy(pb[:, n % DC], r1[:, n % DC]).then_inc(a_pb.sem, 1)

            def kv(b, j):
                act.wait_ge(a_kv.sem, a_kv.at(b, 2 * j + 1))
                act.wait_ge(a_state.sem, a_state.at(b - 1, TILES))
                nc.scalar.copy(k32[:, j], A[0][:, 0:D]).then_inc(a_k32.sem, 1)
                act.wait_ge(a_clip.sem, a_clip.at(b, j + 1))
                act.wait_ge(a_wv.sem, a_wv.at(b - 1, TILES * NQ))
                act.wait_ge(a_O.sem, a_O.at(b - 1, TILES * NQ))
                nc.scalar.activation(vp[:, j, :, HD], g32[:, j, 0:H], ACT.Exp).then_inc(a_i.sem, 1)
                nc.scalar.activation(fg[:, j], g32[:, j, H:2 * H], ACT.Tanh, scale=0.5).then_inc(a_tf.sem, 1)

            def kT(b, k):
                act.wait_ge(d_parts.sem, d_parts.at(b, 3 * DC))
                for m in range(DC):
                    act.wait_ge(a_kT.sem, a_kT.at(b, m + 1))
                    nc.scalar.copy(pa[:, m], A[2 + m][:]).then_inc(a_pa.sem, 1)

            def k2(b, k):
                for m in range(DC):
                    second_part(b, DC + m)

            def fT_(b, k):
                act.wait_ge(a_fT.sem, a_fT.at(b, 1))
                act.wait_ge(d_f.sem, d_f.at(b - 1, 1))
                src = A[0][0:H].rearrange("h (j t) -> h j t", j=TILES)
                nc.scalar.copy(fTz[:, :, 1:P], src[:, :, 1:P]).then_inc(a_fTs.sem, 1)
                nc.scalar.copy(fT[:], src).then_inc(a_fTs.sem, 1)

            def dec(b, k):
                act.wait_ge(a_dT.sem, a_dT.at(b, 1))
                act.wait_ge(a_cb.sem, a_cb.at(b, 0))
                nc.scalar.copy(decay[:], A[1][:, 0:TILES * H + DC * TILES]).then_inc(a_dec.sem, 1)

            def yT_(b, j):
                act.wait_ge(a_yT.sem, a_yT.at(b, j + 1))
                if j:
                    act.wait_ge(a_wo.sem, a_wo.at(b, j))
                else:
                    act.wait_ge(a_wo.sem, a_wo.at(b - 1, TILES))
                nc.scalar.copy(flat(yT_h[:]), A[0][:, 0:D]).then_inc(a_yh.sem, 1)

            def gu(b, i):
                rows = P if i < IT - 1 else last_rows
                act.wait_ge(a_gu.sem, a_gu.at(b, 2 * i + 1))
                nc.scalar.activation(th[:rows], A[2][:rows], ACT.Tanh, scale=0.5).then_inc(a_th.sem, 1)
                act.wait_ge(a_m.sem, a_m.at(b, i + 1))
                if i > 1:
                    act.wait_ge(a_md.sem, a_md.at(b, i - 1))
                nc.scalar.copy(m_h[:rows, i % 2], gm[:rows]).then_inc(a_mh.sem, 1)

            schedule(act, {"early": early_hi, "late": late_hi, "f_tr": tr, "a_copy": acopy, "f_lora": lora, "f_act": relu, "a_tr": atr, "a_q": q, "a_kv": kv, "a_kT": kT,
                           "a_k2": k2, "a_fT": fT_, "a_decay": dec, "a_yT": yT_, "a_tr2": atr2, "a_gu": gu})

        @block.vector
        def _(dve):
            v = nc.vector
            v.memset(cb[:], 0.0).then_inc(s_setup.sem, 1)
            v.memset(keep[:], 1.0).then_inc(s_setup.sem, 1)
            v.memset(zeros[:], 0.0).then_inc(s_setup.sem, 1)
            v.memset(fTz[:], 0.0).then_inc(s_setup.sem, 1)
            v.memset(u_st[LS:P].bitcast(F32), 1.0).then_inc(s_setup.sem, 1)

            def early_lo(n):
                stage, src, hi, lo = early[n]
                s = flat(stage[0:hi.shape[0]])
                dve.wait_ge(s_early[n].sem, s_early[n].at(1, 0))
                dve.wait_ge(s_early_hi.sem, s_early_hi.at(n + 1 + (n > 2), 0))
                if lo is not None:
                    v.tensor_tensor(flat(lo), s, flat(hi).bitcast(F32), ALU.subtract).then_inc(s_early_lo.sem, 1)
                else:
                    v.tensor_tensor(hi[LS:LS2], s[LS:LS2], hi[LS:LS2].bitcast(F32), ALU.subtract).then_inc(s_early_lo.sem, 1)
                    v.tensor_tensor(hi[ER:2 * ER], s[ER:2 * ER], hi[ER:2 * ER].bitcast(F32), ALU.subtract
                                    ).then_inc(s_early_lo.sem, 1)

            def late_lo(n):
                src, hi, lo, factors, const = late[n]
                dve.wait_ge(s_late[n % 2].sem, s_late[n % 2].at(n // 2 + 1, 0))
                for c in range(hi.shape[1]):
                    dve.wait_ge(s_late_hi.sem, s_late_hi.at(late_count(n) + c + 1, 0))
                    v.scalar_tensor_tensor(lo[:, c], late_stage(n)[:, c], const if factors is None else factors[:, c:c + 1],
                                           hi[:, c].bitcast(F32), ALU.mult, ALU.subtract).then_inc(s_late_lo.sem, 1)

            def moments(st, mv, done, run, before, eps):
                means, squares = (st[:, :, 1], st[:, :, 4]), (st[:, :, 2], st[:, :, 5])
                v.tensor_tensor(mv[:, 0], *means, ALU.add).then_inc(done.sem, 1)
                v.tensor_tensor(mv[:, 1], *means, ALU.subtract).then_inc(done.sem, 1)
                v.tensor_tensor(mv[:, 2], *squares, ALU.add).then_inc(done.sem, 1)
                dve.wait_ge(done.sem, done.at(run, before + 1))
                v.tensor_scalar(mv[:, 3], mv[:, 0], 0.5, None, ALU.mult).then_inc(done.sem, 1)
                dve.wait_ge(done.sem, done.at(run, before + 2))
                v.tensor_tensor(mv[:, 4], mv[:, 1], mv[:, 1], ALU.mult).then_inc(done.sem, 1)
                dve.wait_ge(done.sem, done.at(run, before + 3))
                v.tensor_scalar(mv[:, 5], mv[:, 2], 1.0 / D, eps, ALU.mult, ALU.add).then_inc(done.sem, 1)
                dve.wait_ge(done.sem, done.at(run, before + 6))

            def stats(run, b, first, k):
                if first:
                    dve.wait_ge(s_xin.sem, s_xin.at(b, 1))
                    x = x_in
                else:
                    dve.wait_ge(a_x3.sem, a_x3.at(b, TILES))
                    x = x_out
                for j in range(TILES):
                    v.bn_stats(f_st[:, j], x[:, j]).then_inc(f_stats.sem, 1)
                dve.wait_ge(f_stats.sem, f_stats.at(run, TILES))
                moments(f_st, f_mv, f_mean, run, 0, 1e-5)
                v.scalar_tensor_tensor(f_ve[:], f_mv[:, 4], 0.25, f_mv[:, 5], ALU.mult, ALU.add).then_inc(f_var.sem, 1)

            def normal(run, b, first, k):
                x = x_in if first else x_out
                dve.wait_ge(f_rstd.sem, f_rstd.at(run, 1))
                dve.wait_ge(f_tr.sem, f_tr.at(run - 1, DC))
                for j in range(TILES):
                    v.tensor_scalar(xn[:, j], x[:, j], f_mv[:, 3, j:j + 1], f_rs[:, j:j + 1], ALU.subtract, ALU.mult
                                    ).then_inc(f_xn.sem, 1)

            def tr(run, b, first, k):
                for c in range(DC):
                    dve.wait_ge(f_xh.sem, f_xh.at(run, c + 1))
                    v.tensor_tensor(xT_l[:, c], U[c][:], xT_h[:, c].bitcast(F32), ALU.subtract).then_inc(f_xl.sem, 1)

            def gate(run, b, first, k):
                dve.wait_ge(f_route.sem, f_route.at(run, 1))
                routed = T[0][:, 0:TILES * GW].rearrange("p (j n) -> p j n", j=TILES)
                each = lambda t: t[:].unsqueeze(2).to_broadcast([P, TILES, E])
                v.tensor_tensor(lg[:], routed[:, :, 0:E], route_b[:].unsqueeze(1).to_broadcast([P, TILES, E]), ALU.add
                                ).then_inc(f_sel.sem, 1)
                dve.wait_ge(f_sel.sem, f_sel.at(run, 1))
                v.tensor_reduce(lmax[:], lg[:], AX_X, ALU.max).then_inc(f_sel.sem, 1)
                dve.wait_ge(f_sel.sem, f_sel.at(run, 2))
                v.tensor_tensor(won[:], lg[:], each(lmax), ALU.is_ge).then_inc(f_sel.sem, 1)
                dve.wait_ge(f_sel.sem, f_sel.at(run, 3))
                v.tensor_tensor(won2[:], won[:], prio[:], ALU.mult).then_inc(f_sel.sem, 1)
                dve.wait_ge(f_sel.sem, f_sel.at(run, 4))
                v.tensor_reduce(wmax[:], won2[:], AX_X, ALU.max).then_inc(f_sel.sem, 1)
                dve.wait_ge(f_sel.sem, f_sel.at(run, 5))
                v.tensor_tensor(onehot[:], won2[:], each(wmax), ALU.is_equal).then_inc(f_sel.sem, 1)
                dve.wait_ge(f_sel.sem, f_sel.at(run, 6))
                dve.wait_ge(f_uT.sem, f_uT.at(run - 1, 1))
                for n in range(3):
                    v.tensor_tensor(u_rep[:, :, n].rearrange("p j (e r) -> p j e r", e=E),
                                    routed[:, :, E:GW].rearrange("p j (e r) -> p j e r", e=E),
                                    onehot[:].unsqueeze(3).to_broadcast([P, TILES, E, R]), ALU.mult).then_inc(f_u.sem, 1)

            def lora(run, b, first, k):
                dve.wait_ge(f_uh.sem, f_uh.at(run, 2))
                v.tensor_tensor(u_st[2 * ER:LS], T[1][2 * ER:LS], u_hi, ALU.subtract).then_inc(f_ul.sem, 1)

            def relu(run, b, first, f):
                dve.wait_ge(f_rh.sem, f_rh.at(run, f + 1))
                dve.wait_ge(f_dn.sem, f_dn.at(run, f - 1))
                v.scalar_tensor_tensor(r_l[:, f % 2], U[f % 2][:], 0.0, r_h[:, f % 2].bitcast(F32), ALU.max, ALU.subtract
                                       ).then_inc(f_rl.sem, 1)

            def fin(run, b, first, k):
                dve.wait_ge(f_dn.sem, f_dn.at(run, FT))
                dve.wait_ge(f_xb.sem, f_xb.at(run, 1))
                if first:
                    dve.wait_ge(a_xc.sem, a_xc.at(b - 1, 1))
                x, to = (x_in, x_mid) if first else (x_out, x_out)
                for j in range(TILES):
                    v.scalar_tensor_tensor(to[:, j], T[j // 2][:, (j % 2) * D:(j % 2 + 1) * D], 0.5, x[:, j],
                                           ALU.mult, ALU.add).then_inc((f_mid if first else f_out).sem, 1)

            def astats(b, k):
                dve.wait_ge(f_mid.sem, f_mid.at(b, TILES))
                for j in range(TILES):
                    v.bn_stats(a_st[:, j], x_mid[:, j]).then_inc(a_stats.sem, 1)
                dve.wait_ge(a_stats.sem, a_stats.at(b, TILES))
                moments(a_st, a_mv, a_mean, b, 0, 1e-5)
                v.scalar_tensor_tensor(a_sm[:, 0], a_mv[:, 4], 0.25, a_mv[:, 5], ALU.mult, ALU.add).then_inc(a_small.sem, 1)
                v.tensor_scalar(a_sm[:, 5], a_mv[:, 2], 1.0 / D, None, ALU.mult).then_inc(a_small.sem, 1)
                dve.wait_ge(a_small.sem, a_small.at(b, 2))
                v.scalar_tensor_tensor(a_sm[:, 5], a_mv[:, 4], 0.25, a_sm[:, 5], ALU.mult, ALU.add).then_inc(a_small.sem, 1)

            def az(b, k):
                dve.wait_ge(a_pow.sem, a_pow.at(b, 1))
                dve.wait_ge(a_xx.sem, a_xx.at(b - 1, 1))
                v.tensor_tensor(a_sm[:, 3], a_sm[:, 1], a_sm[:, 1], ALU.mult).then_inc(a_small.sem, 1)
                for j in range(TILES):
                    v.tensor_scalar(z[:, j], x_mid[:, j], a_mv[:, 3, j:j + 1], a_sm[:, 1, j:j + 1], ALU.subtract, ALU.mult
                                    ).then_inc(a_z.sem, 1)
                dve.wait_ge(a_small.sem, a_small.at(b, 4))
                v.tensor_tensor(a_sm[:, 3], a_sm[:, 3], a_sm[:, 5], ALU.mult).then_inc(a_small.sem, 1)
                dve.wait_ge(a_small.sem, a_small.at(b, 5))
                v.tensor_scalar(a_sm[:, 0], a_sm[:, 3], 1e-6, None, ALU.add).then_inc(a_small.sem, 1)

            def anormal(b, k):
                dve.wait_ge(a_pow.sem, a_pow.at(b, 2))
                dve.wait_ge(a_tr.sem, a_tr.at(b, 0))
                for j in range(TILES):
                    dve.wait_ge(a_z.sem, a_z.at(b, j + 1))
                    v.tensor_scalar(hn[:, j], z[:, j], a_sm[:, 2, j:j + 1], None, ALU.mult).then_inc(a_h.sem, 1)

            def atr(b, k):
                for c in range(DC):
                    dve.wait_ge(a_hh.sem, a_hh.at(b, c + 1))
                    v.tensor_tensor(hT_l[:, c], T[c][:], hT_h[:, c].bitcast(F32), ALU.subtract).then_inc(a_hl.sem, 1)

            def atr2(b, k):
                for c in range(DC):
                    dve.wait_ge(a_hh.sem, a_hh.at(b, DC + c + 1))
                    v.tensor_tensor(hT_l[:, c], A[c][:], hT_h[:, c].bitcast(F32), ALU.subtract).then_inc(a_hl.sem, 1)

            def q(b, m):
                dve.wait_ge(a_pa.sem, a_pa.at(b, m + 1))
                dve.wait_ge(a_pc.sem, a_pc.at(b, 0))
                v.tensor_tensor(r1[:, m], A[2 + m][:], pa[:, m], ALU.subtract).then_inc(a_r1.sem, 1)

            def kv(b, j):
                dve.wait_ge(a_k32.sem, a_k32.at(b, j + 1))
                dve.wait_ge(a_tf.sem, a_tf.at(b, 0))
                v.tensor_tensor(g32[:, j], A[0][:, D:D + 2 * H], gate_bias[:], ALU.add).then_inc(a_g.sem, 1)
                dve.wait_ge(a_g.sem, a_g.at(b, j + 1))
                v.tensor_scalar(g32[:, j, 0:H], g32[:, j, 0:H], -10.0, 10.0, ALU.max, ALU.min).then_inc(a_clip.sem, 1)
                dve.wait_ge(a_i.sem, a_i.at(b, j + 1))
                dve.wait_ge(a_kv.sem, a_kv.at(b, 2 * j + 2))
                v.tensor_tensor(vp[:, j, :, 0:HD], A[1][:, 0:D].rearrange("p (h d) -> p h d", h=H),
                                vp[:, j, :, HD:HV].to_broadcast([P, H, HD]), ALU.mult).then_inc(a_v.sem, 1)
                dve.wait_ge(a_tf.sem, a_tf.at(b, j + 1))
                v.tensor_scalar(fg[:, j], fg[:, j], 0.5, 0.5, ALU.mult, ALU.add).then_inc(a_f.sem, 1)

            def kT(b, k):
                for m in range(DC):
                    dve.wait_ge(a_pa.sem, a_pa.at(b, DC + m + 1))
                    dve.wait_ge(a_pc.sem, a_pc.at(b, m + 1))
                    v.tensor_tensor(r1[:, m], A[2 + m][:], pa[:, m], ALU.subtract).then_inc(a_r1.sem, 1)

            def fT_(b, k):
                dve.wait_ge(a_fTs.sem, a_fTs.at(b, 2))
                dve.wait_ge(a_dT.sem, a_dT.at(b, 0))
                for j in range(TILES):
                    v.tensor_tensor_scan(cumT[:, j], fT[:, j], zeros[:], 1.0, ALU.mult, ALU.add).then_inc(a_cum.sem, 1)

            def scan(b, u):
                j, g = divmod(u, NQ)
                dve.wait_ge(d_fb[g].sem, d_fb[g].at(b, j + 1))
                v.tensor_tensor_scan(dm[:, g], dm[:, g], ident4[:], 0.0, ALU.mult, ALU.add).then_inc(a_D.sem, 1)

            def score(b, u):
                g = u % NQ
                dve.wait_ge(a_D.sem, a_D.at(b, u + 1))
                dve.wait_ge(a_S.sem, a_S.at(b, u + 1))
                dve.wait_ge(a_O.sem, a_O.at(b, u - 1))
                v.tensor_tensor(pt[:, u % 2], A[2 + u % 2][:], dm[:, g], ALU.mult).then_inc(a_P.sem, 1)

            heads = lambda bank: bank[:, 0:H * HV].rearrange("p (h d) -> p h d", h=H)

            def carry(b, j):
                dve.wait_ge(a_oi.sem, a_oi.at(b, j + 1))
                cum = decay[:, j * H:(j + 1) * H].unsqueeze(2).to_broadcast([P, H, HV])
                v.tensor_tensor(o1[:], heads(A[1]), cum, ALU.mult).then_inc(a_t1.sem, 1)

            def sum_(b, j):
                dve.wait_ge(a_t1.sem, a_t1.at(b, j + 1))
                dve.wait_ge(a_O.sem, a_O.at(b, NQ * (j + 1)))
                v.tensor_tensor(o1[:], heads(A[0]), o1[:], ALU.add).then_inc(a_o.sem, 1)
                dve.wait_ge(a_o.sem, a_o.at(b, j + 1))
                v.tensor_scalar(den[:, 0], o1[:, :, HD], 1.0, None, ALU.max).then_inc(a_den.sem, 1)
                dve.wait_ge(a_den.sem, a_den.at(b, 3 * j + 1))
                v.scalar_tensor_tensor(den[:, 1], o1[:, :, HD], -1.0, den[:, 0], ALU.mult, ALU.max).then_inc(a_den.sem, 1)
                dve.wait_ge(a_den.sem, a_den.at(b, 3 * j + 2))
                v.reciprocal(den[:, 2], den[:, 1]).then_inc(a_den.sem, 1)
                dve.wait_ge(a_den.sem, a_den.at(b, 3 * j + 3))
                if j > 1:
                    dve.wait_ge(a_yT.sem, a_yT.at(b, j - 1))
                else:
                    dve.wait_ge(a_yT.sem, a_yT.at(b, 0))
                v.tensor_tensor(y[:, j % 2].rearrange("p (h d) -> p h d", h=H), o1[:, :, 0:HD],
                                den[:, 2].unsqueeze(2).to_broadcast([P, H, HD]), ALU.mult).then_inc(a_y.sem, 1)

            def state(b, j):
                dve.wait_ge(a_state.sem, a_state.at(b, j + 1))
                v.tensor_tensor(flat(cm[:]), A[1][:, 0:DC * HH * HV], headmask[:], ALU.mult).then_inc(a_cm.sem, 1)
                dve.wait_ge(a_cm.sem, a_cm.at(b, j + 1))
                for m in range(DC):
                    last = TILES * H + m * TILES + j
                    v.scalar_tensor_tensor(cb[:, m], cb[:, m], decay[:, last:last + 1], cm[:, m], ALU.mult, ALU.add
                                           ).then_inc(a_cb.sem, 1)
                dve.wait_ge(a_cb.sem, a_cb.at(b, 2 * j + 2))
                if j == TILES - 1:
                    v.tensor_scalar(flat(cb[:]), flat(cb[:]), keep[:, 0:1], None, ALU.mult).then_inc(a_cb.sem, 1)
                    v.tensor_scalar(keep[:], keep[:], -1.0, 1.0, ALU.mult, ALU.add).then_inc(a_cb.sem, 1)

            def yT_(b, j):
                dve.wait_ge(a_yh.sem, a_yh.at(b, j + 1))
                v.tensor_tensor(flat(yT_l[:]), A[0][:, 0:D], flat(yT_h[:]).bitcast(F32), ALU.subtract).then_inc(a_yl.sem, 1)

            def wo(b, j):
                dve.wait_ge(a_wo.sem, a_wo.at(b, j + 1))
                v.tensor_tensor(z[:, j], A[0][:, D:2 * D], z[:, j], ALU.add).then_inc(a_x2.sem, 1)
                dve.wait_ge(a_x2.sem, a_x2.at(b, j + 1))
                v.bn_stats(a_st[:, j], z[:, j]).then_inc(a_stats.sem, 1)

            def aln2(b, k):
                dve.wait_ge(a_stats.sem, a_stats.at(b, 2 * TILES))
                even, odd = a_st[:, :, 1], a_st[:, :, 4]
                v.tensor_tensor(a_mv[:, 0], even, even, ALU.mult).then_inc(a_mean.sem, 1)
                v.tensor_tensor(a_mv[:, 1], odd, odd, ALU.mult).then_inc(a_mean.sem, 1)
                v.tensor_tensor(a_mv[:, 2], a_st[:, :, 2], a_st[:, :, 5], ALU.add).then_inc(a_mean.sem, 1)
                dve.wait_ge(a_mean.sem, a_mean.at(b, 8))
                v.tensor_tensor(a_mv[:, 3], a_mv[:, 0], a_mv[:, 1], ALU.add).then_inc(a_mean.sem, 1)
                dve.wait_ge(a_mean.sem, a_mean.at(b, 9))
                v.tensor_scalar(a_mv[:, 5], a_mv[:, 2], 1.0 / D, 1e-6, ALU.mult, ALU.add).then_inc(a_mean.sem, 1)
                dve.wait_ge(a_mean.sem, a_mean.at(b, 11))
                v.scalar_tensor_tensor(a_sm[:, 3], a_mv[:, 3], 0.5, a_mv[:, 5], ALU.mult, ALU.add).then_inc(a_small.sem, 1)

            def normal2(b, k):
                dve.wait_ge(a_pow.sem, a_pow.at(b, 3))
                dve.wait_ge(a_tr.sem, a_tr.at(b, DC))
                dve.wait_ge(a_pc.sem, a_pc.at(b, 2 * DC))
                for j in range(TILES):
                    v.tensor_scalar(hn[:, j], z[:, j], a_sm[:, 4, j:j + 1], None, ALU.mult).then_inc(a_h.sem, 1)

            def gu(b, i):
                rows = P if i < IT - 1 else last_rows
                dve.wait_ge(a_th.sem, a_th.at(b, i + 1))
                dve.wait_ge(a_ml.sem, a_ml.at(b, i))
                v.scalar_tensor_tensor(gm[:rows], th[:rows], 1.0, A[2][:rows], ALU.add, ALU.mult).then_inc(a_m1.sem, 1)
                dve.wait_ge(a_m1.sem, a_m1.at(b, i + 1))
                dve.wait_ge(a_gu.sem, a_gu.at(b, 2 * i + 2))
                v.tensor_tensor(gm[:rows], A[3][:rows], gm[:rows], ALU.mult).then_inc(a_m.sem, 1)

            def mfin(b, k):
                dve.wait_ge(a_md.sem, a_md.at(b, IT))
                dve.wait_ge(a_xx.sem, a_xx.at(b, 1))
                dve.wait_ge(s_xout.sem, s_xout.at(b, 0))
                for j in range(TILES):
                    v.tensor_tensor(x_out[:, j], A[j // 2][:, (j % 2) * D:(j % 2 + 1) * D], xc[:, j], ALU.add
                                    ).then_inc(a_x3.sem, 1)

            dve.wait_ge(s_setup.sem, s_setup.at(n_setup, 0))
            dve.wait_ge(s_const.sem, s_const.at(len(consts), 0))
            schedule(dve, {"early": early_lo, "late": late_lo, "f_stats": stats, "f_normal": normal, "f_tr": tr, "f_select": gate, "f_lora": lora,
                           "f_act": relu, "f_fin": fin, "a_stats": astats, "a_z": az, "a_normal": anormal, "a_tr": atr, "a_q": q, "a_kv": kv, "a_kT": kT, "a_fT": fT_,
                           "a_scan": scan, "a_score": score, "a_carry": carry, "a_sum": sum_, "a_state": state, "a_yT": yT_,
                           "a_wo": wo, "a_ln2": aln2,
                           "a_normal2": normal2, "a_tr2": atr2, "a_gu": gu, "a_mfin": mfin})

        @block.tensor
        def _(pe):
            def product(dst, left, right, first=True, last=True, **more):
                (lh, ll), (rh, rl) = left, right
                nc.tensor.matmul(dst, lh, rh, start=first, stop=False, **more)
                nc.tensor.matmul(dst, ll, rh, start=False, stop=False, **more)
                return nc.tensor.matmul(dst, lh, rl, start=False, stop=last, **more)

            def tiles(j):
                return slice((j % 2) * D, (j % 2 + 1) * D)

            def tr(run, b, first, k):
                pe.wait_ge(f_rl.sem, f_rl.at(run - 1, FT))
                for c in range(DC):
                    for j in range(TILES):
                        pe.wait_ge(f_xn.sem, f_xn.at(run, j + 1))
                        done = nc.tensor.transpose(U[c][:, j * P:(j + 1) * P], xn[:, j, c * P:(c + 1) * P], ident[:])
                        if j == TILES - 1:
                            done.then_inc(f_tr.sem, 1)

            def gate(run, b, first, k):
                if first:
                    pe.wait_ge(f_mid.sem, f_mid.at(b - 1, TILES))
                    pe.wait_ge(f_out.sem, f_out.at(b - 3, TILES))
                else:
                    pe.wait_ge(f_mid.sem, f_mid.at(min(b + 2, BLOCKS - 1) if isinstance(b, int) else b + 2, TILES))
                    pe.wait_ge(f_out.sem, f_out.at(b - 1, TILES))
                pe.wait_ge(f_x32.sem, f_x32.at(run, DC))
                for j in range(TILES):
                    for c in range(DC):
                        done = nc.tensor.matmul(T[0][:, j * GW:(j + 1) * GW], xT[:, c, j * P:(j + 1) * P], route_w[:, c],
                                                start=c == 0, stop=c == DC - 1)
                        if j == TILES - 1 and c == DC - 1:
                            done.then_inc(f_route.sem, 1)

            def up(run, b, first, f):
                if isinstance(run, int) and run == 0 and f == 0:
                    pe.wait_ge(s_early_hi.sem, s_early_hi.at(2, 0))
                    pe.wait_ge(s_early_lo.sem, s_early_lo.at(2, 0))
                pe.wait_ge(f_rl.sem, f_rl.at(run, f - 1))
                cols = slice(f * P, (f + 1) * P)
                for c in range(DC):
                    pe.wait_ge(f_xl.sem, f_xl.at(run, c + 1))
                    product(U[f % 2][:], (wi_h[:, c, cols], wi_l[:, c, cols]), (xT_h[:, c], xT_l[:, c]), c == 0, False)

            def lora(run, b, first, k):
                pe.wait_ge(f_u.sem, f_u.at(run, 3))
                pe.wait_ge(f_xl.sem, f_xl.at(run, DC))
                for j in range(TILES):
                    done = nc.tensor.transpose(T[1][0:LS, j * P:(j + 1) * P], flat(u_rep[:, j]), ident[:])
                    if j == TILES - 1:
                        done.then_inc(f_uT.sem, 1)

            def act_(run, b, first, f):
                if isinstance(run, int) and run == 0 and f == 0:
                    pe.wait_ge(s_early_hi.sem, s_early_hi.at(4, 0))
                    pe.wait_ge(s_early_lo.sem, s_early_lo.at(4, 0))
                pe.wait_ge(f_ul.sem, f_ul.at(run, 1))
                pe.wait_ge(f_uh.sem, f_uh.at(run, 1))
                nc.tensor.matmul(U[f % 2][:], lora_b[0:LS2, f * P:(f + 1) * P], u_st[0:LS2], start=False, stop=True
                                 ).then_inc(f_up.sem, 1)

            def down(run, b, first, f):
                if isinstance(run, int) and run == 0 and f == 0:
                    pe.wait_ge(s_early_hi.sem, s_early_hi.at(len(early) + 1, 0))
                    pe.wait_ge(s_early_lo.sem, s_early_lo.at(n_early_lo, 0))
                if f == 0 and first:
                    pe.wait_ge(a_hl.sem, a_hl.at(b - 1, DC))
                if f == 0:
                    pe.wait_ge(f_u.sem, f_u.at(run, 3))
                    pe.wait_ge(f_ul.sem, f_ul.at(run, 1))
                pe.wait_ge(f_rl.sem, f_rl.at(run, f + 1))
                for j in range(TILES):
                    t = slice(j * P, (j + 1) * P)
                    done = product(T[j // 2][:, tiles(j)], (r_h[:, f % 2, t], r_l[:, f % 2, t]), (wo_h[:, f], wo_l[:, f]),
                                   f == 0 and j % 2 == 0, f == FT - 1, skip_group_check=True)
                    if j == TILES - 1:
                        done.then_inc(f_dn.sem, 1)

            def atr(b, k):
                pe.wait_ge(f_mid.sem, f_mid.at(b, TILES))
                pe.wait_ge(f_out.sem, f_out.at(b - 2, TILES))
                pe.wait_ge(a_h.sem, a_h.at(b, TILES))
                for c in range(DC):
                    for j in range(TILES):
                        done = nc.tensor.transpose(T[c][:, j * P:(j + 1) * P], hn[:, j, c * P:(c + 1) * P], ident[:])
                        if j == TILES - 1:
                            done.then_inc(a_tr.sem, 1)

            def atr2(b, k):
                pe.wait_ge(a_x2.sem, a_x2.at(b, TILES))
                pe.wait_ge(a_cb.sem, a_cb.at(b, 2 * TILES))
                for c in range(DC):
                    for j in range(TILES):
                        pe.wait_ge(a_h.sem, a_h.at(b, TILES + j + 1))
                        done = nc.tensor.transpose(A[c][:, j * P:(j + 1) * P], hn[:, j, c * P:(c + 1) * P], ident[:])
                        if j == TILES - 1:
                            done.then_inc(a_tr.sem, 1)

            def q(b, m):
                if isinstance(b, int) and b == 0 and m == 0:
                    pe.wait_ge(s_late_lo.sem, s_late_lo.at(late_count(len(late)), 0))
                pe.wait_ge(a_m.sem, a_m.at(b - 1, IT))
                cols = slice(m * P, (m + 1) * P)
                for c in range(DC):
                    pe.wait_ge(a_hl.sem, a_hl.at(b, c + 1))
                    done = product(A[2 + m][:], (wq_h[:, c, cols], wq_l[:, c, cols]), (hT_h[:, c], hT_l[:, c]),
                                   c == 0, c == DC - 1)
                    if c == DC - 1:
                        done.then_inc(a_q.sem, 1)

            def kv(b, j):
                pe.wait_ge(a_g.sem, a_g.at(b, j))
                t = slice(j * P, (j + 1) * P)
                for n, (lo_col, hi_col) in enumerate(((0, KI), (KI, KI + D))):
                    if j == 0:
                        pe.wait_ge(a_x3.sem, a_x3.at(b - 1, 2 * (n + 1)))
                    if n:
                        pe.wait_ge(a_v.sem, a_v.at(b, j))
                        pe.wait_ge(a_hl.sem, a_hl.at(b, DC))
                    for c in range(DC):
                        done = product(A[n][:, 0:hi_col - lo_col], (hT_h[:, c, t], hT_l[:, c, t]),
                                       (wkv_h[:, c, lo_col:hi_col], wkv_l[:, c, lo_col:hi_col]), c == 0, c == DC - 1)
                        if c == DC - 1:
                            done.then_inc(a_kv.sem, 1)

            def kT(b, k):
                pe.wait_ge(a_k32.sem, a_k32.at(b, TILES))
                for m in range(DC):
                    pe.wait_ge(a_r1.sem, a_r1.at(b, m + 1))
                    for j in range(TILES):
                        done = nc.tensor.transpose(A[2 + m][:, j * P:(j + 1) * P], k32[:, j, m * P:(m + 1) * P], ident[:])
                        if j == TILES - 1:
                            done.then_inc(a_kT.sem, 1)

            def fT_(b, k):
                pe.wait_ge(a_f.sem, a_f.at(b, TILES))
                pe.wait_ge(a_g.sem, a_g.at(b, TILES))
                for j in range(TILES):
                    done = nc.tensor.transpose(A[0][0:H, j * P:(j + 1) * P], fg[:, j], ident[:])
                    if j == TILES - 1:
                        done.then_inc(a_fT.sem, 1)

            def dec(b, k):
                value = held(pe, a_cum.at(b, TILES))
                pe.wait_ge(s_const.sem, s_const.at(len(consts), 0))
                pe.wait_ge(a_cum.sem, value)
                pe.wait_ge(a_v.sem, a_v.at(b, TILES))
                for j in range(TILES):
                    nc.tensor.transpose(A[1][:, j * H:(j + 1) * H], cumT[:, j], ident[0:H, 0:H])
                for m in range(DC):
                    at = TILES * H + m * TILES
                    done = nc.tensor.matmul(A[1][:, at:at + TILES], headsel[:, m], cumT[:, :, P - 1], start=True, stop=True)
                    if m == DC - 1:
                        done.then_inc(a_dT.sem, 1)

            def score(b, u):
                j, g = divmod(u, NQ)
                pe.wait_ge(d_stack.sem, d_stack.at(b, LOADS * max(j, 1)))
                if u < 2:
                    pe.wait_ge(a_r1.sem, a_r1.at(b, 2 * DC))
                else:
                    pe.wait_ge(a_P.sem, a_P.at(b, u - 1))
                t = slice((j % 2) * P, (j % 2 + 1) * P)
                for n in range(QUAD):
                    h = QUAD * g + n
                    done = nc.tensor.matmul(A[2 + u % 2][:, n * P:(n + 1) * P], ks[:, h, t], qs[:, h, t], start=True, stop=True)
                    if n == QUAD - 1:
                        done.then_inc(a_S.sem, 1)

            def mix(b, u):
                j, g = divmod(u, NQ)
                pe.wait_ge(a_P.sem, a_P.at(b, u + 1))
                if u == 0:
                    pe.wait_ge(a_fTs.sem, a_fTs.at(b, 2))
                elif g == 0:
                    pe.wait_ge(a_x2.sem, a_x2.at(b, j))
                for n in range(QUAD):
                    h = QUAD * g + n
                    done = nc.tensor.matmul(A[0][:, h * HV:(h + 1) * HV], pt[:, u % 2, n * P:(n + 1) * P], vp[:, j, h],
                                            start=True, stop=True)
                    if n == QUAD - 1:
                        done.then_inc(a_O.sem, 1)

            def carry(b, j):
                if j == 0:
                    pe.wait_ge(a_dec.sem, a_dec.at(b, 1))
                pe.wait_ge(a_cb.sem, a_cb.at(b, 2 * j))
                t = slice(j * P, (j + 1) * P)
                for m in range(DC):
                    done = nc.tensor.matmul(A[1][:, m * HH * HV:(m + 1) * HH * HV], q32[:, m, t], cb[:, m], start=True, stop=True)
                    if m == DC - 1:
                        done.then_inc(a_oi.sem, 1)

            def state(b, j):
                pe.wait_ge(a_t1.sem, a_t1.at(b, j + 1))
                pe.wait_ge(a_wv.sem, a_wv.at(b, NQ * (j + 1)))
                for m in range(DC):
                    done = nc.tensor.matmul(A[1][:, m * HH * HV:(m + 1) * HH * HV], k32[:, j, m * P:(m + 1) * P],
                                            flat(wv[:, m * HH:(m + 1) * HH]), start=True, stop=True)
                    if m == DC - 1:
                        done.then_inc(a_state.sem, 1)

            def yT_(b, j):
                pe.wait_ge(a_y.sem, a_y.at(b, j + 1))
                pe.wait_ge(a_o.sem, a_o.at(b, j + 1))
                for c in range(DC):
                    done = nc.tensor.transpose(A[0][:, c * P:(c + 1) * P], y[:, j % 2, c * P:(c + 1) * P], ident[:])
                    if c == DC - 1:
                        done.then_inc(a_yT.sem, 1)

            def wo(b, j):
                pe.wait_ge(a_yl.sem, a_yl.at(b, j + 1))
                for c in range(DC):
                    done = product(A[0][:, D:2 * D], (yT_h[:, c], yT_l[:, c]), (wao_h[:, c], wao_l[:, c]), c == 0, c == DC - 1)
                    if c == DC - 1:
                        done.then_inc(a_wo.sem, 1)

            def gu(b, i):
                rows = P if i < IT - 1 else last_rows
                if i:
                    pe.wait_ge(a_m.sem, a_m.at(b, i))
                else:
                    pe.wait_ge(a_P.sem, a_P.at(b, TILES * NQ))
                for n in range(2):
                    cols = slice(n * I + i * P, n * I + i * P + rows)
                    for c in range(DC):
                        pe.wait_ge(a_hl.sem, a_hl.at(b, DC + c + 1))
                        done = product(A[2 + n][:rows], (wgu_h[:, c, cols], wgu_l[:, c, cols]), (hT_h[:, c], hT_l[:, c]),
                                       c == 0, c == DC - 1)
                        if c == DC - 1:
                            done.then_inc(a_gu.sem, 1)

            def mdown(b, i):
                rows = P if i < IT - 1 else last_rows
                pe.wait_ge(a_ml.sem, a_ml.at(b, i + 1))
                for j in range(TILES):
                    t = slice(j * P, (j + 1) * P)
                    done = product(A[j // 2][:, tiles(j)], (m_h[:rows, i % 2, t], m_l[:rows, i % 2, t]),
                                   (wd_h[:rows, i], wd_l[:rows, i]), i == 0 and j % 2 == 0, i == IT - 1,
                                   skip_group_check=True)
                    if j == TILES - 1:
                        done.then_inc(a_md.sem, 1)

            pe.wait_ge(s_const.sem, s_const.at(len(consts), 0))
            pe.wait_ge(s_setup.sem, s_setup.at(n_setup, 0))
            schedule(pe, {"f_tr": tr, "f_gate": gate, "f_up": up, "f_lora": lora, "f_act": act_, "f_down": down,
                          "a_tr": atr, "a_q": q, "a_kv": kv, "a_kT": kT, "a_fT": fT_, "a_decay": dec, "a_score": score,
                          "a_mix": mix, "a_carry": carry, "a_state": state, "a_yT": yT_, "a_wo": wo,
                          "a_tr2": atr2, "a_gu": gu, "a_mdown": mdown})


def kernel(**inputs):
    from concourse import bacc
    from concourse.bass_utils import run_bass_kernel_spmd

    g = {name: np.asarray(v) for name, v in inputs.items()}
    att = lambda name: g["L0_attn_" + name]
    ffn = lambda name: g["L0_ffn_" + name]
    cat = np.concatenate
    lora = ffn("lora_B").transpose(0, 2, 1).reshape(ER, F)
    bias = ffn("wi_b")[None]
    head = np.arange(P) // HD
    arrays = {
        "x": att("x").reshape(BLOCKS, TILES, P, D),
        "wi": ffn("wi_W").T, "wo": ffn("wo_W").T,
        "lora": cat([lora, lora, lora, bias, bias]),
        "wq": att("wq"), "wkv": cat([att("wk"), att("wi"), att("wf"), att("wv")], axis=1), "wao": att("wo"),
        "wgu": cat([att("w_gate"), att("w_up")], axis=1), "wd": att("w_down"),
        "route_w": cat([ffn("gate_W"), ffn("lora_A").reshape(ER, D)]).T,
        "route_b": ffn("gate_b"), "wo_b": ffn("wo_b"), "gate_bias": cat([att("bi"), att("bf")]),
        "ln1": att("ln1_w").reshape(DC, P).T, "ln2": att("ln2_w").reshape(DC, P).T,
        "ident": np.eye(P, dtype=np.float32), "ident4": np.tile(np.eye(P, dtype=np.float32), (1, QUAD)),
        "headmask": np.tile(np.repeat(head[:, None] == np.arange(HH), HV, axis=1), (1, DC)).astype(np.float32),
        "headsel": np.stack([np.arange(H)[:, None] == head + m * HH for m in range(DC)], axis=1).astype(np.float32),
        "prio": np.broadcast_to(np.arange(E, 0, -1, dtype=np.float32), (P, TILES, E)),
    }
    arrays = {k: np.ascontiguousarray(v) for k, v in arrays.items()}
    nc = bacc.Bacc("TRN2", target_bir_lowering=False, num_devices=1, dynamic_dma_scratch_size=1024)
    a = {k: nc.dram_tensor("in_" + k, v.shape, mybir.dt.from_np(v.dtype), kind="ExternalInput").ap() for k, v in arrays.items()}
    out = nc.dram_tensor("out", (BLOCKS, TILES, P, D), F32, kind="ExternalOutput").ap()
    build(nc, a, out)
    r = run_bass_kernel_spmd(nc, [{"in_" + k: v for k, v in arrays.items()}], core_ids=[0])
    return r.results[0]["out"].reshape(N_SEQ, SEQ, D)
```
